# Optimizing a Trainium2 kernel written in Bass

```python
import numpy as np
import jax
import jax.numpy as jnp

def _softmax(x, axis=-1):
    return jax.nn.softmax(x, axis=axis)

def _gelu(x):
    return jax.nn.gelu(x, approximate=True)

def _silu(x):
    return jax.nn.silu(x)

def _sigmoid(x):
    return jax.nn.sigmoid(x)

def _layernorm(x, axis=-1, eps=1e-05):
    m = jnp.mean(x, axis=axis, keepdims=True)
    v = jnp.var(x, axis=axis, keepdims=True)
    return (x - m) / jnp.sqrt(v + eps)

def _scatter_add(tgt, idx, src, axis=0):
    return tgt.at[idx].add(src)

def _segment_sum(src, seg, n):
    return jax.ops.segment_sum(src, seg, n)
kernel_name = 'mk_adaln_attn_ffn_d1_seqx_r4_30e63d'

def setup_inputs(seed: int=0):
    np.random.seed(seed)
    _w = jnp.asarray

    def _rec_inputs():
        import jax
        import jax.numpy as jnp
        _rk = jax.random.key(seed)
        x = -0.0002071 + 1 * jax.random.normal(jax.random.fold_in(_rk, 1), (64, 64, 256), jnp.float32)
        _lenS = 64 - jax.random.randint(jax.random.fold_in(_rk, 7), (64,), 0, max(1, 64 // 4) + 1, jnp.int32)
        _lenS2 = 64 - jax.random.randint(jax.random.fold_in(_rk, 8), (64,), 0, max(1, 64 // 4) + 1, jnp.int32)
        cond_8 = jax.random.uniform(jax.random.fold_in(_rk, 11), (64, 8), jnp.float32, 0.0, 0.983423)
        return (x, cond_8)
    x, cond_8 = _rec_inputs()

    def _L0_cond_setup():
        import jax, jax.numpy as jnp
        import numpy as np
        R = 16
        ALPHA = 32.0
        SCALING = ALPHA / R
        key = jax.random.key(seed)
        ks = jax.random.split(key, 6)
        B, T, C, O, E = (16, 375, 256, 256, 8)
        x = jax.random.normal(ks[0], (B, T, C), dtype=jnp.float32)
        w = jax.random.uniform(ks[1], (B, E), dtype=jnp.float32)
        W_base = jax.random.normal(ks[2], (O, C), dtype=jnp.float32) * 0.02
        b_base = jax.random.normal(ks[3], (O,), dtype=jnp.float32) * 0.02
        As = jax.random.normal(ks[4], (E, R, C), dtype=jnp.float32) * 0.02
        Bs = jax.random.normal(ks[5], (E, O, R), dtype=jnp.float32) * 0.02
        return {'x': x, 'w': w, 'W_base': W_base, 'b_base': b_base, 'As': As, 'Bs': Bs}
    _L0_cond_all = _L0_cond_setup()
    _L0_cond_in = {k: v for k, v in _L0_cond_all.items() if k in ('W_base', 'b_base', 'As', 'Bs')}
    del _L0_cond_all

    def _L0_attn_setup():
        import jax, jax.numpy as jnp
        import numpy as np
        B, T, D, H = (4, 512, 256, 16)
        E = D // H
        DH = D // 4
        key = jax.random.key(seed)
        ks = jax.random.split(key, 9)
        s = D ** (-0.5)
        return {'x': jax.random.normal(ks[0], (B, T, D), jnp.float32), 'q_w': jax.random.normal(ks[1], (D, D), jnp.float32) * s, 'k_w': jax.random.normal(ks[2], (D, D), jnp.float32) * s, 'v_w': jax.random.normal(ks[3], (D, D), jnp.float32) * s, 'o_w': jax.random.normal(ks[4], (D, D), jnp.float32) * s, 'cs_w1': jax.random.normal(ks[5], (DH, D), jnp.float32) * s, 'cs_b1': jnp.zeros((DH,), jnp.float32), 'cs_w2': jax.random.normal(ks[6], (H, DH), jnp.float32) * DH ** (-0.5), 'cs_b2': jnp.zeros((H,), jnp.float32), 'decay_params': jax.random.normal(ks[7], (H, E), jnp.float32) + 3.0}
    _L0_attn_all = _L0_attn_setup()
    _L0_attn_in = {k: v for k, v in _L0_attn_all.items() if k in ('q_w', 'k_w', 'v_w', 'o_w', 'cs_w1', 'cs_b1', 'cs_w2', 'cs_b2', 'decay_params')}
    del _L0_attn_all

    def _L0_cond2_setup():
        import jax, jax.numpy as jnp
        import numpy as np
        key = jax.random.key(seed)
        k1, k2, k3, k4, k5 = jax.random.split(key, 5)
        B, N, T, O, G = (32, 64, 256, 256, 8)
        x = jax.random.normal(k1, (B, N, T), dtype=jnp.float32)
        y = jax.random.uniform(k2, (B, G), dtype=jnp.float32)
        weight = jax.random.normal(k3, (G, O, T), dtype=jnp.float32) * (1.0 / np.sqrt(T))
        mask = jax.random.uniform(k4, (O, T), dtype=jnp.float32)
        bias = jax.random.normal(k5, (O,), dtype=jnp.float32)
        return {'x': x, 'y': y, 'weight': weight, 'mask': mask, 'bias': bias}
    _L0_cond2_all = _L0_cond2_setup()
    _L0_cond2_in = {k: v for k, v in _L0_cond2_all.items() if k in ('weight', 'mask', 'bias')}
    del _L0_cond2_all

    def _L0_ffn_setup():
        import jax, jax.numpy as jnp
        import numpy as np
        B, S, D, H, E, F, K = (2, 256, 256, 16, 8, 1024, 2)
        EPS = 1e-05

        def _layernorm(x, g, b):
            mu = jnp.mean(x, axis=-1, keepdims=True)
            var = jnp.mean(jnp.square(x - mu), axis=-1, keepdims=True)
            return (x - mu) * jax.lax.rsqrt(var + EPS) * g + b
        key = jax.random.key(seed)
        ks = jax.random.split(key, 12)
        w = lambda k, shape: jax.random.normal(k, shape, dtype=jnp.float32) * 0.02
        return {'x': jax.random.normal(ks[0], (B, S, D), dtype=jnp.float32), 'ln1_g': jnp.ones((D,), jnp.float32), 'ln1_b': jnp.zeros((D,), jnp.float32), 'ln2_g': jnp.ones((D,), jnp.float32), 'ln2_b': jnp.zeros((D,), jnp.float32), 'Wq': w(ks[1], (D, D)), 'Wk': w(ks[2], (D, D)), 'Wv': w(ks[3], (D, D)), 'Wo': w(ks[4], (D, D)), 'Wg': w(ks[5], (D, E)), 'W1': w(ks[6], (E, D, F)), 'b1': jnp.zeros((E, F), jnp.float32), 'W2': w(ks[7], (E, F, D)), 'b2': jnp.zeros((E, D), jnp.float32)}
    _L0_ffn_all = _L0_ffn_setup()
    _L0_ffn_in = {k: v for k, v in _L0_ffn_all.items() if k in ('ln1_g', 'ln1_b', 'ln2_g', 'ln2_b', 'Wq', 'Wk', 'Wv', 'Wo', 'Wg', 'W1', 'b1', 'W2', 'b2')}
    del _L0_ffn_all
    return {'x': x, 'cond_8': cond_8, 'L0_cond_W_base': _L0_cond_in['W_base'], 'L0_cond_b_base': _L0_cond_in['b_base'], 'L0_cond_As': _L0_cond_in['As'], 'L0_cond_Bs': _L0_cond_in['Bs'], 'L0_attn_q_w': _L0_attn_in['q_w'], 'L0_attn_k_w': _L0_attn_in['k_w'], 'L0_attn_v_w': _L0_attn_in['v_w'], 'L0_attn_o_w': _L0_attn_in['o_w'], 'L0_attn_cs_w1': _L0_attn_in['cs_w1'], 'L0_attn_cs_b1': _L0_attn_in['cs_b1'], 'L0_attn_cs_w2': _L0_attn_in['cs_w2'], 'L0_attn_cs_b2': _L0_attn_in['cs_b2'], 'L0_attn_decay_params': _L0_attn_in['decay_params'], 'L0_cond2_weight': _L0_cond2_in['weight'], 'L0_cond2_mask': _L0_cond2_in['mask'], 'L0_cond2_bias': _L0_cond2_in['bias'], 'L0_ffn_ln1_g': _L0_ffn_in['ln1_g'], 'L0_ffn_ln1_b': _L0_ffn_in['ln1_b'], 'L0_ffn_ln2_g': _L0_ffn_in['ln2_g'], 'L0_ffn_ln2_b': _L0_ffn_in['ln2_b'], 'L0_ffn_Wq': _L0_ffn_in['Wq'], 'L0_ffn_Wk': _L0_ffn_in['Wk'], 'L0_ffn_Wv': _L0_ffn_in['Wv'], 'L0_ffn_Wo': _L0_ffn_in['Wo'], 'L0_ffn_Wg': _L0_ffn_in['Wg'], 'L0_ffn_W1': _L0_ffn_in['W1'], 'L0_ffn_b1': _L0_ffn_in['b1'], 'L0_ffn_W2': _L0_ffn_in['W2'], 'L0_ffn_b2': _L0_ffn_in['b2']}

def reference(x, cond_8, L0_cond_W_base, L0_cond_b_base, L0_cond_As, L0_cond_Bs, L0_attn_q_w, L0_attn_k_w, L0_attn_v_w, L0_attn_o_w, L0_attn_cs_w1, L0_attn_cs_b1, L0_attn_cs_w2, L0_attn_cs_b2, L0_attn_decay_params, L0_cond2_weight, L0_cond2_mask, L0_cond2_bias, L0_ffn_ln1_g, L0_ffn_ln1_b, L0_ffn_ln2_g, L0_ffn_ln2_b, L0_ffn_Wq, L0_ffn_Wk, L0_ffn_Wv, L0_ffn_Wo, L0_ffn_Wg, L0_ffn_W1, L0_ffn_b1, L0_ffn_W2, L0_ffn_b2):
    import jax
    import jax.numpy as jnp

    def _L0_cond_ref(x, w, W_base, b_base, As, Bs):
        import jax, jax.numpy as jnp
        import numpy as np
        R = 16
        ALPHA = 32.0
        SCALING = ALPHA / R
        out = jnp.einsum('btc,oc->bto', x, W_base) + b_base
        h = jnp.einsum('btc,erc->bter', x, As)
        lora = jnp.einsum('bter,eor,be->bto', h, Bs, w)
        return out + lora * SCALING

    def _L0_attn_ref(x, q_w, k_w, v_w, o_w, cs_w1, cs_b1, cs_w2, cs_b2, decay_params):
        import jax, jax.numpy as jnp
        import numpy as np
        B, T, D, H = (4, 512, 256, 16)
        E = D // H
        DH = D // 4
        Bx, Tx, Dx = x.shape
        q = (x @ q_w.T).reshape(Bx, Tx, H, E)
        k = (x @ k_w.T).reshape(Bx, Tx, H, E)
        v = (x @ v_w.T).reshape(Bx, Tx, H, E)
        lc = jax.nn.sigmoid(jnp.tanh(x @ cs_w1.T + cs_b1) @ cs_w2.T + cs_b2)
        base = jax.nn.sigmoid(decay_params)[None, None]
        lam = jnp.clip(base * (1.0 + 0.2 * lc[..., None]), 0.0, 0.9995)

        def step(state, inp):
            qt, kt, vt, dt = inp
            state = state * dt[..., None] + kt[..., None] * vt[:, :, None, :]
            out_t = jnp.einsum('bhe,bhef->bhf', qt, state)
            return (state, out_t)
        init = jnp.zeros((Bx, H, E, E), x.dtype)
        xs = (jnp.swapaxes(q, 0, 1), jnp.swapaxes(k, 0, 1), jnp.swapaxes(v, 0, 1), jnp.swapaxes(lam, 0, 1))
        _, ys = jax.lax.scan(step, init, xs)
        y = jnp.swapaxes(ys, 0, 1).reshape(Bx, Tx, Dx)
        return y @ o_w.T

    def _L0_cond2_ref(x, y, weight, mask, bias):
        import jax, jax.numpy as jnp
        import numpy as np
        masked_w = weight * mask[None, :, :]
        w_bot = jnp.einsum('bg,got->bot', y, masked_w)
        return jnp.einsum('bnt,bot->bno', x, w_bot) + bias

    def _L0_ffn_ref(x, ln1_g, ln1_b, ln2_g, ln2_b, Wq, Wk, Wv, Wo, Wg, W1, b1, W2, b2):
        import jax, jax.numpy as jnp
        import numpy as np
        B, S, D, H, E, F, K = (2, 256, 256, 16, 8, 1024, 2)
        EPS = 1e-05

        def _layernorm(x, g, b):
            mu = jnp.mean(x, axis=-1, keepdims=True)
            var = jnp.mean(jnp.square(x - mu), axis=-1, keepdims=True)
            return (x - mu) * jax.lax.rsqrt(var + EPS) * g + b
        Bb, Ss, Dd = x.shape
        Dh = Dd // H
        h = _layernorm(x, ln1_g, ln1_b)
        q = (h @ Wq).reshape(Bb, Ss, H, Dh)
        k = (h @ Wk).reshape(Bb, Ss, H, Dh)
        v = (h @ Wv).reshape(Bb, Ss, H, Dh)
        scores = jnp.einsum('bqhd,bkhd->bhqk', q, k) / jnp.sqrt(jnp.float32(Dh))
        attn = jax.nn.softmax(scores, axis=-1)
        ctx = jnp.einsum('bhqk,bkhd->bqhd', attn, v).reshape(Bb, Ss, Dd)
        x = x + ctx @ Wo
        m = _layernorm(x, ln2_g, ln2_b)
        xt = m.reshape(-1, Dd)
        T = xt.shape[0]
        probs = jax.nn.softmax(xt @ Wg, axis=-1)
        wts, idx = jax.lax.top_k(probs, K)
        wts = wts / jnp.sum(wts, axis=-1, keepdims=True)
        h1 = jax.nn.gelu(jnp.einsum('td,edf->etf', xt, W1) + b1[:, None, :])
        ye = jnp.einsum('etf,efd->etd', h1, W2) + b2[:, None, :]
        sel = ye[idx, jnp.arange(T)[:, None], :]
        moe_out = jnp.sum(wts[..., None] * sel, axis=1).reshape(Bb, Ss, Dd)
        return x + moe_out
    x = x + _L0_attn_ref(_L0_cond_ref(x, cond_8, L0_cond_W_base, L0_cond_b_base, L0_cond_As, L0_cond_Bs), L0_attn_q_w, L0_attn_k_w, L0_attn_v_w, L0_attn_o_w, L0_attn_cs_w1, L0_attn_cs_b1, L0_attn_cs_w2, L0_attn_cs_b2, L0_attn_decay_params)
    x = x + _L0_ffn_ref(_L0_cond2_ref(x, cond_8, L0_cond2_weight, L0_cond2_mask, L0_cond2_bias), L0_ffn_ln1_g, L0_ffn_ln1_b, L0_ffn_ln2_g, L0_ffn_ln2_b, L0_ffn_Wq, L0_ffn_Wk, L0_ffn_Wv, L0_ffn_Wo, L0_ffn_Wg, L0_ffn_W1, L0_ffn_b1, L0_ffn_W2, L0_ffn_b2)
    return x

_drawn_inputs = setup_inputs


def setup_inputs(seed=0):
    import zlib

    import numpy as np

    out = dict(_drawn_inputs(seed))
    spreads = {'L0_attn_cs_b1': (0.0, 0.731),
     'L0_attn_cs_b2': (0.0, 0.518),
     'L0_ffn_ln1_g': (1.0, 0.6),
     'L0_ffn_ln1_b': (0.0, 0.8),
     'L0_ffn_ln2_g': (1.0, 0.591),
     'L0_ffn_ln2_b': (0.0, 0.403),
     'L0_ffn_b1': (0.0, 0.649),
     'L0_ffn_b2': (0.0, 0.1)}
    factors = {'L0_attn_cs_w1': 6.505, 'L0_attn_cs_w2': 4.231, 'L0_ffn_Wq': 8.0, 'L0_ffn_Wk': 8.0}
    for name, (base, spread) in spreads.items():
        noise = np.random.default_rng([zlib.crc32(name.encode()), seed]).standard_normal(out[name].shape)
        drawn = base * np.exp(spread * noise) if base else spread * noise
        out[name] = jnp.asarray(drawn.astype(out[name].dtype))
    for name, factor in factors.items():
        out[name] = (out[name] * factor).astype(out[name].dtype)
    return out
```

```python
import concourse.bass as bass
from concourse import mybir
from contextlib import ExitStack

F32 = mybir.dt.float32
U32 = mybir.dt.uint32
ALU = mybir.AluOpType
ACT = mybir.ActivationFunctionType
AX_X = mybir.AxisListType.X

P = 128
B, T, D = 64, 64, 256
H, DH = 16, 16
E, R = 8, 16
F = 1024
CH = D // P
FC = F // P
GB = 8
GT = GB * T
NG = B // GB
NT = GT // P
NR = 4
HB = 4
NH = GB // HB
DC = 64
LORA_SCALE = 32.0 / R
LAM_MAX = 0.9995
EPS = 1e-05
PV = 2 * DH
PW = PV + 2


def bass_adaln_attn_ffn(nc, x_t, cond_t, w_base, b_base, lora_a, lora_b, wq, wk, wv, wo, cs_w1, cs_b1, cs_w2,
                        cs_b2, decay, c2_w, c2_mask, c2_bias, ln1_g, ln1_b, ln2_g, ln2_b, fq, fk, fv, fo, fg,
                        fw1, fb1, fw2, fb2, ident_in, out):
    with ExitStack() as ctx:
        def sb(name, shape, dt=F32):
            return ctx.enter_context(nc.sbuf_tensor(name, shape, dt))

        def sem(name):
            return ctx.enter_context(nc.semaphore(name))

        bank = [ctx.enter_context(nc.psum_tensor(f"bank{i}", [P, 512], F32)) for i in range(8)]

        w_base_s = sb("w_base_s", [P, CH, D])
        lora_a_s = sb("lora_a_s", [P, CH, P])
        lora_b_s = sb("lora_b_s", [P, D])
        wq_s, wk_s, wv_s, wo_s = [sb(n, [P, CH, D]) for n in ("wq_s", "wk_s", "wv_s", "wo_s")]
        fq_s, fk_s, fv_s, fo_s = [sb(n, [P, CH, D]) for n in ("fq_s", "fk_s", "fv_s", "fo_s")]
        cs_w1_s = sb("cs_w1_s", [P, CH, DC])
        cs_w2_s = sb("cs_w2_s", [DC, D])
        fg_s = sb("fg_s", [P, CH, E])
        c2_w_s = sb("c2_w_s", [P, CH, E, D])
        c2_mask_s = sb("c2_mask_s", [P, CH, D])
        c2_bias_s = sb("c2_bias_s", [P, D])
        cond_er = sb("cond_er", [P, B])
        cond_all = sb("cond_all", [P, E, B])
        b_base_s = sb("b_base_s", [P, CH])
        cs_b1_s = sb("cs_b1_s", [DC, 1])
        cs_b2_s = sb("cs_b2_s", [P, CH])
        decay_s = sb("decay_s", [P, CH])
        lng = sb("lng", [P, 4, CH])
        ident = sb("ident", [P, P])
        half_b2 = sb("half_b2", [P, CH])
        base_t = sb("base_t", [P, CH])
        base_11 = sb("base_11", [P, CH])
        base_01 = sb("base_01", [P, CH])
        par_mask = sb("par_mask", [P, 2])
        causal = sb("causal", [P, T])
        same_head = sb("same_head", [P, 2, T])
        diag_ones = sb("diag_ones", [P, T])
        expo = sb("expo", [P, NT])
        iota8 = sb("iota8", [P, E])
        iota8u = sb("iota8u", [P, E], mybir.dt.int32)
        ones_row = sb("ones_row", [1, P])

        xt = sb("xt", [P, CH, GT])
        lora_h = sb("lora_h", [P, GT])
        y0t = sb("y0t", [P, CH, GT])
        cs_h = sb("cs_h", [DC, GT])
        decay_work = sb("decay_work", [P, 2, CH * GT])
        lam, cum_inv = decay_work[:, 0, :], decay_work[:, 1, :]
        lam_first = sb("lam_first", [P, CH * GT])
        cum = sb("cum", [P, CH * GT])
        cum_mid = sb("cum_mid", [P, CH * GB])
        v_pair = sb("v_pair", [P, GB, NR * CH, PW])
        k_pair = sb("k_pair", [P, CH, GB, 2, T])
        q_pair = sb("q_pair", [P, CH, GB, 2, T])
        q_all = sb("q_all", [P, CH, GT])
        k_all = sb("k_all", [P, CH, GT])
        probs = sb("probs", [P, NH, NR, HB, CH, T])
        yt = sb("yt", [P, CH, GT])
        x1t = xt
        xg = decay_work[:, :, :].rearrange("p g (c t) -> p g c t", c=CH)
        z = sb("z", [P, NT, D])
        hn = sb("hn", [P, NT, D])
        lc = hn[:, :, :].rearrange("p n d -> p (n d)").rearrange("p (c t) -> p c t", c=CH)
        tick_s = sb("tick_s", [P, 2])
        stats = sb("stats", [P, NT, 6])
        mv = sb("mv", [P, NT, 2])
        var_e = sb("var_e", [P, NT])
        rstd = sb("rstd", [P, NT])
        row_max = sb("row_max", [P, NH, NR, HB, CH])
        shift = sb("shift", [P, 2, HB * CH, T])
        ctxn = k_all[:, :, :].rearrange("p c t -> p (c t)").rearrange("p (n d) -> p n d", d=D)
        sum_inv = sb("sum_inv", [P, NT, CH * NR, 2])
        lg = sb("lg", [P, NT, E])
        top = sb("top", [P, NT, 8])
        top_i = sb("top_i", [P, NT, 8], U32)
        top_f = sb("top_f", [P, NT, 8])
        ex = sb("ex", [P, NT, E])
        ex_sum = sb("ex_sum", [P, NT])
        two_sum = sb("two_sum", [P, NT])
        wts = sb("wts", [P, NT, 2])
        pick = sb("pick", [P, NT, 2, E])

        mt = sb("mt", [P, CH, B * T])
        acc = sb("acc", [P, NG * NT, D])
        gates = sb("gates", [P, NG * NT, E])

        names = ("weights_in xt_in consts_made mask_done derived "
                 "lora_ready lora_kept y0_ready y0_kept cs1_ready cs1_kept cs2_ready lc_kept v_ready v_kept "
                 "k_ready k_kept q_ready q_kept s_ready s_kept y_ready y_kept o_ready x1t_kept "
                 "xg_made xg_used x1_ready x1_kept z_ready z_kept var_made rstd_made hn_made ht_ready ht_kept "
                 "qb_ready qb_kept kb_ready kb_kept vb_ready vb_kept smax_ready max_kept shift_made st_ready p_kept "
                 "pv_ready ctx_kept ctxt_ready ctxt_kept wo_ready z2_kept acc_made mt_ready mt_kept mt_stored gate_ready lg_made "
                 "ex_made gates_made dve_steps w1_in w2_in h_ready h_kept ye_ready ye_kept out_done").split()
        s = {n: sem(n) for n in names}

        START = 1

        HALF = T // 2
        seg = "p (n h t) -> p n h t"
        F_MID = cum[:, :].rearrange(seg, h=2, t=HALF)

        block = ctx.enter_context(nc.Block())
        N_LOADS = 0
        loads = [
            (w_base_s, w_base), (lora_a_s, lora_a), (lora_b_s, lora_b), (wq_s, wq), (wk_s, wk), (wv_s, wv),
            (wo_s, wo), (fq_s, fq), (fk_s, fk), (fv_s, fv), (fo_s, fo), (cs_w1_s, cs_w1), (cs_w2_s, cs_w2),
            (fg_s, fg), (c2_w_s, c2_w), (c2_mask_s, c2_mask), (cs_b1_s, cs_b1), (cs_b2_s, cs_b2),
            (decay_s, decay), (b_base_s, b_base), (ident, ident_in)]

        w1_s = k_pair[:, :, :, :, :].rearrange("p c b a t -> p (c b a t)").rearrange("p (c f) -> p c f", c=CH)
        w2_s = q_pair[:, :, :, :, :].rearrange("p c b a t -> p (c b a t)").rearrange("p (c f) -> p c f", c=FC)
        b1_s = sb("b1_s", [P, FC])
        b2_s = sb("b2_s", [1, D])
        ht_e = probs[:, :, :, :, :, :].rearrange("p n r b c t -> p (n r) (b c t)")

        @block.sync
        def _(sp):
            for n in names:
                sp.sem_inc(s[n], START)
            for dst, src in loads:
                sp.dma_start(dst[:], src).then_inc(s["weights_in"], 16)
            for j, src in enumerate((ln1_g, ln1_b, ln2_g, ln2_b)):
                sp.dma_start(lng[:, j, :], src).then_inc(s["weights_in"], 16)
            sp.dma_start(c2_bias_s[:], c2_bias.partition_broadcast(P)).then_inc(s["weights_in"], 16)
            sp.dma_start(cond_all[:], cond_t.partition_broadcast(P)).then_inc(s["weights_in"], 16)
            for e in range(E):
                sp.dma_start(cond_er[e * R:(e + 1) * R, :], cond_t[e, :].partition_broadcast(R)).then_inc(s["weights_in"], 16)
            with sp.Fori(0, NG) as i:
                sp.wait_ge(s["xg_made"], START + i * E)
                sp.wait_ge(s["x1_ready"], START + i * 2)
                sp.dma_start(xt[:, :, :], x_t[:, :, bass.ds(i * GT, GT)]).then_inc(s["xt_in"], 16)
            sp.wait_ge(s["pv_ready"], START + NG * NT)
            sp.wait_ge(s["st_ready"], START + NG * NH * NR)
            with sp.Fori(0, E) as e:
                sp.wait_ge(s["ye_ready"], START + e * (NG * 2))
                sp.dma_start(w1_s[:, :, :], fw1[:, bass.ds(e, 1), :, :].rearrange("p e c f -> p (e c) f")).then_inc(s["w1_in"], 16)
                sp.dma_start(w2_s[:, :, :], fw2[:, bass.ds(e, 1), :, :].rearrange("p e c f -> p (e c) f")).then_inc(s["w1_in"], 16)
                sp.dma_start(b2_s[:, :], fb2[bass.ds(e, 1), :]).then_inc(s["w1_in"], 16)
                sp.wait_ge(s["h_kept"], START + e * (NG * FC))
                sp.dma_start(b1_s[:, :], fb1[:, bass.ds(e, 1), :].rearrange("p e c -> p (e c)")).then_inc(s["w1_in"], 16)
            sp.wait_ge(s["ye_kept"], START + E * NG * 2)
            sp.dma_start(out.rearrange("(n p) d -> p n d", p=P), acc[:, :, :]).then_inc(s["out_done"], 16)
            sp.wait_ge(s["out_done"], START + 16)

        W_IN = 16 * (len(loads) + 4 + 2 + E)

        @block.gpsimd
        def _(pool):
            nc.gpsimd.memset(par_mask[:], 1.0).then_inc(s["consts_made"], 1)
            nc.gpsimd.memset(causal[:], 1.0).then_inc(s["consts_made"], 1)
            nc.gpsimd.memset(same_head[:], 1.0).then_inc(s["consts_made"], 1)
            nc.gpsimd.memset(expo[:], -0.5).then_inc(s["consts_made"], 1)
            nc.gpsimd.memset(ones_row[:], 1.0).then_inc(s["consts_made"], 1)
            nc.gpsimd.memset(v_pair[:], 0.0).then_inc(s["consts_made"], 1)
            nc.gpsimd.memset(lam_first[:], 0.0).then_inc(s["consts_made"], 1)
            nc.gpsimd.iota(iota8u[:], [[1, E]], base=0, channel_multiplier=0).then_inc(s["consts_made"], 1)
            pool.wait_ge(s["consts_made"], START + 8)
            for half in range(2):
                rows = slice(half * T, half * T + T)
                nc.gpsimd.affine_select(out=causal[rows, :], in_=causal[rows, :], compare_op=ALU.is_ge, fill=0.0,
                                        base=0, pattern=[[1, T]], channel_multiplier=-1).then_inc(s["consts_made"], 1)
                pool.wait_ge(s["consts_made"], START + 9 + half)
            nc.gpsimd.tensor_copy(iota8[:], iota8u[:]).then_inc(s["consts_made"], 1)
            pool.wait_ge(s["consts_made"], START + 11)
            pool.wait_ge(s["mask_done"], START + 6)
            with pool.Fori(0, NG) as i:
                for n in range(1):
                    pool.wait_ge(s["var_made"], START + i * 2 + 1)
                    nc.gpsimd.tensor_tensor(rstd[:], var_e[:], expo[:], ALU.pow).then_inc(s["rstd_made"], 1)
                for j in range(NH * NR):
                    pool.wait_ge(s["max_kept"], START + i * 8 + j + 1)
                    if j >= 2:
                        pool.wait_ge(s["st_ready"], START + i * 8 + j - 1)
                    nc.gpsimd.tensor_tensor(
                        shift[:, j % 2, :, :],
                        row_max[:, j // NR, j % NR, :, :].rearrange("p b c -> p (b c)").unsqueeze(2).to_broadcast([P, HB * CH, T]),
                        diag_ones[:, :].unsqueeze(1).to_broadcast([P, HB * CH, T]), ALU.mult).then_inc(s["shift_made"], 1)
                pool.wait_ge(s["var_made"], START + i * 2 + 2)
                nc.gpsimd.tensor_tensor(rstd[:], var_e[:], expo[:], ALU.pow).then_inc(s["rstd_made"], 1)
                pool.wait_ge(s["mt_kept"], START + i * 2 + 2)
                nc.gpsimd.tensor_copy(mt[:, :, bass.ds(i * GT, GT)], y0t[:, :, :]).then_inc(s["mt_stored"], 1)

        CONSTS = 8 + 3

        @block.tensor
        def _(pe):
            def mm(o, l, r, first, last):
                return nc.tensor.matmul(o, l, r, start=first, stop=last, skip_group_check=True)

            def wait(name, v):
                pe.wait_ge(s[name], START + v)

            wait("weights_in", W_IN)
            wait("consts_made", CONSTS)
            wait("derived", 1)
            wait("mask_done", 6)
            with pe.Fori(0, NG) as i:
                wait("xt_in", i * 16 + 16)
                wait("y_kept", i * 2)
                for c in range(CH):
                    last = mm(bank[0][:, :], lora_a_s[:, c, :], xt[:, c, :], c == 0, c == CH - 1)
                last.then_inc(s["lora_ready"], 1)
                for o in range(CH):
                    if o == 0:
                        wait("mt_kept", i * 2)
                        wait("lg_made", i)
                    for c in range(CH):
                        mm(bank[1 + o][:, :], w_base_s[:, c, o * P:(o + 1) * P], xt[:, c, :], c == 0, False)
                wait("lora_kept", i + 1)
                for o in range(CH):
                    mm(bank[1 + o][:, :], lora_b_s[:, o * P:(o + 1) * P], lora_h[:, :], False, True).then_inc(s["y0_ready"], 1)
                wait("y0_kept", i * 2 + 2)
                wait("ctx_kept", i * 4)
                for c in range(CH):
                    last = mm(bank[3][0:DC, :], cs_w1_s[:, c, :], y0t[:, c, :], c == 0, c == CH - 1)
                last.then_inc(s["cs1_ready"], 1)
                wait("z2_kept", i * 2)
                for u in range(2):
                    for n in range(2):
                        t = 2 * u + n
                        for c in range(CH):
                            last = mm(bank[6 + u][:, n * D:(n + 1) * D], y0t[:, c, t * P:(t + 1) * P], wv_s[:, c, :], c == 0, c == CH - 1)
                    last.then_inc(s["v_ready"], 1)
                wait("cs1_kept", i + 1)
                wait("ctxt_kept", i * 2)
                for c in range(CH):
                    mm(bank[4 + c][:, :], cs_w2_s[:, c * P:(c + 1) * P], cs_h[:, :], True, True).then_inc(s["cs2_ready"], 1)
                wait("y0_kept", i * 2 + 2)
                for o in range(CH):
                    if o == 0:
                        wait("lora_kept", i + 1)
                    for c in range(CH):
                        last = mm(bank[o][:, :], wk_s[:, c, o * P:(o + 1) * P], y0t[:, c, :], c == 0, c == CH - 1)
                    last.then_inc(s["k_ready"], 1)
                for o in range(CH):
                    if o == 1:
                        wait("cs1_kept", i + 1)
                    for c in range(CH):
                        last = mm(bank[2 + o][:, :], wq_s[:, c, o * P:(o + 1) * P], y0t[:, c, :], c == 0, c == CH - 1)
                    last.then_inc(s["q_ready"], 1)
                wait("lc_kept", i * 2 + 2)
                wait("v_kept", i * 2 + 2)
                wait("k_kept", i * 2 + 2)
                wait("q_kept", i * 2 + 2)
                for hb in range(NH):
                    for r in range(NR):
                        if hb:
                            wait("s_kept", i * 8 + r + 1)
                        rows = slice(32 * r, 32 * r + 32)
                        for b in range(HB):
                            for c in range(CH):
                                bb = hb * HB + b
                                last = mm(bank[4 + r][:, (b * CH + c) * T:(b * CH + c + 1) * T],
                                          k_pair[rows, c, bb, :, :].rearrange("p a t -> p (a t)"),
                                          q_all[rows, c, bb * T:(bb + 1) * T], True, True)
                        last.then_inc(s["s_ready"], 1)
                for hb in range(NH):
                    wait("s_kept", i * 8 + hb * 4 + 4)
                    for r in range(NR):
                        for c in range(CH):
                            for b in range(HB):
                                bb = hb * HB + b
                                vp = v_pair[:, bb, c * NR + r, 0:PV]
                                last = mm(bank[hb][32 * r:32 * r + 32, (c * HB + b) * T:(c * HB + b + 1) * T],
                                          vp, probs[:, hb, r, b, c, :], True, True)
                    last.then_inc(s["y_ready"], 1)
                wait("y_kept", i * 2 + 2)
                for o in range(CH):
                    for c in range(CH):
                        last = mm(bank[2 + o][:, :], wo_s[:, c, o * P:(o + 1) * P], yt[:, c, :], c == 0, c == CH - 1)
                    last.then_inc(s["o_ready"], 1)
                wait("x1t_kept", i * 2 + 2)
                wait("s_kept", i * 8 + 8)
                for u in range(2):
                    for n in range(2):
                        for c in range(CH):
                            t = 2 * u + n
                            last = nc.tensor.transpose(bank[4 + u][:, n * D + c * P:n * D + (c + 1) * P],
                                                       x1t[:, c, t * P:(t + 1) * P], ident[:, :])
                    last.then_inc(s["x1_ready"], 1)
                for g in range(E):
                    wait("xg_made", i * E + g + 1)
                    for t in range(NT):
                        for c in range(CH):
                            last = mm(bank[ZB[t]][:, 0:D], xg[:, g % 2, c, t * P:(t + 1) * P], c2_w_s[:, c, g, :],
                                      g == 0 and c == 0, g == E - 1 and c == CH - 1)
                        if g == E - 1:
                            last.then_inc(s["z_ready"], 1)
                        elif t == NT - 1:
                            last.then_inc(s["xg_used"], 1)
                for c in range(CH):
                    if c == 0:
                        wait("y_kept", i * 2 + 2)
                        wait("z_kept", i * 4 + 4)
                        wait("hn_made", i * 8 + 4)
                    for t in range(NT):
                        last = nc.tensor.transpose(bank[c][:, t * P:(t + 1) * P], hn[:, t, c * P:(c + 1) * P], ident[:, :])
                    last.then_inc(s["ht_ready"], 1)
                wait("ht_kept", i * 2 + 2)
                wait("x1_kept", i * 2 + 2)
                for o in range(CH):
                    for c in range(CH):
                        last = mm(bank[2 + o][:, :], fq_s[:, c, o * P:(o + 1) * P], y0t[:, c, :], c == 0, c == CH - 1)
                    last.then_inc(s["qb_ready"], 1)
                for o in range(CH):
                    for c in range(CH):
                        last = mm(bank[4 + o][:, :], fk_s[:, c, o * P:(o + 1) * P], y0t[:, c, :], c == 0, c == CH - 1)
                    last.then_inc(s["kb_ready"], 1)
                for u in range(2):
                    for n in range(2):
                        t = 2 * u + n
                        for c in range(CH):
                            last = mm(bank[6 + u][:, n * D:(n + 1) * D], y0t[:, c, t * P:(t + 1) * P], fv_s[:, c, :], c == 0, c == CH - 1)
                    last.then_inc(s["vb_ready"], 1)
                wait("kb_kept", i * 2 + 2)
                wait("qb_kept", i * 2 + 2)
                wait("vb_kept", i * 2 + 2)

                def by_query(j):
                    hb, r = j // NR, j % NR
                    rows = slice(32 * r, 32 * r + 32)
                    if j >= 4:
                        wait("max_kept", i * 8 + j - 3)
                    for b in range(HB):
                        for c in range(CH):
                            bb = hb * HB + b
                            last = mm(bank[j % 4][:, (b * CH + c) * T:(b * CH + c + 1) * T],
                                      q_pair[rows, c, bb, :, :].rearrange("p a t -> p (a t)"),
                                      k_all[rows, c, bb * T:(bb + 1) * T], True, True)
                    last.then_inc(s["smax_ready"], 1)

                def by_key(j):
                    hb, r = j // NR, j % NR
                    rows = slice(32 * r, 32 * r + 32)
                    wait("shift_made", i * 8 + j + 1)
                    if j >= 4:
                        wait("p_kept", i * 8 + j - 3)
                    mm(bank[4 + j % 4][:, :], same_head[:, :, :].rearrange("p a t -> p (a t)"),
                       shift[:, j % 2, :, :].rearrange("p n t -> p (n t)"), True, False)
                    for b in range(HB):
                        for c in range(CH):
                            bb = hb * HB + b
                            last = mm(bank[4 + j % 4][:, (b * CH + c) * T:(b * CH + c + 1) * T],
                                      k_pair[rows, c, bb, :, :].rearrange("p a t -> p (a t)"),
                                      q_all[rows, c, bb * T:(bb + 1) * T], False, True)
                    last.then_inc(s["st_ready"], 1)

                for j in range(NH * NR + 2):
                    if j < NH * NR:
                        by_query(j)
                    if j >= 2:
                        by_key(j - 2)
                wait("max_kept", i * 8 + 8)
                for t in range(NT):
                    wait("p_kept", i * 8 + (t * 2 // HB) * 4 + 4)
                    for n in range(2):
                        bb = 2 * t + n
                        for c in range(CH):
                            for r in range(NR):
                                pr = c * NR + r
                                last = mm(bank[t][n * T:(n + 1) * T, pr * PW:(pr + 1) * PW],
                                          probs[:, bb // HB, r, bb % HB, c, :], v_pair[:, bb, pr, :], True, True)
                    last.then_inc(s["pv_ready"], 1)
                for c in range(CH):
                    if c == 0:
                        wait("p_kept", i * 8 + 8)
                        wait("ctx_kept", i * 4 + 4)
                    for t in range(NT):
                        last = nc.tensor.transpose(bank[4 + c][:, t * P:(t + 1) * P], ctxn[:, t, c * P:(c + 1) * P], ident[:, :])
                    last.then_inc(s["ctxt_ready"], 1)
                wait("ctxt_kept", i * 2 + 2)
                for u in range(2):
                    for n in range(2):
                        t = 2 * u + n
                        for c in range(CH):
                            last = mm(bank[6 + u][:, n * D:(n + 1) * D], yt[:, c, t * P:(t + 1) * P], fo_s[:, c, :], c == 0, c == CH - 1)
                    last.then_inc(s["wo_ready"], 1)
                wait("hn_made", i * 8 + 8)
                for c in range(CH):
                    for t in range(NT):
                        last = nc.tensor.transpose(bank[c][:, t * P:(t + 1) * P], hn[:, t, c * P:(c + 1) * P], ident[:, :])
                    last.then_inc(s["mt_ready"], 1)
                wait("mt_kept", i * 2 + 2)
                for t in range(NT):
                    for c in range(CH):
                        last = mm(bank[2][:, t * E:(t + 1) * E], y0t[:, c, t * P:(t + 1) * P], fg_s[:, c, :], c == 0, c == CH - 1)
                last.then_inc(s["gate_ready"], 1)

            wait("lg_made", NG)
            wait("mt_stored", NG)
            with pe.Fori(0, E) as e:
                with pe.Fori(0, NG) as i:
                    wait("w1_in", e * 64 + 64)
                    u0 = e * NG + i
                    for f in range(FC):
                        if f >= 4:
                            wait("h_kept", u0 * FC + f - 3)
                        else:
                            wait("h_kept", u0 * FC + f - 4 + 4)
                        for c in range(CH):
                            last = mm(bank[f % 4][:, :], w1_s[:, c, f * P:(f + 1) * P], mt[:, c, bass.ds(i * GT, GT)], c == 0, c == CH - 1)
                        last.then_inc(s["h_ready"], 1)
                    wait("h_kept", u0 * FC + FC)
                    for u in range(2):
                        wait("ye_kept", u0 * 2 + u)
                        for n in range(2):
                            t = 2 * u + n
                            o = bank[4 + u][:, n * D:(n + 1) * D]
                            mm(o, ones_row[:, :], b2_s[:, :], True, False)
                            for f in range(FC):
                                last = mm(o, ht_e[:, f, t * P:(t + 1) * P], w2_s[:, f, :], False, f == FC - 1)
                        last.then_inc(s["ye_ready"], 1)

        @block.scalar
        def _(act):
            def wait(name, v):
                act.wait_ge(s[name], START + v)

            A = nc.scalar.activation
            wait("weights_in", W_IN)
            A(base_t[:, :], decay_s[:, :], ACT.Tanh, scale=0.5).then_inc(s["derived"], 1)
            wait("consts_made", CONSTS)
            wait("mask_done", 6)
            with act.Fori(0, NG) as i:
                wait("gate_ready", i)
                wait("mt_stored", i)
                for o in range(CH):
                    wait("y0_ready", i * 2 + o + 1)
                    A(y0t[:, o, :], bank[1 + o][:, :], ACT.Identity, bias=b_base_s[:, o:o + 1]).then_inc(s["y0_kept"], 1)
                wait("cs1_ready", i + 1)
                A(cs_h[:, :], bank[3][0:DC, :], ACT.Tanh, bias=cs_b1_s[:, :]).then_inc(s["cs1_kept"], 1)

                def keep_values(bk, ready, kept):
                    for u in range(2):
                        wait(ready, i * 2 + u + 1)
                        for n in range(2):
                            for par in range(2):
                                src = bk[u][n * T:(n + 1) * T, :].rearrange("p (t q a f) -> p t q a f", t=2, q=CH * NR, a=2)[:, :, :, par, :]
                                dst = v_pair[par * T:(par + 1) * T, 4 * u + n:4 * u + n + 3:2, :, par * DH:par * DH + DH]
                                last = nc.scalar.copy(dst, src)
                        last.then_inc(s[kept], 1)

                wait("pv_ready", i * 4)
                keep_values([bank[6], bank[7]], "v_ready", "v_kept")
                for c in range(CH):
                    wait("cs2_ready", i * 2 + c + 1)
                    if c == 0:
                        wait("mt_ready", i * 2)
                    A(lc[:, c, :], bank[4 + c][:, :], ACT.Tanh, scale=0.5, bias=half_b2[:, c:c + 1]).then_inc(s["lc_kept"], 1)
                for u in range(NH):
                    wait("y_ready", i * 2 + u + 1)
                    if u == 0:
                        wait("wo_ready", i * 2)
                    nc.scalar.copy(yt[:, :, u * HB * T:(u + 1) * HB * T], bank[u][:, :].rearrange("p (c t) -> p c t", c=CH)).then_inc(s["y_kept"], 1)
                for u in range(2):
                    wait("x1_ready", i * 2 + u + 1)
                    nc.scalar.copy(acc[:, bass.ds(i * NT + 2 * u, 2), :], bank[4 + u][:, :].rearrange("p (t d) -> p t d", t=2)).then_inc(s["x1_kept"], 1)
                for c in range(CH):
                    wait("ht_ready", i * 2 + c + 1)
                    A(y0t[:, c, :], bank[c][:, :], ACT.Identity, scale=lng[:, 0, c:c + 1], bias=lng[:, 1, c:c + 1]).then_inc(s["ht_kept"], 1)
                for c in range(CH):
                    wait("qb_ready", i * 2 + c + 1)
                    nc.scalar.copy(q_all[:, c, :], bank[2 + c][:, :])
                    for par in range(2):
                        last = A(q_pair[:, c, :, par, :], bank[2 + c][:, :].rearrange("p (b t) -> p b t", t=T), ACT.Identity, scale=par_mask[:, par:par + 1])
                    last.then_inc(s["qb_kept"], 1)
                keep_values([bank[6], bank[7]], "vb_ready", "vb_kept")
                for j in range(NH * NR):
                    wait("st_ready", i * 8 + j + 1)
                    A(probs[:, j // NR, j % NR, :, :, :].rearrange("p b c t -> p (b c t)"), bank[4 + j % 4][:, :], ACT.Exp,
                      scale=float(DH) ** -0.5).then_inc(s["p_kept"], 1)
                for c in range(CH):
                    wait("ctxt_ready", i * 2 + c + 1)
                    nc.scalar.copy(yt[:, c, :], bank[4 + c][:, :]).then_inc(s["ctxt_kept"], 1)
                for c in range(CH):
                    wait("mt_ready", i * 2 + c + 1)
                    A(y0t[:, c, :], bank[c][:, :], ACT.Identity, scale=lng[:, 2, c:c + 1], bias=lng[:, 3, c:c + 1]).then_inc(s["mt_kept"], 1)
                wait("lg_made", i + 1)
                A(ex[:, :, :], lg[:, :, :], ACT.Exp).then_inc(s["ex_made"], 1)
            with act.Fori(0, E) as e:
                with act.Fori(0, NG) as i:
                    wait("w1_in", e * 64 + 64)
                    u0 = e * NG + i
                    for f in range(FC):
                        wait("h_ready", u0 * FC + f + 1)
                        if f == 0:
                            wait("ye_ready", u0 * 2)
                        A(ht_e[:, f, :], bank[f % 4][:, :], ACT.Gelu_apprx_tanh, bias=b1_s[:, f:f + 1]).then_inc(s["h_kept"], 1)

        STEPS = 27

        @block.vector
        def _(dve):
            V = nc.vector
            steps = [0, 0]

            def wait(name, v):
                dve.wait_ge(s[name], START + v)

            def step(ins, i=None):
                steps[0] += 1
                ins.then_inc(s["dve_steps"], 1)
                dve.wait_ge(s["dve_steps"], START + steps[0] if i is None else i * STEPS + (START + steps[1] + steps[0]))

            def tick():
                V.tensor_copy(tick_s[:, 0:1], tick_s[:, 1:2])

            V.memset(tick_s[:, :], 0.0)
            wait("consts_made", CONSTS)
            wait("weights_in", W_IN)
            for half in range(2):
                rows = slice(half * T, half * T + T)
                V.memset(same_head[rows, 1 - half, :], 0.0)
                V.memset(v_pair[rows, :, :, PV + half:PV + half + 1], 1.0)
                V.tensor_copy(diag_ones[rows, :], ident[rows, rows]).then_inc(s["mask_done"], 1)
            V.tensor_reduce(par_mask[:, 0:1], ident[:, :].rearrange("p (q a f) -> p q a f", a=2, f=DH)[:, :, 0, :], mybir.AxisListType.XY, ALU.add).then_inc(s["mask_done"], 1)
            V.tensor_reduce(par_mask[:, 1:2], ident[:, :].rearrange("p (q a f) -> p q a f", a=2, f=DH)[:, :, 1, :], mybir.AxisListType.XY, ALU.add).then_inc(s["mask_done"], 1)
            V.tensor_scalar(half_b2[:], cs_b2_s[:], 0.5, None, ALU.mult).then_inc(s["mask_done"], 1)
            step(V.tensor_tensor(c2_w_s[:, :, :, :], c2_w_s[:, :, :, :],
                                 c2_mask_s[:, :, :].unsqueeze(2).to_broadcast([P, CH, E, D]), ALU.mult))
            wait("derived", 1)
            step(V.tensor_scalar(base_t[:, :], base_t[:, :], 0.5, 0.5, ALU.mult, ALU.add))
            V.tensor_scalar(base_11[:, :], base_t[:, :], 1.1, None, ALU.mult)
            V.tensor_scalar(base_01[:, :], base_t[:, :], 0.1, None, ALU.mult).then_inc(s["mask_done"], 1)
            wait("mask_done", 6)
            steps[1] = steps[0]

            with dve.Fori(0, NG) as i:
                steps[0] = 0
                wait("lora_ready", i + 1)
                V.scalar_tensor_tensor(out=lora_h[:, :].rearrange("p (b t) -> p b t", t=T), in0=bank[0][:, :].rearrange("p (b t) -> p b t", t=T),
                                       scalar=LORA_SCALE, in1=cond_er[:, bass.ds(i * GB, GB)].unsqueeze(2).to_broadcast([P, GB, T]),
                                       op0=ALU.mult, op1=ALU.mult).then_inc(s["lora_kept"], 1)
                wait("z_ready", i * 4)
                for c in range(CH):
                    wait("lc_kept", i * 2 + c + 1)
                    ins = V.tensor_scalar(lam[:, c * GT:(c + 1) * GT], lc[:, c, :], base_01[:, c:c + 1], base_11[:, c:c + 1], ALU.mult, ALU.add)
                step(ins, i)
                step(V.tensor_scalar(lam[:, :], lam[:, :], LAM_MAX, 0.0, ALU.min, ALU.max), i)
                starts = lam[:, 0:CH * GT:HALF]
                step(V.tensor_copy(lam_first[:, 0:CH * GT:HALF], starts), i)
                step(V.memset(starts, 0.0), i)
                step(V.tensor_tensor_scan(cum[:, :], lam[:, :], lam_first[:, :], 0.0, ALU.mult, ALU.add), i)
                step(V.reciprocal(cum_mid[:, :], cum[:, HALF - 1:CH * GT:T]), i)
                first_half = cum[:, :].rearrange("p (n t) -> p n t", t=T)[:, :, 0:HALF]
                step(V.tensor_tensor(first_half, first_half, cum_mid[:, :].unsqueeze(2).to_broadcast([P, CH * GB, HALF]), ALU.mult), i)
                step(V.reciprocal(cum_inv[:, :], cum[:, :]), i)
                wait("st_ready", i * 8)
                for c in range(CH):
                    wait("k_ready", i * 2 + c + 1)
                    for par in range(2):
                        ins = V.scalar_tensor_tensor(out=k_pair[:, c, :, par, :], in0=bank[c][:, :].rearrange("p (b t) -> p b t", t=T),
                                                     scalar=par_mask[:, par:par + 1],
                                                     in1=cum_inv[:, c * GT:(c + 1) * GT].rearrange("p (b t) -> p b t", t=T),
                                                     op0=ALU.mult, op1=ALU.mult)
                    ins.then_inc(s["k_kept"], 1)
                for c in range(CH):
                    wait("q_ready", i * 2 + c + 1)
                    V.tensor_tensor(q_all[:, c, :], bank[2 + c][:, :], cum[:, c * GT:(c + 1) * GT], ALU.mult).then_inc(s["q_kept"], 1)
                wait("pv_ready", i * 4)
                for j in range(NH * NR):
                    wait("s_ready", i * 8 + j + 1)
                    V.tensor_tensor(probs[:, j // NR, j % NR, :, :, :].rearrange("p b c t -> p (b c) t"),
                                    bank[4 + j % NR][:, :].rearrange("p (n t) -> p n t", t=T),
                                    causal[:, :].unsqueeze(1).to_broadcast([P, HB * CH, T]), ALU.mult).then_inc(s["s_kept"], 1)
                for o in range(CH):
                    wait("o_ready", i * 2 + o + 1)
                    V.tensor_tensor(x1t[:, o, :], bank[2 + o][:, :], xt[:, o, :], ALU.add).then_inc(s["x1t_kept"], 1)
                wait("x1t_kept", i * 2 + 2)
                for g in range(E):
                    if g >= 2:
                        wait("xg_used", i * 7 + g - 1)
                    else:
                        wait("z_ready", i * 4)
                    for c in range(CH):
                        ins = V.tensor_tensor(xg[:, g % 2, c, :].rearrange("p (b t) -> p b t", t=T),
                                              x1t[:, c, :].rearrange("p (b t) -> p b t", t=T),
                                              cond_all[:, g, bass.ds(i * GB, GB)].unsqueeze(2).to_broadcast([P, GB, T]), ALU.mult)
                    ins.then_inc(s["xg_made"], 1)

                def norm(k):
                    for t in range(NT):
                        ins = V.bn_stats(stats[:, t, :], z[:, t, :])
                    step(ins, i)
                    tick()
                    for t in range(NT):
                        ins = V.bn_aggr(mv[:, t, :], stats[:, t, :])
                    step(ins, i)
                    V.tensor_scalar(var_e[:, :], mv[:, :, 1], EPS, None, ALU.add).then_inc(s["var_made"], 1)
                    wait("rstd_made", i * 2 + k + 1)
                    for t in range(NT):
                        V.tensor_scalar(hn[:, t, :], z[:, t, :], mv[:, t, 0:1], rstd[:, t:t + 1], ALU.subtract, ALU.mult).then_inc(s["hn_made"], 1)

                for t in range(NT):
                    wait("z_ready", i * 4 + t + 1)
                    ins = V.tensor_tensor(z[:, t, :], bank[ZB[t]][:, 0:D], c2_bias_s[:, :], ALU.add)
                    ins.then_inc(s["z_kept"], 1)
                wait("z_kept", i * 4 + 4)
                norm(0)
                for c in range(CH):
                    wait("kb_ready", i * 2 + c + 1)
                    V.tensor_copy(k_all[:, c, :], bank[4 + c][:, :])
                    for par in range(2):
                        ins = V.tensor_scalar(k_pair[:, c, :, par, :], bank[4 + c][:, :].rearrange("p (b t) -> p b t", t=T),
                                              par_mask[:, par:par + 1], None, ALU.mult)
                    ins.then_inc(s["kb_kept"], 1)
                for j in range(NH * NR):
                    wait("smax_ready", i * 8 + j + 1)
                    V.tensor_reduce(row_max[:, j // NR, j % NR, :, :].rearrange("p b c -> p (b c)"),
                                    bank[j % 4][:, :].rearrange("p (n t) -> p n t", t=T), AX_X, ALU.max,
                                    negate=True).then_inc(s["max_kept"], 1)
                for t in range(NT):
                    wait("pv_ready", i * 4 + t + 1)
                    pv = bank[t][:, 0:CH * NR * PW].rearrange("p (h f) -> p h f", f=PW)
                    step(V.reciprocal(sum_inv[:, t, :, :], pv[:, :, PV:PW]), i)
                    V.tensor_tensor(ctxn[:, t, :].rearrange("p (h a f) -> p h a f", a=2, f=DH),
                                    pv[:, :, 0:PV].rearrange("p h (a f) -> p h a f", a=2),
                                    sum_inv[:, t, :, :].unsqueeze(3).to_broadcast([P, CH * NR, 2, DH]), ALU.mult).then_inc(s["ctx_kept"], 1)
                for u in range(2):
                    wait("wo_ready", i * 2 + u + 1)
                    V.tensor_tensor(z[:, 2 * u:2 * u + 2, :], bank[6 + u][:, :].rearrange("p (t d) -> p t d", t=2),
                                    z[:, 2 * u:2 * u + 2, :], ALU.add).then_inc(s["z2_kept"], 1)
                wait("z2_kept", i * 2 + 2)
                wait("ht_ready", i * 2 + 2)
                norm(1)
                wait("x1_kept", i * 2 + 2)
                V.tensor_tensor(acc[:, bass.ds(i * NT, NT), :], acc[:, bass.ds(i * NT, NT), :], z[:, :, :], ALU.add).then_inc(s["acc_made"], 1)
                wait("gate_ready", i + 1)
                logits = bank[2][:, 0:NT * E].rearrange("p (t e) -> p t e", e=E)
                step(V.tensor_copy(lg[:, :, :], logits), i)
                tick()
                for t in range(NT):
                    ins = V.max(top[:, t, :], lg[:, t, :])
                step(ins, i)
                tick()
                for t in range(NT):
                    ins = V.max_index(top_i[:, t, :], top[:, t, :], lg[:, t, :])
                step(ins, i)
                V.tensor_copy(top_f[:, :, :], top_i[:, :, :])
                step(V.tensor_tensor(lg[:, :, :], lg[:, :, :], top[:, :, 0:1].to_broadcast([P, NT, E]), ALU.subtract), i)
                for j in range(2):
                    ins = V.tensor_tensor(pick[:, :, j, :], iota8[:, :].unsqueeze(1).to_broadcast([P, NT, E]),
                                          top_f[:, :, j:j + 1].to_broadcast([P, NT, E]), ALU.is_equal)
                ins.then_inc(s["lg_made"], 1)
                wait("lg_made", i + 1)
                wait("ex_made", i + 1)
                step(V.tensor_reduce(ex_sum[:, :], ex[:, :, :], AX_X, ALU.add), i)
                step(V.reciprocal(ex_sum[:, :], ex_sum[:, :]), i)
                step(V.tensor_tensor(ex[:, :, :], ex[:, :, :], ex_sum[:, :].unsqueeze(2).to_broadcast([P, NT, E]), ALU.mult), i)
                step(V.tensor_tensor(pick[:, :, 0, :], pick[:, :, 0, :], pick[:, :, 1, :], ALU.add), i)
                step(V.tensor_tensor(ex[:, :, :], ex[:, :, :], pick[:, :, 0, :], ALU.mult), i)
                step(V.tensor_reduce(two_sum[:, :], ex[:, :, :], AX_X, ALU.add), i)
                step(V.reciprocal(two_sum[:, :], two_sum[:, :]), i)
                V.tensor_tensor(gates[:, bass.ds(i * NT, NT), :], ex[:, :, :], two_sum[:, :].unsqueeze(2).to_broadcast([P, NT, E]), ALU.mult).then_inc(s["gates_made"], 1)
                assert steps[0] == STEPS
            wait("gates_made", NG)
            wait("acc_made", NG)
            with dve.Fori(0, E) as e:
                with dve.Fori(0, NG) as i:
                    u0 = e * NG + i
                    for u in range(2):
                        wait("ye_ready", u0 * 2 + u + 1)
                        wait("ye_kept", u0 * 2 + u)
                        for n in range(2):
                            a = acc[:, bass.ds(i * NT + 2 * u + n, 1), :].rearrange("p o d -> p (o d)")
                            ins = V.scalar_tensor_tensor(out=a, in0=bank[4 + u][:, n * D:(n + 1) * D],
                                                         scalar=gates[:, bass.ds(i * NT + 2 * u + n, 1), bass.ds(e, 1)].rearrange("p o d -> p (o d)"),
                                                         in1=a, op0=ALU.mult, op1=ALU.add)
                        ins.then_inc(s["ye_kept"], 1)


ZB = [6, 7, 2, 3]


def kernel(x, cond_8, L0_cond_W_base, L0_cond_b_base, L0_cond_As, L0_cond_Bs, L0_attn_q_w, L0_attn_k_w, L0_attn_v_w,
           L0_attn_o_w, L0_attn_cs_w1, L0_attn_cs_b1, L0_attn_cs_w2, L0_attn_cs_b2, L0_attn_decay_params,
           L0_cond2_weight, L0_cond2_mask, L0_cond2_bias, L0_ffn_ln1_g, L0_ffn_ln1_b, L0_ffn_ln2_g, L0_ffn_ln2_b,
           L0_ffn_Wq, L0_ffn_Wk, L0_ffn_Wv, L0_ffn_Wo, L0_ffn_Wg, L0_ffn_W1, L0_ffn_b1, L0_ffn_W2, L0_ffn_b2):
    import numpy as np
    import concourse.bacc as bacc
    from concourse.bass_utils import run_bass_kernel_spmd

    def rows(a):
        return np.asarray(a).reshape(-1, P, a.shape[-1]).transpose(1, 0, 2)

    def cols(a):
        return np.asarray(a).reshape(-1, P).T

    t = np.transpose
    arrays = {
        "x_t": rows(t(np.asarray(x).reshape(B * T, D))),
        "cond_t": t(np.asarray(cond_8)),
        "w_base": rows(t(L0_cond_W_base)),
        "b_base": cols(L0_cond_b_base),
        "lora_a": rows(t(np.asarray(L0_cond_As).reshape(E * R, D))),
        "lora_b": t(L0_cond_Bs, (0, 2, 1)).reshape(E * R, D),
        "wq": rows(t(L0_attn_q_w)), "wk": rows(t(L0_attn_k_w)), "wv": rows(t(L0_attn_v_w)), "wo": rows(t(L0_attn_o_w)),
        "cs_w1": rows(t(L0_attn_cs_w1)),
        "cs_b1": np.asarray(L0_attn_cs_b1).reshape(DC, 1),
        "cs_w2": np.repeat(t(L0_attn_cs_w2), DH, axis=1),
        "cs_b2": cols(np.repeat(L0_attn_cs_b2, DH)),
        "decay": cols(np.asarray(L0_attn_decay_params).reshape(D)),
        "c2_w": t(np.asarray(L0_cond2_weight).reshape(E, D, CH, P), (3, 2, 0, 1)),
        "c2_mask": rows(t(L0_cond2_mask)),
        "c2_bias": np.asarray(L0_cond2_bias),
        "ln1_g": cols(L0_ffn_ln1_g), "ln1_b": cols(L0_ffn_ln1_b), "ln2_g": cols(L0_ffn_ln2_g), "ln2_b": cols(L0_ffn_ln2_b),
        "fq": rows(L0_ffn_Wq), "fk": rows(L0_ffn_Wk), "fv": rows(L0_ffn_Wv), "fo": rows(L0_ffn_Wo), "fg": rows(L0_ffn_Wg),
        "fw1": t(np.asarray(L0_ffn_W1).reshape(E, CH, P, F), (2, 0, 1, 3)),
        "fb1": t(np.asarray(L0_ffn_b1).reshape(E, FC, P), (2, 0, 1)),
        "fw2": t(np.asarray(L0_ffn_W2).reshape(E, FC, P, D), (2, 0, 1, 3)),
        "fb2": np.asarray(L0_ffn_b2),
        "ident_in": np.eye(P, dtype=np.float32),
    }
    arrays = {n: np.ascontiguousarray(a) for n, a in arrays.items()}
    nc = bacc.Bacc("TRN2", target_bir_lowering=False, num_devices=1)
    args = [nc.dram_tensor(n, a.shape, mybir.dt.from_np(a.dtype), kind="ExternalInput").ap() for n, a in arrays.items()]
    order = ("x_t cond_t w_base b_base lora_a lora_b wq wk wv wo cs_w1 cs_b1 cs_w2 cs_b2 decay c2_w c2_mask c2_bias "
             "ln1_g ln1_b ln2_g ln2_b fq fk fv fo fg fw1 fb1 fw2 fb2 ident_in").split()
    assert order == list(arrays)
    out = nc.dram_tensor("out", (B * T, D), F32, kind="ExternalOutput").ap()
    bass_adaln_attn_ffn(nc, *args, out)
    got = run_bass_kernel_spmd(nc, [arrays], core_ids=[0])
    return got.results[0]["out"].reshape(B, T, D)
```

```python
import concourse.bass as bass
from concourse import mybir
from contextlib import ExitStack

F32 = mybir.dt.float32
F16 = mybir.dt.float16
U32 = mybir.dt.uint32
I32 = mybir.dt.int32
ALU = mybir.AluOpType
ACT = mybir.ActivationFunctionType
AX_X = mybir.AxisListType.X

P = 128
B, T, D = 64, 64, 256
H, DH = 16, 16
E, R = 8, 16
F = 1024
CH = D // P
FC = F // P
GB = 8
GT = GB * T
NG = B // GB
NT = GT // P
NR = 4
HB = 4
NH = GB // HB
NTOK = B * T
K = 2
REGION = NTOK + P
NROWS = E * REGION + P
NJ = NTOK * K // P + E
UNROLL = 4
NI = NJ // UNROLL
NJT = NJ + UNROLL
G_AT = 2 * D
ID_AT = G_AT + 2 * E
ROW = ID_AT + 2
WE = 2 * D * F // P
W2_AT = WE // 2
W_SCALE = 256.0
DC = 64
LORA_SCALE = 32.0 / R
LAM_MAX = 0.9995
EPS = 1e-05
PV = 2 * DH
PW = PV + 2


def bass_adaln_attn_ffn(nc, x_t, cond_t, w_base, b_base, lora_a, lora_b, wq, wk, wv, wo, cs_w1, cs_b1, cs_w2,
                        cs_b2, decay, c2_w, c2_mask, c2_bias, ln1_g, ln1_b, ln2_g, ln2_b, fq, fk, fv, fo, fg,
                        fw, fb1, fb2, ident_in, pad_ids, out):
    with ExitStack() as ctx:
        def sb(name, shape, dt=F32):
            return ctx.enter_context(nc.sbuf_tensor(name, shape, dt))

        def sem(name):
            return ctx.enter_context(nc.semaphore(name))

        bank = [ctx.enter_context(nc.psum_tensor(f"bank{i}", [P, 512], F32)) for i in range(8)]

        tbank = [b[:, 0:2 * CH * P // 2].bitcast(F16) for b in bank[6:8]]

        w_all = sb("w_all", [P, E, 2, WE], F16)
        arena = w_all[:, :, :, :].rearrange("p e s w -> p (e s w)").bitcast(F32)
        taken = [0]

        def carve(shape, dt=F32):
            size = 4
            n = 1
            for k in shape[1:]:
                n *= k
            words = n * (2 if dt == F16 else 4) // 4
            a = arena[:, taken[0]:taken[0] + words]
            taken[0] += words
            
            if dt != F32:
                a = a.bitcast(dt)
            names = "abcdefg"[:len(shape) - 1]
            if len(names) > 1:
                a = a.rearrange(f"p ({' '.join(names)}) -> p {' '.join(names)}", **dict(zip(names[1:], shape[2:])))
            return a

        xs = nc.dram_tensor("rows_by_expert", [NROWS, ROW // 2], I32, kind="Internal").ap()
        w_split = nc.dram_tensor("w_split", [P, E, 2, WE], F16, kind="Internal").ap()

        w_base_s = carve([P, CH, D])
        lora_a_s = carve([P, CH, P])
        lora_b_s = carve([P, D])
        wq_s, wk_s, wv_s, wo_s = [carve([P, CH, D]) for n in ("wq_s", "wk_s", "wv_s", "wo_s")]
        fq_s, fk_s, fv_s, fo_s = [carve([P, CH, D]) for n in ("fq_s", "fk_s", "fv_s", "fo_s")]
        cs_w1_s = sb("cs_w1_s", [P, CH, DC])
        cs_w2_s = sb("cs_w2_s", [DC, D])
        fg_s = sb("fg_s", [P, CH, E])
        c2_w_s = carve([P, CH, E, D])
        c2_mask_s = sb("c2_mask_s", [P, CH, D])
        c2_bias_s = sb("c2_bias_s", [P, D])
        cond_er = sb("cond_er", [P, B])
        cond_all = sb("cond_all", [P, E, B])
        b_base_s = sb("b_base_s", [P, CH])
        cs_b1_s = sb("cs_b1_s", [DC, 1])
        cs_b2_s = sb("cs_b2_s", [P, CH])
        decay_s = sb("decay_s", [P, CH])
        lng = sb("lng", [P, 2, CH])
        ident = sb("ident", [P, P])
        half_b2 = sb("half_b2", [P, CH])
        base_t = sb("base_t", [P, CH])
        base_11 = sb("base_11", [P, CH])
        base_01 = sb("base_01", [P, CH])
        par_mask = sb("par_mask", [P, 2])
        causal = sb("causal", [P, T])
        zeros = sb("zeros", [P, D])
        scale_w = sb("scale_w", [P, 2])
        same_head = sb("same_head", [P, 2, T])
        diag_ones = sb("diag_ones", [P, T])
        expo = sb("expo", [P, NT])
        iota8 = sb("iota8", [P, E])
        iota8u = sb("iota8u", [P, E], mybir.dt.int32)

        xt = carve([P, CH, GT])
        lora_h = carve([P, GT])
        y0t = carve([P, CH, GT])
        cs_h = carve([P, GT])
        decay_work = carve([P, 2, CH * GT])
        lam, cum_inv = decay_work[:, 0, :], decay_work[:, 1, :]
        lam_first = carve([P, CH * GT])
        cum = carve([P, CH * GT])
        cum_mid = carve([P, CH * GB])
        v_pair = carve([P, GB, NR * CH, PW])
        k_pair = carve([P, CH, GB, 2, T])
        q_pair = carve([P, CH, GB, 2, T])
        q_all = carve([P, CH, GT])
        k_all = carve([P, CH, GT])
        probs = carve([P, NH, NR, HB, CH, T])
        yt = carve([P, CH, GT])
        x1t = xt
        xg = decay_work[:, :, :].rearrange("p g (c t) -> p g c t", c=CH)
        z = carve([P, NT, D])
        hn = carve([P, NT, D])
        lc = hn[:, :, :].rearrange("p n d -> p (n d)").rearrange("p (c t) -> p c t", c=CH)
        tick_s = sb("tick_s", [P, 2])
        pool_tick = sb("pool_tick", [P, 2])
        stats = sb("stats", [P, NT, 6])
        mv = sb("mv", [P, NT, 2])
        var_e = sb("var_e", [P, NT])
        rstd = sb("rstd", [P, NT])
        row_max = sb("row_max", [P, NH, NR, HB, CH])
        shift = sb("shift", [P, 2, HB * CH, T])
        ctxn = k_all[:, :, :].rearrange("p c t -> p (c t)").rearrange("p (n d) -> p n d", d=D)
        sum_inv = sb("sum_inv", [P, NT, CH * NR, 2])
        lg = sb("lg", [P, NT, E])
        top = sb("top", [P, NT, 8])
        top_i = sb("top_i", [P, NT, 8], U32)
        top_f = sb("top_f", [P, NT, 8])
        ex = sb("ex", [P, NT, E])
        ex_sum = sb("ex_sum", [P, NT])
        two_sum = sb("two_sum", [P, NT])
        wts = sb("wts", [P, NT, 2])
        pick = sb("pick", [P, NT, 2, E])

        wts_all = sb("wts_all", [P, NT, E])
        m_tm = sb("m_tm", [P, NT, D])
        acc = sb("acc", [P, NT, D])
        stage = sb("stage", [P, WE // 2])
        halves = sb("halves", [P, 2, WE // 2], F16)
        rows = sb("rows", [P, NT, ROW], F16)
        ln2_rows = sb("ln2_rows", [P, 2, D])
        lower = sb("lower", [P, P])
        ones = sb("ones", [P, P])
        picked = sb("picked", [P, NT, E])
        rank = sb("rank", [P, NT, E])
        tot = sb("tot", [P, NT, E])
        before = sb("before", [P, NT + 1, E])
        region0 = sb("region0", [P, E])
        slot = sb("slot", [P, K, NT, E])
        pos_f = sb("pos_f", [P, K, NT])
        pos_u = sb("pos_u", [P, K, NT], U32)
        tok_f = sb("tok_f", [P, 1])
        tok_g = sb("tok_g", [P, NT])

        pad_row = sb("pad_row", [P, ROW], F16)
        pad_pos = sb("pad_pos", [P, E], U32)
        alone_pos = sb("alone_pos", [P, 1], U32)
        pad_pos_f = sb("pad_pos_f", [P, E])
        pid_u = sb("pid_u", [P, 1], I32)
        pid = sb("pid", [P, 1])
        tile_k = sb("tile_k", [P, NTOK // P + 1])
        tile_ku = sb("tile_ku", [P, NJT], I32)
        tile_j = sb("tile_j", [P, NJT])
        cmp_k = sb("cmp_k", [P, E, NTOK // P + 1])
        n_tiles = sb("n_tiles", [P, E])
        tiles_to = sb("tiles_to", [P, E])
        past = sb("past", [P, NJT, E])
        past_n = sb("past_n", [P, NJT, E])
        tile_e = sb("tile_e", [P, NJT])
        tile_first = sb("tile_first", [P, NJT])
        tile_row = sb("tile_row", [P, NJT])
        tile_e_i = sb("tile_e_i", [P, NJT], I32)
        tile_row_i = sb("tile_row_i", [P, NJT], I32)
        ones8 = sb("ones8", [P, E])
        b1_all = sb("b1_all", [P, E, FC])
        b2_f = probs[0:1, :, :, :, :, :].rearrange("p n r b c t -> p (n r b c t)")[:, 0:E * D].rearrange("p (e d) -> p e d", e=E)
        b2_s = sb("b2_s", [1, 2, E, D], F16)
        ones_h = sb("ones_h", [1, P], F16)
        id_h = sb("id_h", [P, P], F16)
        srows = sb("srows", [P, UNROLL, ROW], F16)
        sxt = sb("sxt", [P, 2, 2 * CH, P], F16)
        hid = stage[:, :].rearrange("p (k f t) -> p k f t", k=2, f=FC)
        hid_s = halves[:, :, :].rearrange("p s w -> p (s w)").rearrange("p (k s f t) -> p k s f t", k=2, s=2, f=FC)
        ys = sb("ys", [P, 2, D])

        names = ("weights_in xt_in consts_made mask_done derived "
                 "lora_ready lora_kept y0_ready y0_kept cs1_ready cs1_kept cs2_ready lc_kept v_ready v_kept "
                 "k_ready k_kept q_ready q_kept s_ready s_kept y_ready y_kept o_ready x1t_kept "
                 "xg_made xg_used x1_ready x1_kept z_ready z_kept var_made rstd_made hn_made ht_ready ht_kept "
                 "qb_ready qb_kept kb_ready kb_kept vb_ready vb_kept smax_ready max_kept shift_made st_ready p_kept "
                 "pv_ready ctx_kept ctxt_ready ctxt_kept wo_ready z2_kept acc_made mt_ready mt_kept gate_ready lg_made "
                 "ex_made gates_made dve_steps stage_in split_made split_out m_made rows_made ranks_ready ranks_kept pos_made scattered acc_out "
                 "pool_steps ticks pads_out tables_made experts_made zero_rows w_in t_ready xt_kept h_ready h_kept hid_split hi_made "
                 "ye_ready ye_kept added ").split()
        names += [f"srows_in{k}" for k in range(UNROLL)] + [f"w_in{e}" for e in range(E)]
        s = {n: sem(n) for n in names}

        CONSTS = 17
        POOL_STEPS = 6
        START = 1
        software = ("scattered", "added", "pads_out")

        print("arena", taken[0], E * WE)
        HALF = T // 2
        seg = "p (n h t) -> p n h t"
        F_MID = cum[:, :].rearrange(seg, h=2, t=HALF)

        block = ctx.enter_context(nc.Block())
        N_LOADS = 0
        loads = [
            (w_base_s, w_base), (lora_a_s, lora_a), (lora_b_s, lora_b), (wq_s, wq), (wk_s, wk), (wv_s, wv),
            (wo_s, wo), (fq_s, fq), (fk_s, fk), (fv_s, fv), (fo_s, fo), (cs_w1_s, cs_w1), (cs_w2_s, cs_w2),
            (fg_s, fg), (c2_w_s, c2_w), (c2_mask_s, c2_mask), (cs_b1_s, cs_b1), (cs_b2_s, cs_b2),
            (decay_s, decay), (b_base_s, b_base), (ident, ident_in), (b1_all, fb1), (b2_f, fb2)]

        @block.sync
        def _(sp):
            for n in names:
                if n not in software:
                    sp.sem_inc(s[n], START)
            for dst, src in loads:
                sp.dma_start(dst[:], src).then_inc(s["weights_in"], 16)
            for j, src in enumerate((ln1_g, ln1_b)):
                sp.dma_start(lng[:, j, :], src).then_inc(s["weights_in"], 16)
            sp.dma_start(c2_bias_s[:], c2_bias.partition_broadcast(P)).then_inc(s["weights_in"], 16)
            sp.dma_start(cond_all[:], cond_t.partition_broadcast(P)).then_inc(s["weights_in"], 16)
            for e in range(E):
                sp.dma_start(cond_er[e * R:(e + 1) * R, :], cond_t[e, :].partition_broadcast(R)).then_inc(s["weights_in"], 16)
            for j in range(2):
                sp.dma_start(ln2_rows[:, j, :], (ln2_g, ln2_b)[j].partition_broadcast(P)).then_inc(s["weights_in"], 16)
            sp.wait_ge(s["consts_made"], START + CONSTS)
            sp.dma_start(out[NTOK:NTOK + P, :], zeros[:, :]).then_inc(s["zero_rows"], 16)
            sp.dma_start(pad_row[:, ID_AT:ID_AT + 2].bitcast(I32), pad_ids).then_inc(s["zero_rows"], 16)
            with sp.Fori(0, NG) as i:
                sp.wait_ge(s["xg_made"], START + i * E)
                sp.wait_ge(s["x1_ready"], START + i * 2)
                sp.dma_start(xt[:, :, :], x_t[:, :, bass.ds(i * GT, GT)]).then_inc(s["xt_in"], 16)
                for k in range(2):
                    sp.wait_ge(s["split_made"], START + i * 2 + k)
                    sp.dma_start(stage[:, :], fw[:, bass.ds(i, 1), k, :].rearrange("p e w -> p (e w)")).then_inc(s["stage_in"], 16)
                    sp.wait_ge(s["split_made"], START + i * 2 + k + 1)
                    sp.dma_start(w_split[:, bass.ds(i, 1), :, k * W2_AT:(k + 1) * W2_AT].rearrange("p e s w -> p (e s) w"),
                                 halves[:, :, :]).then_inc(s["split_out"], 16)
                sp.wait_ge(s["acc_made"], START + i + 1)
                sp.dma_start(out[bass.ds(i * GT, GT), :].rearrange("(n p) d -> p n d", p=P), acc[:, :, :]).then_inc(s["acc_out"], 16)
            sp.wait_ge(s["split_out"], START + NG * 2 * 16)
            sp.wait_ge(s["acc_out"], START + NG * 16)
            sp.wait_ge(s["scattered"], 16 + NG * K * NT * 16)
            sp.wait_ge(s["lg_made"], START + NG)
            sp.wait_ge(s["gate_ready"], START + NG)
            sp.wait_ge(s["rows_made"], START + NG)
            sp.wait_ge(s["zero_rows"], START + 32)
            for e in range(E):
                sp.dma_start(w_all[:, e, :, :], w_split[:, e, :, :]).then_inc(s[f"w_in{e}"], 16)
                if e == 0:
                    sp.wait_ge(s["pads_out"], E * 16)
                    sp.wait_ge(s["tables_made"], START + 2)

            def load(i, k):
                j = i * UNROLL + k
                row = sp.value_load(tile_row_i[0:1, bass.ds(j, 1)], min_val=0, max_val=E * REGION)
                sp.dma_start(srows[:, k, :].bitcast(I32), xs[bass.ds(row, P), :]).then_inc(s[f"srows_in{k}"], 16)

            for k in range(UNROLL):
                load(0, k)
            with sp.Fori(1, NI) as i:
                for k in range(UNROLL):
                    sp.wait_ge(s["added"], 16 + (i * UNROLL + (k - UNROLL + 1)) * 16)
                    load(i, k)
            sp.wait_ge(s["added"], 16 + (NJ - UNROLL + 1) * 16)
            load(NI, 0)
            sp.wait_ge(s["added"], 16 + NJ * 16)
            sp.wait_ge(s["srows_in0"], START + (NI + 1) * 16)

        W_IN = 16 * (len(loads) + 2 + 2 + E + 2)

        @block.gpsimd
        def _(pool):
            nc.gpsimd.memset(par_mask[:], 1.0).then_inc(s["consts_made"], 1)
            nc.gpsimd.memset(causal[:], 1.0).then_inc(s["consts_made"], 1)
            nc.gpsimd.memset(same_head[:], 1.0).then_inc(s["consts_made"], 1)
            nc.gpsimd.memset(expo[:], -0.5).then_inc(s["consts_made"], 1)
            nc.gpsimd.memset(ones[:], 1.0).then_inc(s["consts_made"], 1)
            nc.gpsimd.memset(lower[:], 1.0).then_inc(s["consts_made"], 1)
            nc.gpsimd.memset(zeros[:], 0.0).then_inc(s["consts_made"], 1)
            nc.gpsimd.memset(pad_row[:], 0.0).then_inc(s["consts_made"], 1)
            nc.gpsimd.memset(ones_h[:], 1.0).then_inc(s["consts_made"], 1)
            nc.gpsimd.iota(pid_u[:], [[0, 1]], base=0, channel_multiplier=1).then_inc(s["consts_made"], 1)
            nc.gpsimd.iota(tile_ku[:], [[1, NJT]], base=0, channel_multiplier=0).then_inc(s["consts_made"], 1)
            nc.gpsimd.memset(v_pair[:], 0.0).then_inc(s["consts_made"], 1)
            nc.gpsimd.memset(lam_first[:], 0.0).then_inc(s["consts_made"], 1)
            nc.gpsimd.iota(iota8u[:], [[1, E]], base=0, channel_multiplier=0).then_inc(s["consts_made"], 1)
            pool.wait_ge(s["consts_made"], START + 14)
            nc.gpsimd.affine_select(out=lower[:, :], in_=lower[:, :], compare_op=ALU.is_gt, fill=0.0,
                                    base=0, pattern=[[1, P]], channel_multiplier=-1).then_inc(s["consts_made"], 1)
            pool.wait_ge(s["consts_made"], START + 15)
            for half in range(2):
                rows_ = slice(half * T, half * T + T)
                nc.gpsimd.affine_select(out=causal[rows_, :], in_=causal[rows_, :], compare_op=ALU.is_ge, fill=0.0,
                                        base=0, pattern=[[1, T]], channel_multiplier=-1).then_inc(s["consts_made"], 1)
                pool.wait_ge(s["consts_made"], START + 16 + half)
            pool.wait_ge(s["consts_made"], START + CONSTS)
            pool.wait_ge(s["mask_done"], START + 6)
            G = nc.gpsimd
            steps = [0]

            def step(ins, i):
                steps[0] += 1
                ins.then_inc(s["pool_steps"], 1)
                pool.wait_ge(s["pool_steps"], i * POOL_STEPS + (START + steps[0]))

            def tick(n):
                pool.wait_ge(s["ticks"], START + n)
                G.tensor_tensor(pool_tick[:, 0:1], pool_tick[:, 1:2], pool_tick[:, 1:2], ALU.mult).then_inc(s["ticks"], 1)

            def split_weights(i, k):
                pool.wait_ge(s["stage_in"], START + i * 32 + k * 16 + 16)
                step(G.tensor_tensor(stage[:, :], stage[:, :], scale_w[:, 0:1].to_broadcast([P, W2_AT]), ALU.mult), i)
                pool.wait_ge(s["split_out"], START + i * 32 + k * 16)
                step(G.tensor_tensor(halves[:, 0, :], stage[:, :], scale_w[:, 1:2].to_broadcast([P, W2_AT]), ALU.add), i)
                G.tensor_tensor(halves[:, 1, :], stage[:, :], halves[:, 0, :], ALU.subtract).then_inc(s["split_made"], 1)

            pool.wait_ge(s["zero_rows"], START + 32)
            pool.wait_ge(s["mask_done"], START + 6)
            G.indirect_dma_start(out=xs[:, :], out_offset=bass.IndirectOffsetOnAxis(ap=alone_pos[:, :], axis=0),
                                 in_=pad_row[:, :].bitcast(I32), in_offset=None).then_inc(s["scattered"], 16)
            G.indirect_dma_start(out=out[:, :], out_offset=bass.IndirectOffsetOnAxis(ap=pad_row[:, ID_AT:ID_AT + 2].bitcast(U32), axis=0),
                                 in_=zeros[:, :], in_offset=None, compute_op=ALU.add).then_inc(s["added"], 16)
            with pool.Fori(0, NG) as i:
                steps[0] = 0
                split_weights(i, 0)
                pool.wait_ge(s["var_made"], START + i * 2 + 1)
                G.tensor_tensor(rstd[:], var_e[:], expo[:], ALU.pow).then_inc(s["rstd_made"], 1)
                for j in range(NH * NR):
                    pool.wait_ge(s["max_kept"], START + i * 8 + j + 1)
                    if j >= 2:
                        pool.wait_ge(s["st_ready"], START + i * 8 + j - 1)
                    G.tensor_tensor(
                        shift[:, j % 2, :, :],
                        row_max[:, j // NR, j % NR, :, :].rearrange("p b c -> p (b c)").unsqueeze(2).to_broadcast([P, HB * CH, T]),
                        diag_ones[:, :].unsqueeze(1).to_broadcast([P, HB * CH, T]), ALU.mult).then_inc(s["shift_made"], 1)
                split_weights(i, 1)
                pool.wait_ge(s["var_made"], START + i * 2 + 2)
                G.tensor_tensor(rstd[:], var_e[:], expo[:], ALU.pow).then_inc(s["rstd_made"], 1)
                pool.wait_ge(s["hn_made"], START + i * 8 + 8)
                step(G.tensor_tensor(m_tm[:, :, :], hn[:, :, :], ln2_rows[:, 0, :].unsqueeze(1).to_broadcast([P, NT, D]), ALU.mult), i)
                G.tensor_tensor(m_tm[:, :, :], m_tm[:, :, :], ln2_rows[:, 1, :].unsqueeze(1).to_broadcast([P, NT, D]), ALU.add).then_inc(s["m_made"], 1)
                pool.wait_ge(s["m_made"], START + i + 1)
                pool.wait_ge(s["scattered"], 16 + i * (K * NT * 16))
                step(G.tensor_tensor(rows[:, :, 0:D], m_tm[:, :, :], scale_w[:, 1:2].unsqueeze(2).to_broadcast([P, NT, D]), ALU.add), i)
                G.tensor_tensor(rows[:, :, D:2 * D], m_tm[:, :, :], rows[:, :, 0:D], ALU.subtract).then_inc(s["rows_made"], 1)
                pool.wait_ge(s["rows_made"], START + i + 1)
                pool.wait_ge(s["pos_made"], START + i + 1)
                tick(i)
                for t in range(NT):
                    for k in range(K):
                        G.indirect_dma_start(out=xs[:, :], out_offset=bass.IndirectOffsetOnAxis(ap=pos_u[:, k, t:t + 1], axis=0),
                                             in_=rows[:, t, :].bitcast(I32), in_offset=None).then_inc(s["scattered"], 16)
                assert steps[0] == POOL_STEPS, steps[0]
            pool.wait_ge(s["tables_made"], START + 1)
            for e in range(E):
                G.indirect_dma_start(out=xs[:, :], out_offset=bass.IndirectOffsetOnAxis(ap=pad_pos[:, e:e + 1], axis=0),
                                     in_=pad_row[:, :].bitcast(I32), in_offset=None).then_inc(s["pads_out"], 16)
            with pool.Fori(0, NI) as i:
                for k in range(UNROLL):
                    j = i * UNROLL + k
                    pool.wait_ge(s["added"], 16 + j * 16)
                    pool.wait_ge(s["ye_kept"], START + j + 1)
                    tick(NG + j)
                    G.indirect_dma_start(out=out[:, :], out_offset=bass.IndirectOffsetOnAxis(ap=srows[:, k, ID_AT:ID_AT + 2].bitcast(U32), axis=0),
                                         in_=ys[:, k % 2, :], in_offset=None, compute_op=ALU.add).then_inc(s["added"], 16)

        @block.tensor
        def _(pe):
            def mm(o, l, r, first, last):
                return nc.tensor.matmul(o, l, r, start=first, stop=last, skip_group_check=True)

            def wait(name, v):
                pe.wait_ge(s[name], START + v)

            wait("weights_in", W_IN)
            wait("consts_made", CONSTS)
            wait("derived", 1)
            wait("mask_done", 6)
            with pe.Fori(0, NG) as i:
                wait("xt_in", i * 16 + 16)
                wait("y_kept", i * 2)
                for c in range(CH):
                    last = mm(bank[0][:, :], lora_a_s[:, c, :], xt[:, c, :], c == 0, c == CH - 1)
                last.then_inc(s["lora_ready"], 1)
                for o in range(CH):
                    if o == 0:
                        wait("mt_kept", i * 2)
                        wait("ranks_kept", i)
                    for c in range(CH):
                        mm(bank[1 + o][:, :], w_base_s[:, c, o * P:(o + 1) * P], xt[:, c, :], c == 0, False)
                wait("lora_kept", i + 1)
                for o in range(CH):
                    mm(bank[1 + o][:, :], lora_b_s[:, o * P:(o + 1) * P], lora_h[:, :], False, True).then_inc(s["y0_ready"], 1)
                wait("y0_kept", i * 2 + 2)
                wait("ctx_kept", i * 4)
                for c in range(CH):
                    last = mm(bank[3][0:DC, :], cs_w1_s[:, c, :], y0t[:, c, :], c == 0, c == CH - 1)
                last.then_inc(s["cs1_ready"], 1)
                wait("z2_kept", i * 2)
                for u in range(2):
                    for n in range(2):
                        t = 2 * u + n
                        for c in range(CH):
                            last = mm(bank[6 + u][:, n * D:(n + 1) * D], y0t[:, c, t * P:(t + 1) * P], wv_s[:, c, :], c == 0, c == CH - 1)
                    last.then_inc(s["v_ready"], 1)
                wait("cs1_kept", i + 1)
                wait("ctxt_kept", i * 2)
                for c in range(CH):
                    mm(bank[4 + c][:, :], cs_w2_s[:, c * P:(c + 1) * P], cs_h[0:DC, :], True, True).then_inc(s["cs2_ready"], 1)
                wait("y0_kept", i * 2 + 2)
                for o in range(CH):
                    if o == 0:
                        wait("lora_kept", i + 1)
                    for c in range(CH):
                        last = mm(bank[o][:, :], wk_s[:, c, o * P:(o + 1) * P], y0t[:, c, :], c == 0, c == CH - 1)
                    last.then_inc(s["k_ready"], 1)
                for o in range(CH):
                    if o == 1:
                        wait("cs1_kept", i + 1)
                    for c in range(CH):
                        last = mm(bank[2 + o][:, :], wq_s[:, c, o * P:(o + 1) * P], y0t[:, c, :], c == 0, c == CH - 1)
                    last.then_inc(s["q_ready"], 1)
                wait("lc_kept", i * 2 + 2)
                wait("v_kept", i * 2 + 2)
                wait("k_kept", i * 2 + 2)
                wait("q_kept", i * 2 + 2)
                for hb in range(NH):
                    for r in range(NR):
                        if hb:
                            wait("s_kept", i * 8 + r + 1)
                        rows = slice(32 * r, 32 * r + 32)
                        for b in range(HB):
                            for c in range(CH):
                                bb = hb * HB + b
                                last = mm(bank[4 + r][:, (b * CH + c) * T:(b * CH + c + 1) * T],
                                          k_pair[rows, c, bb, :, :].rearrange("p a t -> p (a t)"),
                                          q_all[rows, c, bb * T:(bb + 1) * T], True, True)
                        last.then_inc(s["s_ready"], 1)
                for hb in range(NH):
                    wait("s_kept", i * 8 + hb * 4 + 4)
                    for r in range(NR):
                        for c in range(CH):
                            for b in range(HB):
                                bb = hb * HB + b
                                vp = v_pair[:, bb, c * NR + r, 0:PV]
                                last = mm(bank[hb][32 * r:32 * r + 32, (c * HB + b) * T:(c * HB + b + 1) * T],
                                          vp, probs[:, hb, r, b, c, :], True, True)
                    last.then_inc(s["y_ready"], 1)
                wait("y_kept", i * 2 + 2)
                for o in range(CH):
                    for c in range(CH):
                        last = mm(bank[2 + o][:, :], wo_s[:, c, o * P:(o + 1) * P], yt[:, c, :], c == 0, c == CH - 1)
                    last.then_inc(s["o_ready"], 1)
                wait("x1t_kept", i * 2 + 2)
                wait("s_kept", i * 8 + 8)
                for u in range(2):
                    for n in range(2):
                        for c in range(CH):
                            t = 2 * u + n
                            last = nc.tensor.transpose(bank[4 + u][:, n * D + c * P:n * D + (c + 1) * P],
                                                       x1t[:, c, t * P:(t + 1) * P], ident[:, :])
                    last.then_inc(s["x1_ready"], 1)
                for g in range(E):
                    wait("xg_made", i * E + g + 1)
                    for t in range(NT):
                        for c in range(CH):
                            last = mm(bank[ZB[t]][:, 0:D], xg[:, g % 2, c, t * P:(t + 1) * P], c2_w_s[:, c, g, :],
                                      g == 0 and c == 0, g == E - 1 and c == CH - 1)
                        if g == E - 1:
                            last.then_inc(s["z_ready"], 1)
                        elif t == NT - 1:
                            last.then_inc(s["xg_used"], 1)
                for c in range(CH):
                    if c == 0:
                        wait("y_kept", i * 2 + 2)
                        wait("z_kept", i * 4 + 4)
                        wait("hn_made", i * 8 + 4)
                    for t in range(NT):
                        last = nc.tensor.transpose(bank[c][:, t * P:(t + 1) * P], hn[:, t, c * P:(c + 1) * P], ident[:, :])
                    last.then_inc(s["ht_ready"], 1)
                wait("ht_kept", i * 2 + 2)
                wait("x1_kept", i * 2 + 2)
                for o in range(CH):
                    for c in range(CH):
                        last = mm(bank[2 + o][:, :], fq_s[:, c, o * P:(o + 1) * P], y0t[:, c, :], c == 0, c == CH - 1)
                    last.then_inc(s["qb_ready"], 1)
                for o in range(CH):
                    for c in range(CH):
                        last = mm(bank[4 + o][:, :], fk_s[:, c, o * P:(o + 1) * P], y0t[:, c, :], c == 0, c == CH - 1)
                    last.then_inc(s["kb_ready"], 1)
                for u in range(2):
                    for n in range(2):
                        t = 2 * u + n
                        for c in range(CH):
                            last = mm(bank[6 + u][:, n * D:(n + 1) * D], y0t[:, c, t * P:(t + 1) * P], fv_s[:, c, :], c == 0, c == CH - 1)
                    last.then_inc(s["vb_ready"], 1)
                wait("kb_kept", i * 2 + 2)
                wait("qb_kept", i * 2 + 2)
                wait("vb_kept", i * 2 + 2)

                def by_query(j):
                    hb, r = j // NR, j % NR
                    rows = slice(32 * r, 32 * r + 32)
                    if j >= 4:
                        wait("max_kept", i * 8 + j - 3)
                    for b in range(HB):
                        for c in range(CH):
                            bb = hb * HB + b
                            last = mm(bank[j % 4][:, (b * CH + c) * T:(b * CH + c + 1) * T],
                                      q_pair[rows, c, bb, :, :].rearrange("p a t -> p (a t)"),
                                      k_all[rows, c, bb * T:(bb + 1) * T], True, True)
                    last.then_inc(s["smax_ready"], 1)

                def by_key(j):
                    hb, r = j // NR, j % NR
                    rows = slice(32 * r, 32 * r + 32)
                    wait("shift_made", i * 8 + j + 1)
                    if j >= 4:
                        wait("p_kept", i * 8 + j - 3)
                    mm(bank[4 + j % 4][:, :], same_head[:, :, :].rearrange("p a t -> p (a t)"),
                       shift[:, j % 2, :, :].rearrange("p n t -> p (n t)"), True, False)
                    for b in range(HB):
                        for c in range(CH):
                            bb = hb * HB + b
                            last = mm(bank[4 + j % 4][:, (b * CH + c) * T:(b * CH + c + 1) * T],
                                      k_pair[rows, c, bb, :, :].rearrange("p a t -> p (a t)"),
                                      q_all[rows, c, bb * T:(bb + 1) * T], False, True)
                    last.then_inc(s["st_ready"], 1)

                for j in range(NH * NR + 2):
                    if j < NH * NR:
                        by_query(j)
                    if j >= 2:
                        by_key(j - 2)
                wait("max_kept", i * 8 + 8)
                for t in range(NT):
                    wait("p_kept", i * 8 + (t * 2 // HB) * 4 + 4)
                    for n in range(2):
                        bb = 2 * t + n
                        for c in range(CH):
                            for r in range(NR):
                                pr = c * NR + r
                                last = mm(bank[t][n * T:(n + 1) * T, pr * PW:(pr + 1) * PW],
                                          probs[:, bb // HB, r, bb % HB, c, :], v_pair[:, bb, pr, :], True, True)
                    last.then_inc(s["pv_ready"], 1)
                for c in range(CH):
                    if c == 0:
                        wait("p_kept", i * 8 + 8)
                        wait("ctx_kept", i * 4 + 4)
                    for t in range(NT):
                        last = nc.tensor.transpose(bank[4 + c][:, t * P:(t + 1) * P], ctxn[:, t, c * P:(c + 1) * P], ident[:, :])
                    last.then_inc(s["ctxt_ready"], 1)
                wait("ctxt_kept", i * 2 + 2)
                for u in range(2):
                    for n in range(2):
                        t = 2 * u + n
                        for c in range(CH):
                            last = mm(bank[6 + u][:, n * D:(n + 1) * D], yt[:, c, t * P:(t + 1) * P], fo_s[:, c, :], c == 0, c == CH - 1)
                    last.then_inc(s["wo_ready"], 1)
                wait("m_made", i + 1)
                for c in range(CH):
                    for t in range(NT):
                        last = nc.tensor.transpose(bank[c][:, t * P:(t + 1) * P], m_tm[:, t, c * P:(c + 1) * P], ident[:, :])
                    last.then_inc(s["mt_ready"], 1)
                wait("mt_kept", i * 2 + 2)
                for t in range(NT):
                    for c in range(CH):
                        last = mm(bank[2][:, t * E:(t + 1) * E], y0t[:, c, t * P:(t + 1) * P], fg_s[:, c, :], c == 0, c == CH - 1)
                last.then_inc(s["gate_ready"], 1)

                wait("lg_made", i + 1)
                pk = picked[:, :, :].rearrange("p t e -> p (t e)")
                mm(bank[2][:, 0:NT * E], lower[:, :], pk, True, True)
                mm(bank[2][:, NT * E:2 * NT * E], ones[:, :], pk, True, True).then_inc(s["ranks_ready"], 1)

            wait("ranks_kept", NG)
            wait("mt_kept", NG * 2)
            wait("tables_made", 3)

            def transposes(i, k):
                wait(f"srows_in{k % UNROLL}", (i + k // UNROLL) * 16 + 16)
                for q in range(2 * CH):
                    last = nc.tensor.transpose(tbank[k % 2][:, q * P:(q + 1) * P], srows[:, k % UNROLL, q * P:(q + 1) * P], id_h[:, :])
                last.then_inc(s["t_ready"], 1)

            def up(i, k, e, first):
                j = i * UNROLL + k
                x = sxt[:, k % 2, :, :]
                wait("xt_kept", j + 1)
                for hf in range(2):
                    if not (first and k < 2):
                        wait("h_kept", i * (2 * UNROLL) + (2 * k + hf - 3))
                    for f in range(4):
                        o = bank[2 * (k % 2) + hf][:, f * P:(f + 1) * P]
                        at = (hf * 4 + f) * P
                        n = 0
                        for c in range(CH):
                            for ws, xsi in ((0, 0), (0, 1), (1, 0)):
                                w = w_all[:, bass.ds(e, 1), ws, c * F + at:c * F + at + P].rearrange("p o w -> p (o w)")
                                last = mm(o, w, x[:, xsi * CH + c, :], n == 0, n == 5)
                                n += 1
                    last.then_inc(s["h_ready"], 1)

            def down(i, k, e):
                j = i * UNROLL + k
                wait("hid_split", j * 2 + 2)
                o = bank[4 + k % 2][:, 0:D]
                for sp_ in range(2):
                    mm(o, ones_h[:, :], b2_s[:, sp_, bass.ds(e, 1), :].rearrange("p o w -> p (o w)"), sp_ == 0, False)
                for f in range(FC):
                    for ws, hs in ((0, 0), (0, 1), (1, 0)):
                        w = w_all[:, bass.ds(e, 1), ws, W2_AT + f * D:W2_AT + (f + 1) * D].rearrange("p o w -> p (o w)")
                        last = mm(o, hid_s[:, k % 2, hs, f, :], w, False, f == FC - 1)
                last.then_inc(s["ye_ready"], 1)

            def expert(i, k):
                j = i * UNROLL + k
                return pe.value_load(tile_e_i[0:1, bass.ds(j, 1)], min_val=0, max_val=E - 1)

            def body(i, first):
                for k in range(UNROLL):
                    up(i, k, expert(i, k), first)
                    transposes(i, k + 1)
                    if not (first and k == 0):
                        down(i, k - 1, expert(i, k - 1))

            for e in range(E):
                wait(f"w_in{e}", 16)
            transposes(0, 0)
            body(0, True)
            with pe.Fori(1, NI) as i:
                body(i, False)
            down(NI - 1, UNROLL - 1, expert(NI - 1, UNROLL - 1))

        @block.scalar
        def _(act):
            def wait(name, v):
                act.wait_ge(s[name], START + v)

            A = nc.scalar.activation
            wait("weights_in", W_IN)
            A(base_t[:, :], decay_s[:, :], ACT.Tanh, scale=0.5).then_inc(s["derived"], 1)
            wait("consts_made", CONSTS)
            wait("mask_done", 6)
            with act.Fori(0, NG) as i:
                wait("gate_ready", i)
                for o in range(CH):
                    wait("y0_ready", i * 2 + o + 1)
                    A(y0t[:, o, :], bank[1 + o][:, :], ACT.Identity, bias=b_base_s[:, o:o + 1]).then_inc(s["y0_kept"], 1)
                wait("cs1_ready", i + 1)
                A(cs_h[0:DC, :], bank[3][0:DC, :], ACT.Tanh, bias=cs_b1_s[:, :]).then_inc(s["cs1_kept"], 1)

                def keep_values(bk, ready, kept):
                    for u in range(2):
                        wait(ready, i * 2 + u + 1)
                        for n in range(2):
                            for par in range(2):
                                src = bk[u][n * T:(n + 1) * T, :].rearrange("p (t q a f) -> p t q a f", t=2, q=CH * NR, a=2)[:, :, :, par, :]
                                dst = v_pair[par * T:(par + 1) * T, 4 * u + n:4 * u + n + 3:2, :, par * DH:par * DH + DH]
                                last = nc.scalar.copy(dst, src)
                        last.then_inc(s[kept], 1)

                wait("pv_ready", i * 4)
                keep_values([bank[6], bank[7]], "v_ready", "v_kept")
                for c in range(CH):
                    wait("cs2_ready", i * 2 + c + 1)
                    if c == 0:
                        wait("mt_ready", i * 2)
                    A(lc[:, c, :], bank[4 + c][:, :], ACT.Tanh, scale=0.5, bias=half_b2[:, c:c + 1]).then_inc(s["lc_kept"], 1)
                for u in range(NH):
                    wait("y_ready", i * 2 + u + 1)
                    if u == 0:
                        wait("wo_ready", i * 2)
                    nc.scalar.copy(yt[:, :, u * HB * T:(u + 1) * HB * T], bank[u][:, :].rearrange("p (c t) -> p c t", c=CH)).then_inc(s["y_kept"], 1)
                wait("acc_out", i * 16)
                for u in range(2):
                    wait("x1_ready", i * 2 + u + 1)
                    nc.scalar.copy(acc[:, 2 * u:2 * u + 2, :], bank[4 + u][:, :].rearrange("p (t d) -> p t d", t=2)).then_inc(s["x1_kept"], 1)
                for c in range(CH):
                    wait("ht_ready", i * 2 + c + 1)
                    A(y0t[:, c, :], bank[c][:, :], ACT.Identity, scale=lng[:, 0, c:c + 1], bias=lng[:, 1, c:c + 1]).then_inc(s["ht_kept"], 1)
                for c in range(CH):
                    wait("qb_ready", i * 2 + c + 1)
                    nc.scalar.copy(q_all[:, c, :], bank[2 + c][:, :])
                    for par in range(2):
                        last = A(q_pair[:, c, :, par, :], bank[2 + c][:, :].rearrange("p (b t) -> p b t", t=T), ACT.Identity, scale=par_mask[:, par:par + 1])
                    last.then_inc(s["qb_kept"], 1)
                keep_values([bank[6], bank[7]], "vb_ready", "vb_kept")
                for j in range(NH * NR):
                    wait("st_ready", i * 8 + j + 1)
                    A(probs[:, j // NR, j % NR, :, :, :].rearrange("p b c t -> p (b c t)"), bank[4 + j % 4][:, :], ACT.Exp,
                      scale=float(DH) ** -0.5).then_inc(s["p_kept"], 1)
                for c in range(CH):
                    wait("ctxt_ready", i * 2 + c + 1)
                    nc.scalar.copy(yt[:, c, :], bank[4 + c][:, :]).then_inc(s["ctxt_kept"], 1)
                for c in range(CH):
                    wait("mt_ready", i * 2 + c + 1)
                    nc.scalar.copy(y0t[:, c, :], bank[c][:, :]).then_inc(s["mt_kept"], 1)
                wait("lg_made", i + 1)
                A(ex[:, :, :], lg[:, :, :], ACT.Exp).then_inc(s["ex_made"], 1)
            wait("tables_made", 3)
            wait("split_made", NG * 2)
            def hidden(i, first):
                for k in range(UNROLL):
                    e = act.value_load(tile_e_i[0:1, bass.ds(i * UNROLL + k, 1)], min_val=0, max_val=E - 1)
                    for hf in range(2):
                        wait("h_ready", i * (2 * UNROLL) + 2 * k + hf + 1)
                        if not (first and k < 2):
                            wait("hid_split", i * (2 * UNROLL) + (2 * k + hf - 3))
                        for f in range(4):
                            last = A(hid[:, k % 2, hf * 4 + f, :], bank[2 * (k % 2) + hf][:, f * P:(f + 1) * P], ACT.Gelu_apprx_tanh,
                                     scale=1.0 / W_SCALE, bias=b1_all[:, bass.ds(e, 1), hf * 4 + f])
                        last.then_inc(s["h_kept"], 1)

            hidden(0, True)
            with act.Fori(1, NI) as i:
                hidden(i, False)

        STEPS = 37

        @block.vector
        def _(dve):
            V = nc.vector
            steps = [0, 0]

            def wait(name, v):
                dve.wait_ge(s[name], (16 if name in software else START) + v)

            def step(ins, i=None):
                steps[0] += 1
                ins.then_inc(s["dve_steps"], 1)
                dve.wait_ge(s["dve_steps"], START + steps[0] if i is None else i * STEPS + (START + steps[1] + steps[0]))

            def tick():
                V.tensor_copy(tick_s[:, 0:1], tick_s[:, 1:2])

            V.memset(tick_s[:, :], 0.0)
            wait("consts_made", CONSTS)
            wait("weights_in", W_IN)
            V.memset(region0[:, :], 0.0)
            V.memset(pool_tick[:, :], 0.0)
            V.memset(before[:, 0, :], 0.0)
            V.memset(ones8[:, :], 1.0)
            V.memset(scale_w[:, 0:1], W_SCALE)
            V.memset(scale_w[:, 1:2], 0.0)
            V.tensor_copy(pid[:, :], pid_u[:, :])
            V.tensor_copy(id_h[:, :], ident[:, :])
            V.tensor_copy(tile_j[:, :], tile_ku[:, :])
            step(V.tensor_copy(iota8[:, :], iota8u[:, :]))
            V.tensor_scalar(alone_pos[:, :], pid[:, :], float(E * REGION), None, ALU.add)
            V.tensor_scalar(tile_k[:, :], tile_j[:, 0:NTOK // P + 1], float(P), None, ALU.mult)
            step(V.tensor_scalar(region0[:, :], iota8[:, :], float(REGION), None, ALU.mult))
            step(V.tensor_scalar(tok_g[:, :], tile_j[:, 0:NT], float(P), None, ALU.mult))
            step(V.tensor_scalar(tok_g[:, :], tok_g[:, :], pid[:, 0:1], None, ALU.add))
            step(V.tensor_scalar(b2_f[:, :, :], b2_f[:, :, :], W_SCALE, None, ALU.mult))
            step(V.tensor_copy(b2_s[:, 0, :, :], b2_f[:, :, :]))
            step(V.tensor_tensor(b2_s[:, 1, :, :], b2_f[:, :, :], b2_s[:, 0, :, :], ALU.subtract))
            for half in range(2):
                rows_ = slice(half * T, half * T + T)
                V.memset(same_head[rows_, 1 - half, :], 0.0)
                V.memset(v_pair[rows_, :, :, PV + half:PV + half + 1], 1.0)
                V.tensor_copy(diag_ones[rows_, :], ident[rows_, rows_]).then_inc(s["mask_done"], 1)
            V.tensor_reduce(par_mask[:, 0:1], ident[:, :].rearrange("p (q a f) -> p q a f", a=2, f=DH)[:, :, 0, :], mybir.AxisListType.XY, ALU.add).then_inc(s["mask_done"], 1)
            V.tensor_reduce(par_mask[:, 1:2], ident[:, :].rearrange("p (q a f) -> p q a f", a=2, f=DH)[:, :, 1, :], mybir.AxisListType.XY, ALU.add).then_inc(s["mask_done"], 1)
            V.tensor_scalar(half_b2[:], cs_b2_s[:], 0.5, None, ALU.mult).then_inc(s["mask_done"], 1)
            step(V.tensor_tensor(c2_w_s[:, :, :, :], c2_w_s[:, :, :, :],
                                 c2_mask_s[:, :, :].unsqueeze(2).to_broadcast([P, CH, E, D]), ALU.mult))
            wait("derived", 1)
            step(V.tensor_scalar(base_t[:, :], base_t[:, :], 0.5, 0.5, ALU.mult, ALU.add))
            V.tensor_scalar(base_11[:, :], base_t[:, :], 1.1, None, ALU.mult)
            V.tensor_scalar(base_01[:, :], base_t[:, :], 0.1, None, ALU.mult).then_inc(s["mask_done"], 1)
            wait("mask_done", 6)
            steps[1] = steps[0]

            with dve.Fori(0, NG) as i:
                steps[0] = 0
                wait("lora_ready", i + 1)
                V.scalar_tensor_tensor(out=lora_h[:, :].rearrange("p (b t) -> p b t", t=T), in0=bank[0][:, :].rearrange("p (b t) -> p b t", t=T),
                                       scalar=LORA_SCALE, in1=cond_er[:, bass.ds(i * GB, GB)].unsqueeze(2).to_broadcast([P, GB, T]),
                                       op0=ALU.mult, op1=ALU.mult).then_inc(s["lora_kept"], 1)
                wait("z_ready", i * 4)
                for c in range(CH):
                    wait("lc_kept", i * 2 + c + 1)
                    ins = V.tensor_scalar(lam[:, c * GT:(c + 1) * GT], lc[:, c, :], base_01[:, c:c + 1], base_11[:, c:c + 1], ALU.mult, ALU.add)
                step(ins, i)
                step(V.tensor_scalar(lam[:, :], lam[:, :], LAM_MAX, 0.0, ALU.min, ALU.max), i)
                starts = lam[:, 0:CH * GT:HALF]
                step(V.tensor_copy(lam_first[:, 0:CH * GT:HALF], starts), i)
                step(V.memset(starts, 0.0), i)
                step(V.tensor_tensor_scan(cum[:, :], lam[:, :], lam_first[:, :], 0.0, ALU.mult, ALU.add), i)
                step(V.reciprocal(cum_mid[:, :], cum[:, HALF - 1:CH * GT:T]), i)
                first_half = cum[:, :].rearrange("p (n t) -> p n t", t=T)[:, :, 0:HALF]
                step(V.tensor_tensor(first_half, first_half, cum_mid[:, :].unsqueeze(2).to_broadcast([P, CH * GB, HALF]), ALU.mult), i)
                step(V.reciprocal(cum_inv[:, :], cum[:, :]), i)
                wait("st_ready", i * 8)
                for c in range(CH):
                    wait("k_ready", i * 2 + c + 1)
                    for par in range(2):
                        ins = V.scalar_tensor_tensor(out=k_pair[:, c, :, par, :], in0=bank[c][:, :].rearrange("p (b t) -> p b t", t=T),
                                                     scalar=par_mask[:, par:par + 1],
                                                     in1=cum_inv[:, c * GT:(c + 1) * GT].rearrange("p (b t) -> p b t", t=T),
                                                     op0=ALU.mult, op1=ALU.mult)
                    ins.then_inc(s["k_kept"], 1)
                for c in range(CH):
                    wait("q_ready", i * 2 + c + 1)
                    V.tensor_tensor(q_all[:, c, :], bank[2 + c][:, :], cum[:, c * GT:(c + 1) * GT], ALU.mult).then_inc(s["q_kept"], 1)
                wait("pv_ready", i * 4)
                for j in range(NH * NR):
                    wait("s_ready", i * 8 + j + 1)
                    V.tensor_tensor(probs[:, j // NR, j % NR, :, :, :].rearrange("p b c t -> p (b c) t"),
                                    bank[4 + j % NR][:, :].rearrange("p (n t) -> p n t", t=T),
                                    causal[:, :].unsqueeze(1).to_broadcast([P, HB * CH, T]), ALU.mult).then_inc(s["s_kept"], 1)
                for o in range(CH):
                    wait("o_ready", i * 2 + o + 1)
                    V.tensor_tensor(x1t[:, o, :], bank[2 + o][:, :], xt[:, o, :], ALU.add).then_inc(s["x1t_kept"], 1)
                wait("x1t_kept", i * 2 + 2)
                for g in range(E):
                    if g >= 2:
                        wait("xg_used", i * 7 + g - 1)
                    else:
                        wait("z_ready", i * 4)
                    for c in range(CH):
                        ins = V.tensor_tensor(xg[:, g % 2, c, :].rearrange("p (b t) -> p b t", t=T),
                                              x1t[:, c, :].rearrange("p (b t) -> p b t", t=T),
                                              cond_all[:, g, bass.ds(i * GB, GB)].unsqueeze(2).to_broadcast([P, GB, T]), ALU.mult)
                    ins.then_inc(s["xg_made"], 1)

                def norm(k):
                    for t in range(NT):
                        ins = V.bn_stats(stats[:, t, :], z[:, t, :])
                    step(ins, i)
                    tick()
                    for t in range(NT):
                        ins = V.bn_aggr(mv[:, t, :], stats[:, t, :])
                    step(ins, i)
                    V.tensor_scalar(var_e[:, :], mv[:, :, 1], EPS, None, ALU.add).then_inc(s["var_made"], 1)
                    wait("rstd_made", i * 2 + k + 1)
                    for t in range(NT):
                        V.tensor_scalar(hn[:, t, :], z[:, t, :], mv[:, t, 0:1], rstd[:, t:t + 1], ALU.subtract, ALU.mult).then_inc(s["hn_made"], 1)

                for t in range(NT):
                    wait("z_ready", i * 4 + t + 1)
                    ins = V.tensor_tensor(z[:, t, :], bank[ZB[t]][:, 0:D], c2_bias_s[:, :], ALU.add)
                    ins.then_inc(s["z_kept"], 1)
                wait("z_kept", i * 4 + 4)
                norm(0)
                for c in range(CH):
                    wait("kb_ready", i * 2 + c + 1)
                    V.tensor_copy(k_all[:, c, :], bank[4 + c][:, :])
                    for par in range(2):
                        ins = V.tensor_scalar(k_pair[:, c, :, par, :], bank[4 + c][:, :].rearrange("p (b t) -> p b t", t=T),
                                              par_mask[:, par:par + 1], None, ALU.mult)
                    ins.then_inc(s["kb_kept"], 1)
                for j in range(NH * NR):
                    wait("smax_ready", i * 8 + j + 1)
                    V.tensor_reduce(row_max[:, j // NR, j % NR, :, :].rearrange("p b c -> p (b c)"),
                                    bank[j % 4][:, :].rearrange("p (n t) -> p n t", t=T), AX_X, ALU.max,
                                    negate=True).then_inc(s["max_kept"], 1)
                for t in range(NT):
                    wait("pv_ready", i * 4 + t + 1)
                    pv = bank[t][:, 0:CH * NR * PW].rearrange("p (h f) -> p h f", f=PW)
                    step(V.reciprocal(sum_inv[:, t, :, :], pv[:, :, PV:PW]), i)
                    V.tensor_tensor(ctxn[:, t, :].rearrange("p (h a f) -> p h a f", a=2, f=DH),
                                    pv[:, :, 0:PV].rearrange("p h (a f) -> p h a f", a=2),
                                    sum_inv[:, t, :, :].unsqueeze(3).to_broadcast([P, CH * NR, 2, DH]), ALU.mult).then_inc(s["ctx_kept"], 1)
                for u in range(2):
                    wait("wo_ready", i * 2 + u + 1)
                    V.tensor_tensor(z[:, 2 * u:2 * u + 2, :], bank[6 + u][:, :].rearrange("p (t d) -> p t d", t=2),
                                    z[:, 2 * u:2 * u + 2, :], ALU.add).then_inc(s["z2_kept"], 1)
                wait("z2_kept", i * 2 + 2)
                wait("ht_ready", i * 2 + 2)
                norm(1)
                wait("x1_kept", i * 2 + 2)
                V.tensor_tensor(acc[:, :, :], acc[:, :, :], z[:, :, :], ALU.add).then_inc(s["acc_made"], 1)
                wait("gate_ready", i + 1)
                logits = bank[2][:, 0:NT * E].rearrange("p (t e) -> p t e", e=E)
                step(V.tensor_copy(lg[:, :, :], logits), i)
                tick()
                for t in range(NT):
                    ins = V.max(top[:, t, :], lg[:, t, :])
                step(ins, i)
                tick()
                for t in range(NT):
                    ins = V.max_index(top_i[:, t, :], top[:, t, :], lg[:, t, :])
                step(ins, i)
                V.tensor_copy(top_f[:, :, :], top_i[:, :, :])
                step(V.tensor_tensor(lg[:, :, :], lg[:, :, :], top[:, :, 0:1].to_broadcast([P, NT, E]), ALU.subtract), i)
                for j in range(2):
                    ins = V.tensor_tensor(pick[:, :, j, :], iota8[:, :].unsqueeze(1).to_broadcast([P, NT, E]),
                                          top_f[:, :, j:j + 1].to_broadcast([P, NT, E]), ALU.is_equal)
                step(ins, i)
                V.tensor_tensor(picked[:, :, :], pick[:, :, 0, :], pick[:, :, 1, :], ALU.add).then_inc(s["lg_made"], 1)
                wait("lg_made", i + 1)
                wait("ex_made", i + 1)
                step(V.tensor_reduce(ex_sum[:, :], ex[:, :, :], AX_X, ALU.add), i)
                step(V.reciprocal(ex_sum[:, :], ex_sum[:, :]), i)
                step(V.tensor_tensor(ex[:, :, :], ex[:, :, :], ex_sum[:, :].unsqueeze(2).to_broadcast([P, NT, E]), ALU.mult), i)
                step(V.tensor_tensor(ex[:, :, :], ex[:, :, :], picked[:, :, :], ALU.mult), i)
                step(V.tensor_reduce(two_sum[:, :], ex[:, :, :], AX_X, ALU.add), i)
                step(V.reciprocal(two_sum[:, :], two_sum[:, :]), i)
                wait("scattered", i * (K * NT * 16))
                V.tensor_tensor(rows[:, :, G_AT:ID_AT].bitcast(F32), ex[:, :, :], two_sum[:, :].unsqueeze(2).to_broadcast([P, NT, E]), ALU.mult)
                V.tensor_copy(rows[:, :, ID_AT:ID_AT + 2].bitcast(I32).rearrange("p t o -> p (t o)"), tok_g[:, :])
                wait("ranks_ready", i + 1)
                V.tensor_copy(rank[:, :, :], bank[2][:, 0:NT * E].rearrange("p (t e) -> p t e", e=E))
                step(V.tensor_copy(tot[:, :, :], bank[2][:, NT * E:2 * NT * E].rearrange("p (t e) -> p t e", e=E)), i)
                for t in range(NT):
                    step(V.tensor_tensor(before[:, t + 1, :], before[:, t, :], tot[:, t, :], ALU.add), i)
                step(V.tensor_tensor(rank[:, :, :], rank[:, :, :], before[:, 0:NT, :], ALU.add), i)
                step(V.tensor_tensor(rank[:, :, :], rank[:, :, :], region0[:, :].unsqueeze(1).to_broadcast([P, NT, E]), ALU.add), i)
                for k in range(K):
                    ins = V.tensor_tensor(slot[:, k, :, :], pick[:, :, k, :], rank[:, :, :], ALU.mult)
                step(ins, i)
                step(V.tensor_reduce(pos_f[:, :, :], slot[:, :, :, :], AX_X, ALU.add), i)
                V.tensor_copy(pos_u[:, :, :], pos_f[:, :, :]).then_inc(s["pos_made"], 1)
                step(V.tensor_scalar(tok_g[:, :], tok_g[:, :], float(GT), None, ALU.add), i)
                V.tensor_copy(before[:, 0, :], before[:, NT, :]).then_inc(s["ranks_kept"], 1)
                wait("ranks_kept", i + 1)
                assert steps[0] == STEPS, steps[0]
            steps[1] += NG * STEPS
            steps[0] = 0

            def link(ins):
                steps[0] += 1
                ins.then_inc(s["dve_steps"], 1)
                dve.wait_ge(s["dve_steps"], START + steps[1] + steps[0])

            count = before[:, 0, :]
            link(V.tensor_tensor(pad_pos_f[:, :], count, region0[:, :], ALU.add))
            link(V.tensor_scalar(pad_pos_f[:, :], pad_pos_f[:, :], pid[:, 0:1], None, ALU.add))
            V.tensor_copy(pad_pos[:, :], pad_pos_f[:, :]).then_inc(s["tables_made"], 1)
            link(V.tensor_tensor(cmp_k[:, :, :], count.unsqueeze(2).to_broadcast([P, E, NTOK // P + 1]),
                                 tile_k[:, :].unsqueeze(1).to_broadcast([P, E, NTOK // P + 1]), ALU.is_gt))
            link(V.tensor_reduce(n_tiles[:, :], cmp_k[:, :, :], AX_X, ALU.add))
            link(V.tensor_tensor_scan(tiles_to[:, :], ones8[:, :], n_tiles[:, :], 0.0, ALU.mult, ALU.add))
            bc_e = [P, NJT, E]
            link(V.tensor_tensor(past[:, :, :], tiles_to[:, :].unsqueeze(1).to_broadcast(bc_e),
                                 tile_j[:, :].unsqueeze(2).to_broadcast(bc_e), ALU.is_le))
            link(V.tensor_tensor(past_n[:, :, :], past[:, :, :], n_tiles[:, :].unsqueeze(1).to_broadcast(bc_e), ALU.mult))
            V.tensor_reduce(tile_e[:, :], past[:, :, :], AX_X, ALU.add)
            link(V.tensor_reduce(tile_first[:, :], past_n[:, :, :], AX_X, ALU.add))
            link(V.tensor_tensor(tile_row[:, :], tile_j[:, :], tile_first[:, :], ALU.subtract))
            link(V.tensor_scalar(tile_row[:, :], tile_row[:, :], float(P), None, ALU.mult))
            link(V.scalar_tensor_tensor(out=tile_row[:, :], in0=tile_e[:, :], scalar=float(REGION), in1=tile_row[:, :],
                                        op0=ALU.mult, op1=ALU.add))
            link(V.tensor_scalar(tile_row[:, :], tile_row[:, :], float(E * REGION), None, ALU.min))
            link(V.tensor_scalar(tile_e[:, :], tile_e[:, :], float(E - 1), None, ALU.min))
            V.tensor_copy(tile_row_i[:, :], tile_row[:, :]).then_inc(s["tables_made"], 1)
            V.tensor_copy(tile_e_i[:, :], tile_e[:, :]).then_inc(s["tables_made"], 1)
            wait("tables_made", 3)

            def keep_xt(i, k):
                j = i * UNROLL + k
                wait("t_ready", j + 1)
                if not (isinstance(i, int) and j < 2):
                    wait("h_ready", 2 * j - 2)
                V.tensor_copy(sxt[:, k % 2, :, :], tbank[k % 2][:, :].rearrange("p (q t) -> p q t", t=P)).then_inc(s["xt_kept"], 1)

            def split_hidden(i, k, hf, first):
                j = i * UNROLL + k
                fs = slice(hf * 4, hf * 4 + 4)
                wait("h_kept", 2 * j + hf + 1)
                if not (first and k < 2):
                    wait("ye_ready", j - 1)
                V.tensor_copy(hid_s[:, k % 2, 0, fs, :], hid[:, k % 2, fs, :]).then_inc(s["hi_made"], 1)
                wait("hi_made", 2 * j + hf + 1)
                V.tensor_tensor(hid_s[:, k % 2, 1, fs, :], hid[:, k % 2, fs, :], hid_s[:, k % 2, 0, fs, :], ALU.subtract).then_inc(s["hid_split"], 1)

            def keep_y(i, k, e, first):
                j = i * UNROLL + k
                wait("ye_ready", j + 1)
                if not (first and k < 2):
                    wait("added", (j - 1) * 16)
                gate = srows[:, k % UNROLL, G_AT:ID_AT].bitcast(F32)[:, bass.ds(e, 1)]
                V.tensor_scalar(ys[:, k % 2, :], bank[4 + k % 2][:, 0:D], gate, 1.0 / W_SCALE, ALU.mult, ALU.mult).then_inc(s["ye_kept"], 1)

            def expert(i, k):
                return dve.value_load(tile_e_i[0:1, bass.ds(i * UNROLL + k, 1)], min_val=0, max_val=E - 1)

            def body(i, first):
                for k in range(UNROLL):
                    split_hidden(i, k, 0, first)
                    keep_xt(i, k + 1)
                    split_hidden(i, k, 1, first)
                    if not (first and k == 0):
                        keep_y(i, k - 1, expert(i, k - 1), first)

            wait("split_out", NG * 32)
            keep_xt(0, 0)
            body(0, True)
            with dve.Fori(1, NI) as i:
                body(i, False)
            keep_y(NI - 1, UNROLL - 1, expert(NI - 1, UNROLL - 1), False)


ZB = [6, 7, 2, 3]


def kernel(x, cond_8, L0_cond_W_base, L0_cond_b_base, L0_cond_As, L0_cond_Bs, L0_attn_q_w, L0_attn_k_w, L0_attn_v_w,
           L0_attn_o_w, L0_attn_cs_w1, L0_attn_cs_b1, L0_attn_cs_w2, L0_attn_cs_b2, L0_attn_decay_params,
           L0_cond2_weight, L0_cond2_mask, L0_cond2_bias, L0_ffn_ln1_g, L0_ffn_ln1_b, L0_ffn_ln2_g, L0_ffn_ln2_b,
           L0_ffn_Wq, L0_ffn_Wk, L0_ffn_Wv, L0_ffn_Wo, L0_ffn_Wg, L0_ffn_W1, L0_ffn_b1, L0_ffn_W2, L0_ffn_b2):
    import numpy as np
    import concourse.bacc as bacc
    from concourse.bass_utils import run_bass_kernel_spmd

    def rows(a):
        return np.asarray(a).reshape(-1, P, a.shape[-1]).transpose(1, 0, 2)

    def cols(a):
        return np.asarray(a).reshape(-1, P).T

    t = np.transpose
    arrays = {
        "x_t": rows(t(np.asarray(x).reshape(B * T, D))),
        "cond_t": t(np.asarray(cond_8)),
        "w_base": rows(t(L0_cond_W_base)),
        "b_base": cols(L0_cond_b_base),
        "lora_a": rows(t(np.asarray(L0_cond_As).reshape(E * R, D))),
        "lora_b": t(L0_cond_Bs, (0, 2, 1)).reshape(E * R, D),
        "wq": rows(t(L0_attn_q_w)), "wk": rows(t(L0_attn_k_w)), "wv": rows(t(L0_attn_v_w)), "wo": rows(t(L0_attn_o_w)),
        "cs_w1": rows(t(L0_attn_cs_w1)),
        "cs_b1": np.asarray(L0_attn_cs_b1).reshape(DC, 1),
        "cs_w2": np.repeat(t(L0_attn_cs_w2), DH, axis=1),
        "cs_b2": cols(np.repeat(L0_attn_cs_b2, DH)),
        "decay": cols(np.asarray(L0_attn_decay_params).reshape(D)),
        "c2_w": t(np.asarray(L0_cond2_weight).reshape(E, D, CH, P), (3, 2, 0, 1)),
        "c2_mask": rows(t(L0_cond2_mask)),
        "c2_bias": np.asarray(L0_cond2_bias),
        "ln1_g": cols(L0_ffn_ln1_g), "ln1_b": cols(L0_ffn_ln1_b),
        "ln2_g": np.asarray(L0_ffn_ln2_g), "ln2_b": np.asarray(L0_ffn_ln2_b),
        "fq": rows(L0_ffn_Wq), "fk": rows(L0_ffn_Wk), "fv": rows(L0_ffn_Wv), "fo": rows(L0_ffn_Wo), "fg": rows(L0_ffn_Wg),
        "fw": np.stack([t(np.asarray(L0_ffn_W1).reshape(E, CH, P, F), (2, 0, 1, 3)).reshape(P, E, CH * F),
                        t(np.asarray(L0_ffn_W2).reshape(E, FC, P, D), (2, 0, 1, 3)).reshape(P, E, FC * D)], axis=2),
        "fb1": t(np.asarray(L0_ffn_b1).reshape(E, FC, P), (2, 0, 1)),
        "fb2": np.asarray(L0_ffn_b2).reshape(1, E, D),
        "ident_in": np.eye(P, dtype=np.float32),
        "pad_ids": np.arange(NTOK, NTOK + P, dtype=np.int32).reshape(P, 1),
    }
    arrays = {n: np.ascontiguousarray(a) for n, a in arrays.items()}
    nc = bacc.Bacc("TRN2", target_bir_lowering=False, num_devices=1)
    args = [nc.dram_tensor(n, a.shape, mybir.dt.from_np(a.dtype), kind="ExternalInput").ap() for n, a in arrays.items()]
    order = ("x_t cond_t w_base b_base lora_a lora_b wq wk wv wo cs_w1 cs_b1 cs_w2 cs_b2 decay c2_w c2_mask c2_bias "
             "ln1_g ln1_b ln2_g ln2_b fq fk fv fo fg fw fb1 fb2 ident_in pad_ids").split()
    assert order == list(arrays)
    out = nc.dram_tensor("out", (NTOK + P, D), F32, kind="ExternalOutput").ap()
    bass_adaln_attn_ffn(nc, *args, out)
    got = run_bass_kernel_spmd(nc, [arrays], core_ids=[0])
    return got.results[0]["out"][:NTOK].reshape(B, T, D)
```

```python
import concourse.bass as bass
from concourse import mybir
from contextlib import ExitStack


F32 = mybir.dt.float32
F16 = mybir.dt.float16
BF16 = mybir.dt.bfloat16
U32 = mybir.dt.uint32
I32 = mybir.dt.int32
ALU = mybir.AluOpType
ACT = mybir.ActivationFunctionType
AX_X = mybir.AxisListType.X

P = 128
B, T, D = 64, 64, 256
H, DH = 16, 16
E, R = 8, 16
F = 1024
CH = D // P
FC = F // P
GB = 4
GT = GB * T
NG = B // GB
NT = GT // P
NR = 4
NTOK = B * T
K = 2
ST = 2
TB = ST * P
REGION = NTOK + TB
NROWS = E * REGION + TB
NJ = NTOK * K // TB + E - 1
UNROLL = 4
NI = NJ // UNROLL
REST = NJ - NI * UNROLL
NK = NTOK // TB + 1
HC = 4
G_AT = 2 * D
ID_AT = G_AT + 2 * E
ROW = ID_AT + 2
WE = 2 * D * F // P
W2_AT = WE // 2
W_SCALE = 256.0
DC = 64
LORA_SCALE = 32.0 / R
LAM_MAX = 0.9995
EPS = 1e-05
PV = 2 * DH
PW = PV + 2


def bass_adaln_attn_ffn(nc, x_t, cond_t, cond_er_in, w_base, b_base, lora_a, lora_b, wq, wk, wv, wo, cs_w1, cs_b1, cs_w2,
                        cs_b2, decay, c2_w, c2_mask, c2_bias, ln1_g, ln1_b, ln2_g, ln2_b, fq, fk, fv, fo, fg,
                        fw, fb1, fb2, ident_in, pad_ids, out):
    with ExitStack() as ctx:
        def sb(name, shape, dt=F32):
            return ctx.enter_context(nc.sbuf_tensor(name, shape, dt))

        def sem(name):
            return ctx.enter_context(nc.semaphore(name))

        bank = [ctx.enter_context(nc.psum_tensor(f"bank{i}", [P, 512], F32)) for i in range(8)]

        tbank = [b[:, :].bitcast(F16).rearrange("p (q t) -> p q t", t=TB) for b in bank[6:8]]

        w_all = sb("w_all", [P, E, 2, 2, W2_AT], F16)
        arena = w_all[:, :, :, :, :].rearrange("p e k s w -> p (e k s w)").bitcast(F32)
        taken = [0]

        def carve(shape, dt=F32):
            n = 1
            for k in shape[1:]:
                n *= k
            words = n * (2 if dt in (F16, BF16) else 4) // 4
            a = arena[:, taken[0]:taken[0] + words]
            taken[0] += words
            assert taken[0] <= E * WE
            if dt != F32:
                a = a.bitcast(dt)
            names = "abcdefg"[:len(shape) - 1]
            if len(names) > 1:
                a = a.rearrange(f"p ({' '.join(names)}) -> p {' '.join(names)}", **dict(zip(names[1:], shape[2:])))
            return a

        xs = nc.dram_tensor("rows_by_expert", [NROWS, ROW // 2], I32, kind="Internal").ap()
        w_split = nc.dram_tensor("w_split", [P, E * 2, 2, W2_AT], F16, kind="Internal").ap()

        w_base_s = carve([P, CH, D])
        lora_a_s = carve([P, CH, P])
        lora_b_s = carve([P, D])
        wq_s, wk_s, wv_s, wo_s = [carve([P, CH, D]) for n in ("wq_s", "wk_s", "wv_s", "wo_s")]
        cs_w1_s = sb("cs_w1_s", [P, CH, DC])
        cs_w2_s = sb("cs_w2_s", [DC, D])
        fg_s = sb("fg_s", [P, CH, E])
        c2_mask_s = sb("c2_mask_s", [P, CH, D])
        c2_bias_s = sb("c2_bias_s", [P, D])
        cond_er = sb("cond_er_s", [P, B])
        cond_all = sb("cond_all", [P, E, B])
        b_base_s = sb("b_base_s", [P, CH])
        cs_b1_s = sb("cs_b1_s", [DC, 1])
        cs_b2_s = sb("cs_b2_s", [P, CH])
        decay_s = sb("decay_s", [P, CH])
        lng = sb("lng", [P, 2, CH])
        ident = sb("ident", [P, P])
        half_b2 = sb("half_b2", [P, CH])
        base_t = sb("base_t", [P, CH])
        base_11 = sb("base_11", [P, CH])
        base_01 = sb("base_01", [P, CH])
        par_mask = sb("par_mask", [P, 2])
        causal = sb("causal", [P, T])
        zeros = sb("zeros", [P, D])
        scale_w = sb("scale_w", [P, 2])
        same_head = sb("same_head", [P, 2, T], BF16)
        diag_ones = sb("diag_ones", [P, T])
        expo = sb("expo", [P, NT])
        iota8 = sb("iota8", [P, E])
        iota8u = sb("iota8u", [P, E], mybir.dt.int32)

        xt = carve([P, CH, GT])
        lora_h = carve([P, GT])
        y0t = carve([P, CH, GT])
        cs_h = carve([P, GT])
        lc = carve([P, CH * GT])
        lam = carve([P, CH * GT])
        lam_first = carve([P, CH * GT])
        cum = carve([P, CH * GT])
        cum_mid = carve([P, CH * GB])
        cum_inv = carve([P, CH * GT])
        v_decay = carve([P, GB, NR * CH, PW])
        k_decay = carve([P, CH, GB, 2, T])
        q_decay = carve([P, CH, GB, NR, T])
        s_decay = carve([P, GB, CH, NR, T])
        yt = carve([P, CH, GT])
        c2_w_s = carve([P, CH, E, D])
        xg = carve([P, 2, CH, GT])
        x1t = carve([P, CH, GT])
        fq_s, fk_s, fv_s, fo_s = [carve([P, CH, D]) for n in ("fq_s", "fk_s", "fv_s", "fo_s")]
        ht = carve([P, CH, GT])
        v_pair = carve([P, GB, NR * CH, PW])
        k_pair = carve([P, CH, GB, 2, T])
        q_block = carve([P, CH, GB, NR, T])
        q_pair = carve([P, CH, GB, 2, T], BF16)
        k_block = carve([P, CH, GB, NR, T], BF16)
        probs = carve([P, GB, CH, NR, T])
        ctx_t = carve([P, CH, GT])
        hn = carve([P, NT, D])
        z = carve([P, NT, D])
        ctxn = carve([P, NT, D])
        tick_s = sb("tick_s", [P, 2])
        pool_tick = sb("pool_tick", [P, 2])
        stats = sb("stats", [P, NT, 6])
        mv = sb("mv", [P, NT, 2])
        var_e = sb("var_e", [P, NT])
        rstd = sb("rstd", [P, NT])
        row_max = sb("row_max", [P, GB, CH * NR])
        shift = sb("shift", [P, 2, CH * NR, T], BF16)
        sum_inv = sb("sum_inv", [P, NT, CH * NR, 2])
        lg = sb("lg", [P, NT, E])
        top = sb("top", [P, NT, 8])
        top_i = sb("top_i", [P, NT, 8], U32)
        top_f = sb("top_f", [P, NT, 8])
        ex = sb("ex", [P, NT, E])
        ex_sum = sb("ex_sum", [P, NT])
        two_sum = sb("two_sum", [P, NT])
        pick = sb("pick", [P, NT, 2, E])
        m_tm = sb("m_tm", [P, NT, D])
        acc = sb("acc", [P, NT, D])
        stage = sb("stage", [P, W2_AT])
        hid_s = sb("hid_s", [P, 2, 2, FC, TB], F16)
        halves = hid_s[:, 0, :, :, :].rearrange("p s f t -> p s (f t)")
        rows = sb("rows", [P, NT, ROW], F16)
        ln2_rows = sb("ln2_rows", [P, 2, D])
        lower = sb("lower", [P, P])
        ones = sb("ones", [P, P])
        picked = sb("picked", [P, NT, E])
        rank = sb("rank", [P, NT, E])
        tot = sb("tot", [P, NT, E])
        before = sb("before", [P, NT + 1, E])
        region0 = sb("region0", [P, E])
        slot = sb("slot", [P, K, NT, E])
        pos_f = sb("pos_f", [P, K, NT])
        pos_u = sb("pos_u", [P, K, NT], U32)
        tok_g = sb("tok_g", [P, NT])

        pad_row = sb("pad_row", [P, ROW], F16)
        pad_at = sb("pad_at", [P, E], I32)
        alone_pos = sb("alone_pos", [P, 1], U32)
        pad_at_f = sb("pad_at_f", [P, E])
        pid_u = sb("pid_u", [P, 1], I32)
        pid = sb("pid", [P, 1])
        tile_k = sb("tile_k", [P, NK])
        tile_ku = sb("tile_ku", [P, NJ], I32)
        tile_j = sb("tile_j", [P, NJ])
        cmp_k = sb("cmp_k", [P, E, NK])
        n_tiles = sb("n_tiles", [P, E])
        tiles_to = sb("tiles_to", [P, E])
        past = sb("past", [P, NJ, E])
        past_n = sb("past_n", [P, NJ, E])
        tile_e = sb("tile_e", [P, NJ])
        tile_first = sb("tile_first", [P, NJ])
        tile_row = sb("tile_row", [P, NJ])
        tile_e_i = sb("tile_e_i", [P, NJ], I32)
        tile_row_i = sb("tile_row_i", [P, NJ], I32)
        ones8 = sb("ones8", [P, E])
        b1_all = sb("b1_all", [P, E, FC])
        b2_f = probs[0:1, :, :, :, :].rearrange("p b c r t -> p (b c r t)")[:, 0:E * D].rearrange("p (e d) -> p e d", e=E)
        b2_s = sb("b2_s", [1, 2, E, D], F16)
        ones_h = sb("ones_h", [1, P], F16)
        id_h = sb("id_h", [P, P], F16)
        srows = sb("srows", [P, UNROLL, ST, ROW], F16)
        sxt = sb("sxt", [P, 2, 2 * CH, TB], F16)
        hid = stage[:, :].rearrange("p (f t) -> p f t", f=FC)
        ys = sb("ys", [P, ST, D])

        names = ("first_in weights_in z_weights xt_in consts_made mask_done derived setup_steps decay_steps ffn_steps route_steps table_steps row_steps split_steps ticks "
                 "lora_ready lora_kept y0_ready y0_kept cs1_ready cs1_kept cs2_ready lc_kept v_ready v_kept "
                 "k_ready k_kept q_ready q_kept s_ready s_kept y_ready y_kept o_ready x1t_kept "
                 "xg_made xg_used x1_ready x1_kept z_ready z_kept var_made rstd_made hn_made ht_ready ht_kept "
                 "qb_ready qb_kept kb_ready kb_kept kp_kept qp_kept vb_ready vb_kept smax_ready max_kept shift_made st_ready p_kept "
                 "pv_ready ctx_kept ctxt_ready ctxt_kept wo_ready z2_kept acc_made mt_ready mt_kept gate_ready lg_made "
                 "logits_kept ex_made stage_in split_made split_out m_made rows_made ranks_ready ranks_kept pos_made scattered acc_out "
                 "w_in pads_out tables_made zero_rows t_ready xt_kept h_ready h_kept hid_split hi_made "
                 "ye_ready ye_kept added ").split()
        names += [f"srows_in{k}" for k in range(UNROLL)]
        s = {n: sem(n) for n in names}

        CONSTS = 21
        DECAY_STEPS = 8
        FFN_STEPS = 6
        ROUTE_STEPS = 18
        START = 1
        software = ("scattered", "added")

        HALF = T // 2

        block = ctx.enter_context(nc.Block())
        first_loads = [
            (lora_a_s, lora_a), (cond_er, cond_er_in), (ident, ident_in), (w_base_s, w_base), (lora_b_s, lora_b),
            (b_base_s, b_base), (decay_s, decay), (cs_b2_s, cs_b2), (cs_b1_s, cs_b1), (cs_w1_s, cs_w1), (wv_s, wv),
            (cs_w2_s, cs_w2), (wk_s, wk), (wq_s, wq)]
        loads = [
            (c2_w_s, c2_w), (c2_mask_s, c2_mask), (b2_f, fb2), (wo_s, wo), (c2_bias_s, c2_bias.partition_broadcast(P)),
            (cond_all, cond_t.partition_broadcast(P)), (fq_s, fq), (fk_s, fk), (fv_s, fv), (lng[:, 0, :], ln1_g),
            (lng[:, 1, :], ln1_b), (fo_s, fo), (fg_s, fg), (ln2_rows[:, 0, :], ln2_g.partition_broadcast(P)),
            (ln2_rows[:, 1, :], ln2_b.partition_broadcast(P)), (b1_all, fb1)]
        FIRST_IN, W_IN = 16 * len(first_loads), 16 * len(loads)

        def fill_up(queue, experts):
            queue.wait_ge(s["tables_made"], START + 1)
            pads = pad_row[:, :].bitcast(I32).unsqueeze(1).to_broadcast([P, ST, ROW // 2])
            for e in experts:
                at = queue.value_load(pad_at[0:1, e:e + 1], min_val=0, max_val=E * REGION)
                queue.dma_start(xs[bass.ds(at, TB), :].rearrange("(n p) w -> p n w", p=P), pads).then_inc(s["pads_out"], 16)

        @block.sync
        def _(sp):
            sp.dma_start(xt[:, :, :], x_t[:, :, 0:GT]).then_inc(s["xt_in"], 16)
            for dst, src in first_loads:
                sp.dma_start(dst[:], src).then_inc(s["first_in"], 16)
            for n in names:
                if n not in software:
                    sp.sem_inc(s[n], START)
            for dst, src in loads:
                sp.dma_start(dst[:], src).then_inc(s["weights_in"], 16)
            sp.wait_ge(s["consts_made"], START + CONSTS)
            sp.dma_start(out[NTOK:NTOK + P, :], zeros[:, :]).then_inc(s["zero_rows"], 16)
            sp.dma_start(pad_row[:, ID_AT:ID_AT + 2].bitcast(I32), pad_ids).then_inc(s["zero_rows"], 16)
            sp.wait_ge(s["zero_rows"], START + 32)
            sp.dma_start(xs[E * REGION + P:NROWS, :], pad_row[:, :].bitcast(I32)).then_inc(s["pads_out"], 16)

            def weights_in(i):
                sp.wait_ge(s["split_made"], START + i)
                sp.dma_start(stage[:, :], fw[:, bass.ds(i, 1), :].rearrange("p e w -> p (e w)")).then_inc(s["stage_in"], 16)

            def halves_out(i):
                sp.wait_ge(s["split_made"], START + i + 1)
                sp.dma_start(w_split[:, bass.ds(i, 1), :, :].rearrange("p e s w -> p (e s) w"),
                             halves[:, :, :]).then_inc(s["split_out"], 16)

            def x_in(i):
                sp.wait_ge(s["x1t_kept"], START + i)
                sp.dma_start(xt[:, :, :], x_t[:, :, bass.ds(i * GT, GT)]).then_inc(s["xt_in"], 16)

            weights_in(0)
            x_in(1)
            with sp.Fori(2, NG) as i:
                x_in(i)
                halves_out(i - 2)
                weights_in(i - 1)

            def expert_in(e):
                if e:
                    sp.wait_ge(s["w_in"], START + e * 16)
                sp.dma_start(w_all[:, e, :, :, :], w_split[:, 2 * e:2 * e + 2, :, :]).then_inc(s["w_in"], 16)

            halves_out(NG - 2)
            weights_in(NG - 1)
            sp.wait_ge(s["split_out"], START + (NG - 1) * 16)
            sp.wait_ge(s["x1t_kept"], START + NG)
            expert_in(0)
            sp.wait_ge(s["acc_out"], START + (NG - 1) * 16)
            expert_in(1)
            expert_in(2)
            sp.wait_ge(s["z_ready"], START + NG)
            expert_in(3)
            sp.wait_ge(s["x1_ready"], START + NG)
            sp.wait_ge(s["ht_kept"], START + NG)
            sp.wait_ge(s["vb_ready"], START + NG)
            expert_in(4)
            halves_out(NG - 1)
            sp.wait_ge(s["zero_rows"], START + 32)
            fill_up(sp, range(0, E, 2))
            sp.wait_ge(s["pads_out"], START + (E + 1) * 16)
            sp.wait_ge(s["scattered"], 16 + NG * K * NT * 16)
            sp.wait_ge(s["tables_made"], START + 3)

            def load(i, k):
                j = i * UNROLL + k
                row = sp.value_load(tile_row_i[0:1, bass.ds(j, 1)], min_val=0, max_val=E * REGION)
                sp.dma_start(srows[:, k, :, :].bitcast(I32),
                             xs[bass.ds(row, TB), :].rearrange("(n p) w -> p n w", p=P)).then_inc(s[f"srows_in{k}"], 16)

            for k in range(UNROLL):
                load(0, k)
            sp.wait_ge(s["split_out"], START + NG * 16)
            sp.wait_ge(s["acc_made"], START + NG)
            sp.wait_ge(s["gate_ready"], START + NG)
            for e in range(5, E):
                expert_in(e)
            with sp.Fori(1, NI) as i:
                for k in range(UNROLL):
                    sp.wait_ge(s["added"], 16 + (i * UNROLL + (k - UNROLL + 1)) * (ST * 16))
                    load(i, k)
            for k in range(REST):
                sp.wait_ge(s["added"], 16 + (NI * UNROLL + (k - UNROLL + 1)) * (ST * 16))
                load(NI, k)
            sp.wait_ge(s["added"], 16 + NJ * ST * 16)
            sp.wait_ge(s["acc_out"], START + NG * 16)

        @block.gpsimd
        def _(pool):
            nc.gpsimd.memset(par_mask[:], 1.0).then_inc(s["consts_made"], 1)
            nc.gpsimd.memset(causal[:], 1.0).then_inc(s["consts_made"], 1)
            nc.gpsimd.memset(same_head[:], 1.0).then_inc(s["consts_made"], 1)
            nc.gpsimd.memset(expo[:], -0.5).then_inc(s["consts_made"], 1)
            nc.gpsimd.memset(ones[:], 1.0).then_inc(s["consts_made"], 1)
            nc.gpsimd.memset(lower[:], 1.0).then_inc(s["consts_made"], 1)
            nc.gpsimd.memset(zeros[:], 0.0).then_inc(s["consts_made"], 1)
            nc.gpsimd.memset(pad_row[:], 0.0).then_inc(s["consts_made"], 1)
            nc.gpsimd.memset(ones_h[:], 1.0).then_inc(s["consts_made"], 1)
            nc.gpsimd.iota(pid_u[:], [[0, 1]], base=0, channel_multiplier=1).then_inc(s["consts_made"], 1)
            nc.gpsimd.iota(tile_ku[:], [[1, NJ]], base=0, channel_multiplier=0).then_inc(s["consts_made"], 1)
            nc.gpsimd.memset(v_pair[:], 0.0).then_inc(s["consts_made"], 1)
            nc.gpsimd.memset(v_decay[:], 0.0).then_inc(s["consts_made"], 1)
            nc.gpsimd.memset(q_decay[:], 0.0).then_inc(s["consts_made"], 1)
            nc.gpsimd.memset(q_block[:], 0.0).then_inc(s["consts_made"], 1)
            nc.gpsimd.memset(k_block[:], 0.0).then_inc(s["consts_made"], 1)
            nc.gpsimd.memset(lam_first[:], 0.0).then_inc(s["consts_made"], 1)
            nc.gpsimd.iota(iota8u[:], [[1, E]], base=0, channel_multiplier=0).then_inc(s["consts_made"], 1)
            pool.wait_ge(s["consts_made"], START + 18)
            nc.gpsimd.affine_select(out=lower[:, :], in_=lower[:, :], compare_op=ALU.is_gt, fill=0.0,
                                    base=0, pattern=[[1, P]], channel_multiplier=-1).then_inc(s["consts_made"], 1)
            pool.wait_ge(s["consts_made"], START + 19)
            for half in range(2):
                rows_ = slice(half * T, half * T + T)
                nc.gpsimd.affine_select(out=causal[rows_, :], in_=causal[rows_, :], compare_op=ALU.is_ge, fill=0.0,
                                        base=0, pattern=[[1, T]], channel_multiplier=-1).then_inc(s["consts_made"], 1)
                pool.wait_ge(s["consts_made"], START + 20 + half)
            pool.wait_ge(s["consts_made"], START + CONSTS)
            pool.wait_ge(s["mask_done"], START + 6)
            pool.wait_ge(s["weights_in"], START + W_IN)
            G = nc.gpsimd

            def then(ins, name, i, k):
                ins.then_inc(s[name], 1)
                pool.wait_ge(s[name], i * 2 + (START + k))

            def tick(n):
                pool.wait_ge(s["ticks"], START + n)
                G.tensor_tensor(pool_tick[:, 0:1], pool_tick[:, 1:2], pool_tick[:, 1:2], ALU.mult).then_inc(s["ticks"], 1)

            def first_norm(i):
                pool.wait_ge(s["var_made"], START + i * 2 + 1)
                G.tensor_tensor(rstd[:], var_e[:], expo[:], ALU.pow).then_inc(s["rstd_made"], 1)

            def scale_weights(i):
                pool.wait_ge(s["stage_in"], START + i * 16 + 16)
                then(G.tensor_tensor(stage[:, :], stage[:, :], scale_w[:, 0:1].to_broadcast([P, W2_AT]), ALU.mult), "split_steps", i, 1)

            def split_weights(i):
                pool.wait_ge(s["split_out"], START + i * 16)
                then(G.tensor_tensor(halves[:, 0, :], stage[:, :], scale_w[:, 1:2].to_broadcast([P, W2_AT]), ALU.add), "split_steps", i, 2)
                G.tensor_tensor(halves[:, 1, :], stage[:, :], halves[:, 0, :], ALU.subtract).then_inc(s["split_made"], 1)

            def shifts(i):
                for b in range(GB):
                    pool.wait_ge(s["max_kept"], START + i * GB + b + 1)
                    if b >= 2:
                        pool.wait_ge(s["st_ready"], START + i * GB + b - 1)
                    G.tensor_tensor(shift[:, b % 2, :, :], row_max[:, b, :].unsqueeze(2).to_broadcast([P, CH * NR, T]),
                                    diag_ones[:, :].unsqueeze(1).to_broadcast([P, CH * NR, T]), ALU.mult).then_inc(s["shift_made"], 1)

            def second_norm(i):
                pool.wait_ge(s["var_made"], START + i * 2 + 2)
                G.tensor_tensor(rstd[:], var_e[:], expo[:], ALU.pow).then_inc(s["rstd_made"], 1)
                pool.wait_ge(s["hn_made"], START + i * (2 * NT) + 2 * NT)
                then(G.tensor_tensor(m_tm[:, :, :], hn[:, :, :], ln2_rows[:, 0, :].unsqueeze(1).to_broadcast([P, NT, D]), ALU.mult), "row_steps", i, 1)
                G.tensor_tensor(m_tm[:, :, :], m_tm[:, :, :], ln2_rows[:, 1, :].unsqueeze(1).to_broadcast([P, NT, D]), ALU.add).then_inc(s["m_made"], 1)

            def expert_rows(i):
                pool.wait_ge(s["m_made"], START + i + 1)
                pool.wait_ge(s["scattered"], 16 + i * (K * NT * 16))
                then(G.tensor_tensor(rows[:, :, 0:D], m_tm[:, :, :], scale_w[:, 1:2].unsqueeze(2).to_broadcast([P, NT, D]), ALU.add), "row_steps", i, 2)
                G.tensor_tensor(rows[:, :, D:2 * D], m_tm[:, :, :], rows[:, :, 0:D], ALU.subtract).then_inc(s["rows_made"], 1)

            def scatter(i):
                pool.wait_ge(s["rows_made"], START + i + 1)
                pool.wait_ge(s["pos_made"], START + i + 1)
                tick(i)
                for t in range(NT):
                    for k in range(K):
                        G.indirect_dma_start(out=xs[:, :], out_offset=bass.IndirectOffsetOnAxis(ap=pos_u[:, k, t:t + 1], axis=0),
                                             in_=rows[:, t, :].bitcast(I32), in_offset=None).then_inc(s["scattered"], 16)

            def groups(h, finish=True, send=True):
                if finish:
                    second_norm(h - 1)
                if send:
                    scatter(h - 2)
                scale_weights(h)
                first_norm(h)
                if finish:
                    expert_rows(h - 1)
                shifts(h)
                split_weights(h)

            pool.wait_ge(s["zero_rows"], START + 32)
            pool.wait_ge(s["mask_done"], START + 6)
            G.indirect_dma_start(out=xs[:, :], out_offset=bass.IndirectOffsetOnAxis(ap=alone_pos[:, :], axis=0),
                                 in_=pad_row[:, :].bitcast(I32), in_offset=None).then_inc(s["scattered"], 16)
            G.indirect_dma_start(out=out[:, :], out_offset=bass.IndirectOffsetOnAxis(ap=pad_row[:, ID_AT:ID_AT + 2].bitcast(U32), axis=0),
                                 in_=zeros[:, :], in_offset=None, compute_op=ALU.add).then_inc(s["added"], 16)
            groups(0, finish=False, send=False)
            groups(1, send=False)
            with pool.Fori(2, NG) as h:
                groups(h)
            second_norm(NG - 1)
            scatter(NG - 2)
            expert_rows(NG - 1)
            scatter(NG - 1)
            pool.wait_ge(s["acc_out"], START + NG * 16)

            def add(i, tiles):
                for k in range(tiles):
                    for st in range(ST):
                        j = i * (UNROLL * ST) + (k * ST + st)
                        pool.wait_ge(s["added"], 16 + j * 16)
                        pool.wait_ge(s["ye_kept"], START + j + 1)
                        tick(NG + j)
                        G.indirect_dma_start(out=out[:, :],
                                             out_offset=bass.IndirectOffsetOnAxis(ap=srows[:, k, st, ID_AT:ID_AT + 2].bitcast(U32), axis=0),
                                             in_=ys[:, st, :], in_offset=None, compute_op=ALU.add).then_inc(s["added"], 16)

            with pool.Fori(0, NI) as i:
                add(i, UNROLL)
            add(NI, REST)

        @block.tensor
        def _(pe):
            def mm(o, l, r, first, last):
                return nc.tensor.matmul(o, l, r, start=first, stop=last, skip_group_check=True)

            def wait(name, v):
                pe.wait_ge(s[name], START + v)

            wait("first_in", FIRST_IN)
            wait("consts_made", CONSTS)
            wait("derived", 1)
            wait("mask_done", 6)

            def project(o, w, x):
                for n in range(CH):
                    for c in range(CH):
                        last = mm(o[:, n * GT:(n + 1) * GT], w[:, c, n * P:(n + 1) * P], x[:, c, :], c == 0, c == CH - 1)
                return last

            def project_tokens(o, w, x):
                for t in range(NT):
                    for c in range(CH):
                        last = mm(o[:, t * D:(t + 1) * D], x[:, c, t * P:(t + 1) * P], w[:, c, :], c == 0, c == CH - 1)
                return last

            def to_features(o, x):
                for c in range(CH):
                    for t in range(NT):
                        last = nc.tensor.transpose(o[:, c * GT + t * P:c * GT + (t + 1) * P], x[:, t, c * P:(c + 1) * P], ident[:, :])
                return last

            def lora(i):
                wait("xt_in", i * 16 + 16)
                wait("s_kept", i * GB)
                for c in range(CH):
                    last = mm(bank[0][:, 0:GT], lora_a_s[:, c, :], xt[:, c, :], c == 0, c == CH - 1)
                last.then_inc(s["lora_ready"], 1)

            def conditioned(i):
                wait("y_kept", i)
                for o in range(CH):
                    for c in range(CH):
                        mm(bank[1][:, o * GT:(o + 1) * GT], w_base_s[:, c, o * P:(o + 1) * P], xt[:, c, :], o == 0 and c == 0, False)

            def conditioned_lora(i):
                wait("lora_kept", i + 1)
                for o in range(CH):
                    last = mm(bank[1][:, o * GT:(o + 1) * GT], lora_b_s[:, o * P:(o + 1) * P], lora_h[:, :], False, True)
                last.then_inc(s["y0_ready"], 1)

            def decay_first(i):
                wait("y0_kept", i + 1)
                wait("x1t_kept", i)
                for c in range(CH):
                    last = mm(bank[2][0:DC, 0:GT], cs_w1_s[:, c, :], y0t[:, c, :], c == 0, c == CH - 1)
                last.then_inc(s["cs1_ready"], 1)
                project_tokens(bank[3], wv_s, y0t).then_inc(s["v_ready"], 1)

            def decay_second(i):
                wait("cs1_kept", i + 1)
                for c in range(CH):
                    last = mm(bank[0][:, c * GT:(c + 1) * GT], cs_w2_s[:, c * P:(c + 1) * P], cs_h[0:DC, :], True, True)
                last.then_inc(s["cs2_ready"], 1)
                project(bank[1], wk_s, y0t).then_inc(s["k_ready"], 1)
                project(bank[2], wq_s, y0t).then_inc(s["q_ready"], 1)

            def decayed_scores(i, sequences):
                for b in sequences:
                    if b == 0:
                        wait("lc_kept", i + 1)
                        wait("v_kept", i + 1)
                        wait("k_kept", i + 1)
                        wait("q_kept", i + 1)
                    if b >= 2:
                        wait("s_kept", i * GB + b - 1)
                    for c in range(CH):
                        last = mm(bank[3 * (b % 2)][:, c * NR * T:(c + 1) * NR * T],
                                  k_decay[:, c, b, :, :].rearrange("p a t -> p (a t)"),
                                  q_decay[:, c, b, :, :].rearrange("p r t -> p (r t)"), True, True)
                    last.then_inc(s["s_ready"], 1)

            def attended(i):
                for b in range(GB):
                    wait("s_kept", i * GB + b + 1)
                    for c in range(CH):
                        for r in range(NR):
                            last = mm(bank[1][32 * r:32 * r + 32, (c * GB + b) * T:(c * GB + b + 1) * T],
                                      v_decay[:, b, c * NR + r, 0:PV], s_decay[:, b, c, r, :], True, True)
                last.then_inc(s["y_ready"], 1)

            def output_projection(i):
                wait("y_kept", i + 1)
                project(bank[2], wo_s, yt).then_inc(s["o_ready"], 1)

            def x1_to_tokens(i):
                wait("x1t_kept", i + 1)
                wait("mt_kept", i)
                for t in range(NT):
                    for c in range(CH):
                        last = nc.tensor.transpose(bank[5][:, t * D + c * P:t * D + (c + 1) * P], x1t[:, c, t * P:(t + 1) * P], ident[:, :])
                last.then_inc(s["x1_ready"], 1)

            def mixed(i, g):
                if g == 0:
                    wait("z2_kept", i)
                wait("xg_made", i * E + g + 1)
                for t in range(NT):
                    for c in range(CH):
                        last = mm(bank[4][:, t * D:(t + 1) * D], xg[:, g % 2, c, t * P:(t + 1) * P], c2_w_s[:, c, g, :],
                                  g == 0 and t == 0 and c == 0, g == E - 1 and c == CH - 1)
                last.then_inc(s["z_ready"] if g == E - 1 else s["xg_used"], 1)

            def first_norm(i):
                wait("x1_kept", i + 1)
                wait("hn_made", i * (2 * NT) + NT)
                to_features(bank[5], hn).then_inc(s["ht_ready"], 1)

            def softmax_operands(i):
                wait("ht_kept", i + 1)
                wait("ctxt_kept", i)
                project(bank[7], fk_s, ht).then_inc(s["kb_ready"], 1)
                wait("logits_kept", i)
                project(bank[6], fq_s, ht).then_inc(s["qb_ready"], 1)
                wait("z_kept", i + 1)
                project_tokens(bank[4], fv_s, ht).then_inc(s["vb_ready"], 1)

            def by_query(i, b):
                if b == 0:
                    wait("kb_kept", i + 1)
                    wait("qp_kept", i + 1)
                if b == 1:
                    wait("qb_kept", i + 1)
                if b >= 2:
                    wait("max_kept", i * GB + b - 1)
                for c in range(CH):
                    last = mm(bank[5 + b % 2][:, c * NR * T:(c + 1) * NR * T],
                              q_pair[:, c, b, :, :].rearrange("p a t -> p (a t)"),
                              k_block[:, c, b, :, :].rearrange("p r t -> p (r t)"), True, True)
                last.then_inc(s["smax_ready"], 1)

            def by_key(i, b):
                bk = bank[7 if b % 2 == 0 else 4]
                wait("shift_made", i * GB + b + 1)
                if b == 0:
                    wait("kp_kept", i + 1)
                    wait("vb_kept", i + 1)
                if b >= 2:
                    wait("p_kept", i * GB + b - 1)
                mm(bk[:, :], same_head[:, :, :].rearrange("p a t -> p (a t)"),
                   shift[:, b % 2, :, :].rearrange("p n t -> p (n t)"), True, False)
                for c in range(CH):
                    last = mm(bk[:, c * NR * T:(c + 1) * NR * T],
                              k_pair[:, c, b, :, :].rearrange("p a t -> p (a t)"),
                              q_block[:, c, b, :, :].rearrange("p r t -> p (r t)"), False, True)
                last.then_inc(s["st_ready"], 1)

            def weighted(i, b):
                t, n = b // 2, b % 2
                wait("p_kept", i * GB + b + 1)
                if b == 0:
                    wait("max_kept", i * GB + GB)
                for pr in range(CH * NR):
                    last = mm(bank[5 + t][n * T:(n + 1) * T, pr * PW:(pr + 1) * PW],
                              probs[:, b, pr // NR, pr % NR, :], v_pair[:, b, pr, :], True, True)
                if n == 1:
                    last.then_inc(s["pv_ready"], 1)

            def context_to_features(i):
                wait("p_kept", i * GB + GB)
                wait("ctx_kept", i * NT + NT)
                to_features(bank[7], ctxn).then_inc(s["ctxt_ready"], 1)

            def context_projection(i):
                wait("ctxt_kept", i + 1)
                project_tokens(bank[4], fo_s, ctx_t).then_inc(s["wo_ready"], 1)

            def second_norm(i):
                wait("m_made", i + 1)
                to_features(bank[5], m_tm).then_inc(s["mt_ready"], 1)

            def gating(i):
                wait("mt_kept", i + 1)
                for t in range(NT):
                    for c in range(CH):
                        last = mm(bank[6][:, t * E:(t + 1) * E], ht[:, c, t * P:(t + 1) * P], fg_s[:, c, :], c == 0, c == CH - 1)
                last.then_inc(s["gate_ready"], 1)

            def ranks(i):
                wait("lg_made", i + 1)
                pk = picked[:, :, :].rearrange("p t e -> p (t e)")
                mm(bank[3][:, 0:NT * E], lower[:, :], pk, True, True)
                mm(bank[3][:, NT * E:2 * NT * E], ones[:, :], pk, True, True).then_inc(s["ranks_ready"], 1)

            def groups(i, finish=True, begin=True):
                h, g = i - 1, i - 2
                if not finish:
                    mixed(h, 0)
                    mixed(h, 1)
                if begin:
                    lora(i)
                if finish:
                    context_to_features(g)
                if begin:
                    conditioned(i)
                if finish:
                    context_projection(g)
                if begin:
                    conditioned_lora(i)
                if finish:
                    mixed(h, 0)
                    mixed(h, 1)
                if begin:
                    decay_first(i)
                mixed(h, 2)
                if begin:
                    decay_second(i)
                mixed(h, 3)
                if finish:
                    second_norm(g)
                mixed(h, 4)
                if finish:
                    gating(g)
                mixed(h, 5)
                mixed(h, 6)
                mixed(h, 7)
                if begin:
                    decayed_scores(i, (0, 1))
                x1_to_tokens(h)
                if begin:
                    decayed_scores(i, (2,))
                first_norm(h)
                if begin:
                    decayed_scores(i, (3,))
                softmax_operands(h)
                if begin:
                    attended(i)
                by_query(h, 0)
                by_query(h, 1)
                if begin:
                    output_projection(i)
                by_query(h, 2)
                by_query(h, 3)
                by_key(h, 0)
                by_key(h, 1)
                by_key(h, 2)
                weighted(h, 0)
                by_key(h, 3)
                weighted(h, 1)
                if finish:
                    ranks(g)
                weighted(h, 2)
                weighted(h, 3)

            lora(0)
            conditioned(0)
            conditioned_lora(0)
            decay_first(0)
            decay_second(0)
            decayed_scores(0, range(GB))
            attended(0)
            wait("weights_in", W_IN)
            output_projection(0)
            wait("z_weights", 1)
            groups(1, finish=False)
            with pe.Fori(2, NG) as i:
                groups(i)
            groups(NG, begin=False)
            context_to_features(NG - 1)
            context_projection(NG - 1)
            second_norm(NG - 1)
            gating(NG - 1)
            ranks(NG - 1)

            wait("ranks_kept", NG)
            wait("mt_kept", NG)
            wait("tables_made", 3)

            def transposes(i, k):
                wait(f"srows_in{k % UNROLL}", (i + k // UNROLL) * 16 + 16)
                for q in range(2 * CH):
                    for st in range(ST):
                        last = nc.tensor.transpose(tbank[k % 2][:, q, st * P:(st + 1) * P],
                                                   srows[:, k % UNROLL, st, q * P:(q + 1) * P], id_h[:, :])
                last.then_inc(s["t_ready"], 1)

            def up(i, k, e, first):
                j = i * UNROLL + k
                x = sxt[:, k % 2, :, :]
                if first:
                    wait("w_in", e * 16 + 16)
                wait("xt_kept", j + 1)
                for n in range(HC):
                    if not (first and k == 0):
                        wait("h_kept", j * HC + (n + 1 - HC))
                    for f in range(2 * n, 2 * n + 2):
                        o = bank[n][:, (f % 2) * TB:(f % 2 + 1) * TB]
                        for c in range(CH):
                            for ws, xsi in ((0, 0), (0, 1), (1, 0)):
                                w = w_all[:, bass.ds(e, 1), 0, ws, c * F + f * P:c * F + (f + 1) * P].rearrange("p o w -> p (o w)")
                                last = mm(o, w, x[:, xsi * CH + c, :], c == 0 and ws == 0 and xsi == 0, c == CH - 1 and ws == 1)
                    last.then_inc(s["h_ready"], 1)

            def down(i, k, e, first):
                j = i * UNROLL + k
                if not first:
                    wait("ye_kept", j * ST)
                wait("hid_split", j * HC + HC)
                for st in range(ST):
                    o = bank[4 + st][:, 0:D]
                    for half in range(2):
                        mm(o, ones_h[:, :], b2_s[:, half, bass.ds(e, 1), :].rearrange("p o w -> p (o w)"), half == 0, False)
                    for f in range(FC):
                        for ws, hs in ((0, 0), (0, 1), (1, 0)):
                            w = w_all[:, bass.ds(e, 1), 1, ws, f * D:(f + 1) * D].rearrange("p o w -> p (o w)")
                            last = mm(o, hid_s[:, k % 2, hs, f, st * P:(st + 1) * P], w, False, f == FC - 1 and ws == 1)
                    last.then_inc(s["ye_ready"], 1)

            def expert(i, k):
                return pe.value_load(tile_e_i[0:1, bass.ds(i * UNROLL + k, 1)], min_val=0, max_val=E - 1)

            def body(i, first, tiles=UNROLL):
                e = {0: expert(i, 0)}
                for k in range(tiles):
                    up(i, k, e[k], first)
                    if tiles == UNROLL or k + 1 < tiles:
                        transposes(i, k + 1)
                    if k + 1 < tiles:
                        e[k + 1] = expert(i, k + 1)
                    if k == 0 and not first:
                        e[-1] = expert(i, -1)
                    if not (first and k == 0):
                        down(i, k - 1, e[k - 1], first and k == 1)

            transposes(0, 0)
            body(0, True)
            wait("w_in", E * 16)
            with pe.Fori(1, NI) as i:
                body(i, False)
            body(NI, False, REST)
            down(NI, REST - 1, expert(NI, REST - 1), False)

        @block.scalar
        def _(act):
            def wait(name, v):
                act.wait_ge(s[name], START + v)

            A = nc.scalar.activation
            wait("first_in", FIRST_IN)
            A(base_t[:, :], decay_s[:, :], ACT.Tanh, scale=0.5).then_inc(s["derived"], 1)
            wait("consts_made", CONSTS)
            wait("mask_done", 6)

            def keep_values(bk, dst):
                for n in range(2):
                    for par in range(2):
                        src = bk[n * T:(n + 1) * T, :].rearrange("p (t q a f) -> p t q a f", t=NT, q=CH * NR, a=2)[:, :, :, par, :]
                        last = nc.scalar.copy(dst[par * T:(par + 1) * T, n:GB:2, :, par * DH:par * DH + DH], src)
                return last

            def keep_y0(i):
                wait("y0_ready", i + 1)
                wait("q_ready", i)
                for o in range(CH):
                    last = A(y0t[:, o, :], bank[1][:, o * GT:(o + 1) * GT], ACT.Identity, bias=b_base_s[:, o:o + 1])
                last.then_inc(s["y0_kept"], 1)

            def keep_decay_first(i):
                wait("cs1_ready", i + 1)
                A(cs_h[0:DC, :], bank[2][0:DC, 0:GT], ACT.Tanh, bias=cs_b1_s[:, :]).then_inc(s["cs1_kept"], 1)

            def keep_decay_second(i):
                wait("cs2_ready", i + 1)
                wait("k_kept", i)
                for c in range(CH):
                    last = A(lc[:, c * GT:(c + 1) * GT], bank[0][:, c * GT:(c + 1) * GT], ACT.Tanh, scale=0.5, bias=half_b2[:, c:c + 1])
                last.then_inc(s["lc_kept"], 1)

            def keep_decay_values(i):
                wait("v_ready", i + 1)
                wait("y_ready", i)
                keep_values(bank[3], v_decay).then_inc(s["v_kept"], 1)

            def keep_y(i):
                wait("y_ready", i + 1)
                wait("o_ready", i)
                nc.scalar.copy(yt[:, :, :], bank[1][:, :].rearrange("p (c t) -> p c t", c=CH)).then_inc(s["y_kept"], 1)

            def keep_x1(i):
                wait("acc_out", i * 16)
                wait("x1_ready", i + 1)
                nc.scalar.copy(acc[:, :, :], bank[5][:, :].rearrange("p (t d) -> p t d", t=NT)).then_inc(s["x1_kept"], 1)

            def keep_norm(i):
                wait("ht_ready", i + 1)
                wait("gate_ready", i)
                for c in range(CH):
                    last = A(ht[:, c, :], bank[5][:, c * GT:(c + 1) * GT], ACT.Identity, scale=lng[:, 0, c:c + 1], bias=lng[:, 1, c:c + 1])
                last.then_inc(s["ht_kept"], 1)

            def keep_queries(i):
                wait("qb_ready", i + 1)
                wait("st_ready", i * GB)
                src = bank[6][:, :].rearrange("p (n t) -> p n t", t=T)
                for par in range(2):
                    last = A(q_pair[:, :, :, par, :].rearrange("p c b t -> p (c b) t"), src, ACT.Identity, scale=par_mask[:, par:par + 1])
                last.then_inc(s["qp_kept"], 1)
                for r in range(NR):
                    q = slice(32 * r, 32 * r + 32)
                    last = nc.scalar.copy(q_block[q, :, :, r, :].rearrange("p c b t -> p (c b) t"), src[q, :, :])
                last.then_inc(s["qb_kept"], 1)

            def keep_softmax_values(i):
                wait("vb_ready", i + 1)
                wait("pv_ready", i * NT)
                keep_values(bank[4], v_pair).then_inc(s["vb_kept"], 1)

            def exponentials(i, b):
                wait("st_ready", i * GB + b + 1)
                A(probs[:, b, :, :, :].rearrange("p c r t -> p (c r t)"), bank[7 if b % 2 == 0 else 4][:, :], ACT.Exp,
                  scale=float(DH) ** -0.5).then_inc(s["p_kept"], 1)

            def keep_context(i):
                wait("ctxt_ready", i + 1)
                nc.scalar.copy(ctx_t[:, :, :], bank[7][:, :].rearrange("p (c t) -> p c t", c=CH)).then_inc(s["ctxt_kept"], 1)

            def keep_second_norm(i):
                wait("mt_ready", i + 1)
                nc.scalar.copy(ht[:, :, :], bank[5][:, :].rearrange("p (c t) -> p c t", c=CH)).then_inc(s["mt_kept"], 1)

            def router(i):
                wait("lg_made", i + 1)
                A(ex[:, :, :], lg[:, :, :], ACT.Exp).then_inc(s["ex_made"], 1)

            def put_out(i):
                wait("acc_made", i + 1)
                act.dma_start(out[bass.ds(i * GT, GT), :].rearrange("(n p) d -> p n d", p=P), acc[:, :, :]).then_inc(s["acc_out"], 16)

            def groups(i, finish=True, begin=True):
                h, g = i - 1, i - 2
                if finish:
                    keep_context(g)
                if begin:
                    keep_y0(i)
                    keep_decay_first(i)
                    keep_decay_values(i)
                    keep_decay_second(i)
                if finish:
                    keep_second_norm(g)
                    put_out(g)
                keep_x1(h)
                keep_norm(h)
                keep_queries(h)
                if begin:
                    keep_y(i)
                keep_softmax_values(h)
                for b in range(GB):
                    exponentials(h, b)
                if finish:
                    router(g)

            keep_y0(0)
            keep_decay_first(0)
            keep_decay_values(0)
            keep_decay_second(0)
            keep_y(0)
            wait("weights_in", W_IN)
            groups(1, finish=False)
            with act.Fori(2, NG) as i:
                groups(i)
            groups(NG, begin=False)
            keep_context(NG - 1)
            keep_second_norm(NG - 1)
            router(NG - 1)
            put_out(NG - 1)
            wait("zero_rows", 32)
            fill_up(act, range(1, E, 2))
            wait("tables_made", 3)
            wait("split_made", NG)
            wait("split_out", NG * 16)

            def hidden(i, first, tiles=UNROLL):
                for k in range(tiles):
                    j = i * UNROLL + k
                    e = act.value_load(tile_e_i[0:1, bass.ds(j, 1)], min_val=0, max_val=E - 1)
                    for n in range(HC):
                        wait("h_ready", j * HC + (n + 1))
                        if not (first and k == 0):
                            wait("hid_split", j * HC + (n + 1 - HC))
                        for f in range(2 * n, 2 * n + 2):
                            last = A(hid[:, f, :], bank[n][:, (f % 2) * TB:(f % 2 + 1) * TB], ACT.Gelu_apprx_tanh,
                                     scale=1.0 / W_SCALE, bias=b1_all[:, bass.ds(e, 1), f])
                        last.then_inc(s["h_kept"], 1)

            hidden(0, True)
            with act.Fori(1, NI) as i:
                hidden(i, False)
            hidden(NI, False, REST)

        @block.vector
        def _(dve):
            V = nc.vector
            steps = {"setup_steps": 0, "decay_steps": 0, "ffn_steps": 0, "route_steps": 0, "table_steps": 0}

            def wait(name, v):
                dve.wait_ge(s[name], (16 if name in software else START) + v)

            def then(ins, name, base=0):
                steps[name] += 1
                ins.then_inc(s[name], 1)
                dve.wait_ge(s[name], base + (START + steps[name]))

            def step(ins):
                then(ins, "setup_steps")

            def tick():
                V.tensor_copy(tick_s[:, 0:1], tick_s[:, 1:2])

            V.memset(tick_s[:, :], 0.0)
            wait("consts_made", CONSTS)
            wait("first_in", FIRST_IN)
            V.memset(region0[:, :], 0.0)
            V.memset(pool_tick[:, :], 0.0)
            V.memset(before[:, 0, :], 0.0)
            V.memset(ones8[:, :], 1.0)
            V.memset(scale_w[:, 0:1], W_SCALE)
            V.memset(scale_w[:, 1:2], 0.0)
            V.tensor_copy(pid[:, :], pid_u[:, :])
            V.tensor_copy(id_h[:, :], ident[:, :])
            V.tensor_copy(tile_j[:, :], tile_ku[:, :])
            step(V.tensor_copy(iota8[:, :], iota8u[:, :]))
            V.tensor_scalar(alone_pos[:, :], pid[:, :], float(E * REGION), None, ALU.add)
            V.tensor_scalar(tile_k[:, :], tile_j[:, 0:NK], float(TB), None, ALU.mult)
            step(V.tensor_scalar(region0[:, :], iota8[:, :], float(REGION), None, ALU.mult))
            step(V.tensor_scalar(tok_g[:, :], tile_j[:, 0:NT], float(P), None, ALU.mult))
            step(V.tensor_scalar(tok_g[:, :], tok_g[:, :], pid[:, 0:1], None, ALU.add))
            for half in range(2):
                rows_ = slice(half * T, half * T + T)
                V.memset(same_head[rows_, 1 - half, :], 0.0)
                V.memset(v_pair[rows_, :, :, PV + half:PV + half + 1], 1.0)
                V.tensor_copy(diag_ones[rows_, :], ident[rows_, rows_]).then_inc(s["mask_done"], 1)
            V.tensor_reduce(par_mask[:, 0:1], ident[:, :].rearrange("p (q a f) -> p q a f", a=2, f=DH)[:, :, 0, :], mybir.AxisListType.XY, ALU.add).then_inc(s["mask_done"], 1)
            V.tensor_reduce(par_mask[:, 1:2], ident[:, :].rearrange("p (q a f) -> p q a f", a=2, f=DH)[:, :, 1, :], mybir.AxisListType.XY, ALU.add).then_inc(s["mask_done"], 1)
            V.tensor_scalar(half_b2[:], cs_b2_s[:], 0.5, None, ALU.mult).then_inc(s["mask_done"], 1)
            wait("derived", 1)
            step(V.tensor_scalar(base_t[:, :], base_t[:, :], 0.5, 0.5, ALU.mult, ALU.add))
            V.tensor_scalar(base_11[:, :], base_t[:, :], 1.1, None, ALU.mult)
            V.tensor_scalar(base_01[:, :], base_t[:, :], 0.1, None, ALU.mult).then_inc(s["mask_done"], 1)
            wait("mask_done", 6)

            def keep_lora(i):
                wait("lora_ready", i + 1)
                wait("y0_ready", i)
                V.scalar_tensor_tensor(out=lora_h[:, :].rearrange("p (b t) -> p b t", t=T), in0=bank[0][:, 0:GT].rearrange("p (b t) -> p b t", t=T),
                                       scalar=LORA_SCALE, in1=cond_er[:, bass.ds(i * GB, GB)].unsqueeze(2).to_broadcast([P, GB, T]),
                                       op0=ALU.mult, op1=ALU.mult).then_inc(s["lora_kept"], 1)

            def decays(i):
                steps["decay_steps"] = 0

                def step(ins):
                    then(ins, "decay_steps", i * DECAY_STEPS)

                wait("lc_kept", i + 1)
                wait("q_kept", i)
                for c in range(CH):
                    ins = V.tensor_scalar(lam[:, c * GT:(c + 1) * GT], lc[:, c * GT:(c + 1) * GT], base_01[:, c:c + 1], base_11[:, c:c + 1], ALU.mult, ALU.add)
                step(ins)
                step(V.tensor_scalar(lam[:, :], lam[:, :], LAM_MAX, 0.0, ALU.min, ALU.max))
                starts = lam[:, 0:CH * GT:HALF]
                step(V.tensor_copy(lam_first[:, 0:CH * GT:HALF], starts))
                step(V.memset(starts, 0.0))
                step(V.tensor_tensor_scan(cum[:, :], lam[:, :], lam_first[:, :], 0.0, ALU.mult, ALU.add))
                step(V.reciprocal(cum_mid[:, :], cum[:, HALF - 1:CH * GT:T]))
                first = cum[:, :].rearrange("p (n t) -> p n t", t=T)[:, :, 0:HALF]
                step(V.tensor_tensor(first, first, cum_mid[:, :].unsqueeze(2).to_broadcast([P, CH * GB, HALF]), ALU.mult))

            def inverse_decays(i):
                then(V.reciprocal(cum_inv[:, :], cum[:, :]), "decay_steps", i * DECAY_STEPS)
                assert steps["decay_steps"] == DECAY_STEPS

            def keep_decayed(i):
                wait("k_ready", i + 1)
                wait("s_ready", i * GB)
                for par in range(2):
                    ins = V.scalar_tensor_tensor(out=k_decay[:, :, :, par, :].rearrange("p c b t -> p (c b) t"),
                                                 in0=bank[1][:, :].rearrange("p (n t) -> p n t", t=T), scalar=par_mask[:, par:par + 1],
                                                 in1=cum_inv[:, :].rearrange("p (n t) -> p n t", t=T), op0=ALU.mult, op1=ALU.mult)
                ins.then_inc(s["k_kept"], 1)

            def keep_decayed_queries(i):
                wait("q_ready", i + 1)
                for r in range(NR):
                    q = slice(32 * r, 32 * r + 32)
                    ins = V.tensor_tensor(q_decay[q, :, :, r, :].rearrange("p c b t -> p (c b) t"), bank[2][q, :].rearrange("p (n t) -> p n t", t=T),
                                          cum[q, :].rearrange("p (n t) -> p n t", t=T), ALU.mult)
                ins.then_inc(s["q_kept"], 1)

            def keep_scores(i, b):
                wait("s_ready", i * GB + b + 1)
                wait("y_ready", i)
                V.tensor_tensor(s_decay[:, b, :, :, :].rearrange("p c r t -> p (c r) t"),
                                bank[3 * (b % 2)][:, :].rearrange("p (n t) -> p n t", t=T),
                                causal[:, :].unsqueeze(1).to_broadcast([P, CH * NR, T]), ALU.mult).then_inc(s["s_kept"], 1)

            def keep_x1t(i):
                wait("o_ready", i + 1)
                wait("xg_made", i * E)
                wait("x1_ready", i)
                V.tensor_tensor(x1t[:, :, :], bank[2][:, :].rearrange("p (c t) -> p c t", c=CH), xt[:, :, :], ALU.add).then_inc(s["x1t_kept"], 1)

            def mix_operand(i, g):
                if g == 0:
                    wait("x1t_kept", i + 1)
                if g >= 2:
                    wait("xg_used", i * (E - 1) + g - 1)
                else:
                    wait("z_ready", i)
                V.tensor_tensor(xg[:, g % 2, :, :].rearrange("p c (b t) -> p c b t", t=T),
                                x1t[:, :, :].rearrange("p c (b t) -> p c b t", t=T),
                                cond_all[:, g, bass.ds(i * GB, GB)].unsqueeze(1).unsqueeze(3).to_broadcast([P, CH, GB, T]), ALU.mult).then_inc(s["xg_made"], 1)

            def ffn_step(ins, i):
                then(ins, "ffn_steps", i * FFN_STEPS)

            def norm(i, k):
                for t in range(NT):
                    ins = V.bn_stats(stats[:, t, :], z[:, t, :])
                ffn_step(ins, i)
                tick()
                for t in range(NT):
                    ins = V.bn_aggr(mv[:, t, :], stats[:, t, :])
                ffn_step(ins, i)
                V.tensor_scalar(var_e[:, :], mv[:, :, 1], EPS, None, ALU.add).then_inc(s["var_made"], 1)

            def normalise(i, k):
                wait("rstd_made", i * 2 + k + 1)
                wait("ht_ready", i + k)
                for t in range(NT):
                    V.tensor_scalar(hn[:, t, :], z[:, t, :], mv[:, t, 0:1], rstd[:, t:t + 1], ALU.subtract, ALU.mult).then_inc(s["hn_made"], 1)

            def keep_z(i):
                steps["ffn_steps"] = 0
                wait("z_ready", i + 1)
                V.tensor_tensor(z[:, :, :], bank[4][:, :].rearrange("p (t d) -> p t d", t=NT),
                                c2_bias_s[:, :].unsqueeze(1).to_broadcast([P, NT, D]), ALU.add).then_inc(s["z_kept"], 1)
                wait("z_kept", i + 1)
                norm(i, 0)

            def first_norm(i):
                wait("m_made", i)
                normalise(i, 0)

            def keep_keys(i):
                wait("kb_ready", i + 1)
                wait("st_ready", i * GB)
                src = bank[7][:, :].rearrange("p (n t) -> p n t", t=T)
                for r in range(NR):
                    q = slice(32 * r, 32 * r + 32)
                    ins = V.tensor_copy(k_block[q, :, :, r, :].rearrange("p c b t -> p (c b) t"), src[q, :, :])
                ins.then_inc(s["kb_kept"], 1)
                for par in range(2):
                    ins = V.tensor_scalar(k_pair[:, :, :, par, :].rearrange("p c b t -> p (c b) t"), src, par_mask[:, par:par + 1], None, ALU.mult)
                ins.then_inc(s["kp_kept"], 1)

            def maxima(i, b):
                wait("smax_ready", i * GB + b + 1)
                wait("shift_made", i * GB)
                V.tensor_reduce(row_max[:, b, :], bank[5 + b % 2][:, :].rearrange("p (n t) -> p n t", t=T), AX_X, ALU.max,
                                negate=True).then_inc(s["max_kept"], 1)

            def keep_weighted(i, t):
                wait("pv_ready", i * NT + t + 1)
                wait("ctxt_ready", i)
                pv = bank[5 + t][:, 0:CH * NR * PW].rearrange("p (h f) -> p h f", f=PW)
                ffn_step(V.reciprocal(sum_inv[:, t, :, :], pv[:, :, PV:PW]), i)
                V.tensor_tensor(ctxn[:, t, :].rearrange("p (h a f) -> p h a f", a=2, f=DH),
                                pv[:, :, 0:PV].rearrange("p h (a f) -> p h a f", a=2),
                                sum_inv[:, t, :, :].unsqueeze(3).to_broadcast([P, CH * NR, 2, DH]), ALU.mult).then_inc(s["ctx_kept"], 1)

            def keep_z2(i):
                wait("wo_ready", i + 1)
                V.tensor_tensor(z[:, :, :], bank[4][:, :].rearrange("p (t d) -> p t d", t=NT), z[:, :, :], ALU.add).then_inc(s["z2_kept"], 1)
                wait("z2_kept", i + 1)
                norm(i, 1)

            def finish_z2(i):
                normalise(i, 1)
                wait("x1_kept", i + 1)
                V.tensor_tensor(acc[:, :, :], acc[:, :, :], z[:, :, :], ALU.add).then_inc(s["acc_made"], 1)

            def keep_logits(i):
                wait("gate_ready", i + 1)
                V.tensor_copy(lg[:, :, :], bank[6][:, 0:NT * E].rearrange("p (t e) -> p t e", e=E)).then_inc(s["logits_kept"], 1)

            def route(i):
                steps["route_steps"] = 0

                def step(ins):
                    then(ins, "route_steps", i * ROUTE_STEPS)

                wait("logits_kept", i + 1)
                tick()
                for t in range(NT):
                    ins = V.max(top[:, t, :], lg[:, t, :])
                step(ins)
                tick()
                for t in range(NT):
                    ins = V.max_index(top_i[:, t, :], top[:, t, :], lg[:, t, :])
                step(ins)
                V.tensor_copy(top_f[:, :, :], top_i[:, :, :])
                step(V.tensor_tensor(lg[:, :, :], lg[:, :, :], top[:, :, 0:1].to_broadcast([P, NT, E]), ALU.subtract))
                for j in range(2):
                    ins = V.tensor_tensor(pick[:, :, j, :], iota8[:, :].unsqueeze(1).to_broadcast([P, NT, E]),
                                          top_f[:, :, j:j + 1].to_broadcast([P, NT, E]), ALU.is_equal)
                step(ins)
                V.tensor_tensor(picked[:, :, :], pick[:, :, 0, :], pick[:, :, 1, :], ALU.add).then_inc(s["lg_made"], 1)
                wait("lg_made", i + 1)

            def keep_ranks(i):
                wait("ranks_ready", i + 1)
                V.tensor_copy(rank[:, :, :], bank[3][:, 0:NT * E].rearrange("p (t e) -> p t e", e=E))
                then(V.tensor_copy(tot[:, :, :], bank[3][:, NT * E:2 * NT * E].rearrange("p (t e) -> p t e", e=E)),
                     "route_steps", i * ROUTE_STEPS)

            def rank_rows(i):
                def step(ins):
                    then(ins, "route_steps", i * ROUTE_STEPS)

                wait("ex_made", i + 1)
                step(V.tensor_reduce(ex_sum[:, :], ex[:, :, :], AX_X, ALU.add))
                step(V.reciprocal(ex_sum[:, :], ex_sum[:, :]))
                step(V.tensor_tensor(ex[:, :, :], ex[:, :, :], ex_sum[:, :].unsqueeze(2).to_broadcast([P, NT, E]), ALU.mult))
                step(V.tensor_tensor(ex[:, :, :], ex[:, :, :], picked[:, :, :], ALU.mult))
                step(V.tensor_reduce(two_sum[:, :], ex[:, :, :], AX_X, ALU.add))
                step(V.reciprocal(two_sum[:, :], two_sum[:, :]))
                wait("scattered", i * (K * NT * 16))
                V.tensor_tensor(rows[:, :, G_AT:ID_AT].bitcast(F32), ex[:, :, :], two_sum[:, :].unsqueeze(2).to_broadcast([P, NT, E]), ALU.mult)
                V.tensor_copy(rows[:, :, ID_AT:ID_AT + 2].bitcast(I32).rearrange("p t o -> p (t o)"), tok_g[:, :])
                for t in range(NT):
                    step(V.tensor_tensor(before[:, t + 1, :], before[:, t, :], tot[:, t, :], ALU.add))
                step(V.tensor_tensor(rank[:, :, :], rank[:, :, :], before[:, 0:NT, :], ALU.add))
                step(V.tensor_tensor(rank[:, :, :], rank[:, :, :], region0[:, :].unsqueeze(1).to_broadcast([P, NT, E]), ALU.add))
                for k in range(K):
                    ins = V.tensor_tensor(slot[:, k, :, :], pick[:, :, k, :], rank[:, :, :], ALU.mult)
                step(ins)
                step(V.tensor_reduce(pos_f[:, :, :], slot[:, :, :, :], AX_X, ALU.add))
                V.tensor_copy(pos_u[:, :, :], pos_f[:, :, :]).then_inc(s["pos_made"], 1)
                step(V.tensor_scalar(tok_g[:, :], tok_g[:, :], float(GT), None, ALU.add))
                V.tensor_copy(before[:, 0, :], before[:, NT, :]).then_inc(s["ranks_kept"], 1)
                wait("ranks_kept", i + 1)
                assert steps["route_steps"] == ROUTE_STEPS, steps

            def groups(i, send=True, finish=True, begin=True):
                h, g = i - 1, i - 2
                if begin:
                    keep_lora(i)
                if finish:
                    keep_z2(g)
                    finish_z2(g)
                mix_operand(h, 2)
                mix_operand(h, 3)
                if send:
                    rank_rows(i - 3)
                mix_operand(h, 4)
                if begin:
                    decays(i)
                    inverse_decays(i)
                mix_operand(h, 5)
                mix_operand(h, 6)
                if finish:
                    keep_logits(g)
                if begin:
                    keep_decayed(i)
                mix_operand(h, 7)
                if begin:
                    keep_decayed_queries(i)
                keep_z(h)
                if begin:
                    keep_scores(i, 0)
                first_norm(h)
                if begin:
                    for b in range(1, GB):
                        keep_scores(i, b)
                keep_keys(h)
                for b in range(2):
                    maxima(h, b)
                if begin:
                    keep_x1t(i)
                for b in range(2, GB):
                    maxima(h, b)
                if begin:
                    mix_operand(i, 0)
                    mix_operand(i, 1)
                if finish:
                    route(g)
                keep_weighted(h, 0)
                if finish:
                    keep_ranks(g)
                keep_weighted(h, 1)

            keep_lora(0)
            decays(0)
            inverse_decays(0)
            keep_decayed(0)
            keep_decayed_queries(0)
            for b in range(GB):
                keep_scores(0, b)
            wait("weights_in", W_IN)
            V.tensor_tensor(c2_w_s[:, :, :, :], c2_w_s[:, :, :, :],
                            c2_mask_s[:, :, :].unsqueeze(2).to_broadcast([P, CH, E, D]), ALU.mult).then_inc(s["z_weights"], 1)
            keep_x1t(0)
            mix_operand(0, 0)
            mix_operand(0, 1)
            step(V.tensor_scalar(b2_f[:, :, :], b2_f[:, :, :], W_SCALE, None, ALU.mult))
            step(V.tensor_copy(b2_s[:, 0, :, :], b2_f[:, :, :]))
            step(V.tensor_tensor(b2_s[:, 1, :, :], b2_f[:, :, :], b2_s[:, 0, :, :], ALU.subtract))
            groups(1, send=False, finish=False)
            groups(2, send=False)
            with dve.Fori(3, NG) as i:
                groups(i)
            groups(NG, begin=False)
            rank_rows(NG - 2)
            keep_z2(NG - 1)
            finish_z2(NG - 1)
            keep_logits(NG - 1)
            route(NG - 1)
            keep_ranks(NG - 1)
            rank_rows(NG - 1)
            def link(ins):
                then(ins, "table_steps")

            count = before[:, 0, :]
            link(V.tensor_tensor(pad_at_f[:, :], count, region0[:, :], ALU.add))
            V.tensor_copy(pad_at[:, :], pad_at_f[:, :]).then_inc(s["tables_made"], 1)
            link(V.tensor_tensor(cmp_k[:, :, :], count.unsqueeze(2).to_broadcast([P, E, NK]),
                                 tile_k[:, :].unsqueeze(1).to_broadcast([P, E, NK]), ALU.is_gt))
            link(V.tensor_reduce(n_tiles[:, :], cmp_k[:, :, :], AX_X, ALU.add))
            link(V.tensor_tensor_scan(tiles_to[:, :], ones8[:, :], n_tiles[:, :], 0.0, ALU.mult, ALU.add))
            bc_e = [P, NJ, E]
            link(V.tensor_tensor(past[:, :, :], tiles_to[:, :].unsqueeze(1).to_broadcast(bc_e),
                                 tile_j[:, :].unsqueeze(2).to_broadcast(bc_e), ALU.is_le))
            link(V.tensor_tensor(past_n[:, :, :], past[:, :, :], n_tiles[:, :].unsqueeze(1).to_broadcast(bc_e), ALU.mult))
            V.tensor_reduce(tile_e[:, :], past[:, :, :], AX_X, ALU.add)
            link(V.tensor_reduce(tile_first[:, :], past_n[:, :, :], AX_X, ALU.add))
            link(V.tensor_tensor(tile_row[:, :], tile_j[:, :], tile_first[:, :], ALU.subtract))
            link(V.tensor_scalar(tile_row[:, :], tile_row[:, :], float(TB), None, ALU.mult))
            link(V.scalar_tensor_tensor(out=tile_row[:, :], in0=tile_e[:, :], scalar=float(REGION), in1=tile_row[:, :],
                                        op0=ALU.mult, op1=ALU.add))
            link(V.tensor_scalar(tile_row[:, :], tile_row[:, :], float(E * REGION), None, ALU.min))
            link(V.tensor_scalar(tile_e[:, :], tile_e[:, :], float(E - 1), None, ALU.min))
            V.tensor_copy(tile_row_i[:, :], tile_row[:, :]).then_inc(s["tables_made"], 1)
            V.tensor_copy(tile_e_i[:, :], tile_e[:, :]).then_inc(s["tables_made"], 1)
            wait("tables_made", 3)

            def keep_xt(i, k, first):
                j = i * UNROLL + k
                wait("t_ready", j + 1)
                if not (first and k < 2):
                    wait("h_ready", j * HC - HC)
                V.tensor_copy(sxt[:, k % 2, :, :], tbank[k % 2][:, :, :]).then_inc(s["xt_kept"], 1)

            def split_hidden(i, k, n, first):
                j = i * UNROLL + k
                fs = slice(2 * n, 2 * n + 2)
                wait("h_kept", j * HC + (n + 1))
                if not (first and k < 2):
                    wait("ye_ready", j * ST - ST)
                V.tensor_copy(hid_s[:, k % 2, 0, fs, :], hid[:, fs, :]).then_inc(s["hi_made"], 1)
                wait("hi_made", j * HC + (n + 1))
                V.tensor_tensor(hid_s[:, k % 2, 1, fs, :], hid[:, fs, :], hid_s[:, k % 2, 0, fs, :], ALU.subtract).then_inc(s["hid_split"], 1)

            def keep_y(i, k, e, first):
                for st in range(ST):
                    j = i * (UNROLL * ST) + (k * ST + st)
                    wait("ye_ready", j + 1)
                    if not first:
                        wait("added", (j + 1 - ST) * 16)
                    gate = srows[:, k % UNROLL, st, G_AT:ID_AT].bitcast(F32)[:, bass.ds(e, 1)]
                    V.tensor_scalar(ys[:, st, :], bank[4 + st][:, 0:D], gate, 1.0 / W_SCALE, ALU.mult, ALU.mult).then_inc(s["ye_kept"], 1)

            def expert(i, k):
                return dve.value_load(tile_e_i[0:1, bass.ds(i * UNROLL + k, 1)], min_val=0, max_val=E - 1)

            def body(i, first, tiles=UNROLL):
                for k in range(tiles):
                    for n in range(HC):
                        split_hidden(i, k, n, first)
                    if tiles == UNROLL or k + 1 < tiles:
                        keep_xt(i, k + 1, first)
                    if not (first and k == 0):
                        keep_y(i, k - 1, expert(i, k - 1), first and k == 1)

            wait("split_out", NG * 16)
            keep_xt(0, 0, True)
            body(0, True)
            with dve.Fori(1, NI) as i:
                body(i, False)
            body(NI, False, REST)
            keep_y(NI, REST - 1, expert(NI, REST - 1), False)


def kernel(x, cond_8, L0_cond_W_base, L0_cond_b_base, L0_cond_As, L0_cond_Bs, L0_attn_q_w, L0_attn_k_w, L0_attn_v_w,
           L0_attn_o_w, L0_attn_cs_w1, L0_attn_cs_b1, L0_attn_cs_w2, L0_attn_cs_b2, L0_attn_decay_params,
           L0_cond2_weight, L0_cond2_mask, L0_cond2_bias, L0_ffn_ln1_g, L0_ffn_ln1_b, L0_ffn_ln2_g, L0_ffn_ln2_b,
           L0_ffn_Wq, L0_ffn_Wk, L0_ffn_Wv, L0_ffn_Wo, L0_ffn_Wg, L0_ffn_W1, L0_ffn_b1, L0_ffn_W2, L0_ffn_b2):
    import numpy as np
    import concourse.bacc as bacc
    from concourse.bass_utils import run_bass_kernel_spmd

    def rows(a):
        return np.asarray(a).reshape(-1, P, a.shape[-1]).transpose(1, 0, 2)

    def cols(a):
        return np.asarray(a).reshape(-1, P).T

    t = np.transpose
    arrays = {
        "x_t": rows(t(np.asarray(x).reshape(B * T, D))),
        "cond_t": t(np.asarray(cond_8)),
        "cond_er": np.repeat(t(np.asarray(cond_8)), R, axis=0),
        "w_base": rows(t(L0_cond_W_base)),
        "b_base": cols(L0_cond_b_base),
        "lora_a": rows(t(np.asarray(L0_cond_As).reshape(E * R, D))),
        "lora_b": t(L0_cond_Bs, (0, 2, 1)).reshape(E * R, D),
        "wq": rows(t(L0_attn_q_w)), "wk": rows(t(L0_attn_k_w)), "wv": rows(t(L0_attn_v_w)), "wo": rows(t(L0_attn_o_w)),
        "cs_w1": rows(t(L0_attn_cs_w1)),
        "cs_b1": np.asarray(L0_attn_cs_b1).reshape(DC, 1),
        "cs_w2": np.repeat(t(L0_attn_cs_w2), DH, axis=1),
        "cs_b2": cols(np.repeat(L0_attn_cs_b2, DH)),
        "decay": cols(np.asarray(L0_attn_decay_params).reshape(D)),
        "c2_w": t(np.asarray(L0_cond2_weight).reshape(E, D, CH, P), (3, 2, 0, 1)),
        "c2_mask": rows(t(L0_cond2_mask)),
        "c2_bias": np.asarray(L0_cond2_bias),
        "ln1_g": cols(L0_ffn_ln1_g), "ln1_b": cols(L0_ffn_ln1_b),
        "ln2_g": np.asarray(L0_ffn_ln2_g), "ln2_b": np.asarray(L0_ffn_ln2_b),
        "fq": rows(L0_ffn_Wq), "fk": rows(L0_ffn_Wk), "fv": rows(L0_ffn_Wv), "fo": rows(L0_ffn_Wo), "fg": rows(L0_ffn_Wg),
        "fw": np.stack([t(np.asarray(L0_ffn_W1).reshape(E, CH, P, F), (2, 0, 1, 3)).reshape(P, E, CH * F),
                        t(np.asarray(L0_ffn_W2).reshape(E, FC, P, D), (2, 0, 1, 3)).reshape(P, E, FC * D)], axis=2).reshape(P, E * 2, W2_AT),
        "fb1": t(np.asarray(L0_ffn_b1).reshape(E, FC, P), (2, 0, 1)),
        "fb2": np.asarray(L0_ffn_b2).reshape(1, E, D),
        "ident_in": np.eye(P, dtype=np.float32),
        "pad_ids": np.arange(NTOK, NTOK + P, dtype=np.int32).reshape(P, 1),
    }
    arrays = {n: np.ascontiguousarray(a) for n, a in arrays.items()}
    nc = bacc.Bacc("TRN2", target_bir_lowering=False, num_devices=1)
    args = [nc.dram_tensor(n, a.shape, mybir.dt.from_np(a.dtype), kind="ExternalInput").ap() for n, a in arrays.items()]
    order = ("x_t cond_t cond_er w_base b_base lora_a lora_b wq wk wv wo cs_w1 cs_b1 cs_w2 cs_b2 decay c2_w c2_mask c2_bias "
             "ln1_g ln1_b ln2_g ln2_b fq fk fv fo fg fw fb1 fb2 ident_in pad_ids").split()
    assert order == list(arrays)
    out = nc.dram_tensor("out", (NTOK + P, D), F32, kind="ExternalOutput").ap()
    bass_adaln_attn_ffn(nc, *args, out)
    got = run_bass_kernel_spmd(nc, [arrays], core_ids=[0])
    return got.results[0]["out"][:NTOK].reshape(B, T, D)
```
